# Optimizing a Trainium2 kernel written in Bass

```python
import numpy as np
import jax
import jax.numpy as jnp

def _softmax(x, axis=-1):
    return jax.nn.softmax(x, axis=axis)

def _gelu(x):
    return jax.nn.gelu(x, approximate=True)

def _silu(x):
    return jax.nn.silu(x)

def _sigmoid(x):
    return jax.nn.sigmoid(x)

def _layernorm(x, axis=-1, eps=1e-05):
    m = jnp.mean(x, axis=axis, keepdims=True)
    v = jnp.var(x, axis=axis, keepdims=True)
    return (x - m) / jnp.sqrt(v + eps)

def _scatter_add(tgt, idx, src, axis=0):
    return tgt.at[idx].add(src)

def _segment_sum(src, seg, n):
    return jax.ops.segment_sum(src, seg, n)
kernel_name = 'mk_adj_resnorm_d4_adj_r2_681d5d'

def setup_inputs(seed: int=0):
    np.random.seed(seed)
    _w = jnp.asarray

    def _rec_inputs():
        import jax
        import jax.numpy as jnp
        _gk = jax.random.key(seed)
        x = -0.0004039 + 1 * jax.random.normal(jax.random.fold_in(_gk, 1), (64, 128, 384), jnp.float32)
        _a = jax.random.bernoulli(jax.random.fold_in(_gk, 2), 0.0625, (64, 128, 128))
        _af = _a.astype(jnp.float32)
        adj = _af
        return (x, adj)
    x, adj = _rec_inputs()

    def _L0_gnn_setup():
        import jax, jax.numpy as jnp
        import numpy as np
        B, S, H, L = (32, 256, 384, 2)

        def _layer_norm(z, a, b, eps=0.001):
            mu = jnp.mean(z, axis=-1, keepdims=True)
            sigma = jnp.std(z, axis=-1, keepdims=True, ddof=1)
            return (z - mu) / (sigma + eps) * a + b
        key = jax.random.key(seed)
        ks = jax.random.split(key, 6)
        hidden_state = jax.random.normal(ks[0], (B, S, H), dtype=jnp.float32)
        adjacency_matrix = (jax.random.uniform(ks[1], (B, S, S)) < 0.2).astype(jnp.float32)
        W_left = 0.05 * jax.random.normal(ks[2], (L, H, H), dtype=jnp.float32)
        W_right = 0.05 * jax.random.normal(ks[3], (L, H, H), dtype=jnp.float32)
        W_lin = 0.05 * jax.random.normal(ks[4], (L, H, H), dtype=jnp.float32)
        b_lin = jnp.zeros((L, H), dtype=jnp.float32)
        ln_a = jnp.ones((L, H), dtype=jnp.float32)
        ln_b = jnp.zeros((L, H), dtype=jnp.float32)
        return {'hidden_state': hidden_state, 'adjacency_matrix': adjacency_matrix, 'W_left': W_left, 'W_right': W_right, 'W_lin': W_lin, 'b_lin': b_lin, 'ln_a': ln_a, 'ln_b': ln_b}
    _L0_gnn_all = _L0_gnn_setup()
    _L0_gnn_in = {k: v for k, v in _L0_gnn_all.items() if k in ('W_left', 'W_right', 'W_lin', 'b_lin', 'ln_a', 'ln_b')}
    del _L0_gnn_all

    def _L1_gnn_setup():
        import jax, jax.numpy as jnp
        import numpy as np
        NUM_HEADS = 12
        HIDDEN = 384
        HEAD = HIDDEN // NUM_HEADS
        B, N = (16, 256)
        key = jax.random.key(seed)
        ks = jax.random.split(key, 9)
        s = 0.02
        return {'x': jax.random.normal(ks[0], (B, N, HIDDEN), jnp.float32), 'spatial_encoding': jax.random.normal(ks[1], (B, N, N), jnp.float32), 'edge_encoding': jax.random.normal(ks[2], (B, N, N), jnp.float32), 'Wq': jax.random.normal(ks[3], (HIDDEN, HIDDEN), jnp.float32) * s, 'Wk': jax.random.normal(ks[4], (HIDDEN, HIDDEN), jnp.float32) * s, 'Wv': jax.random.normal(ks[5], (HIDDEN, HIDDEN), jnp.float32) * s, 'bv': jax.random.normal(ks[6], (HIDDEN,), jnp.float32) * s, 'Wo': jax.random.normal(ks[7], (HIDDEN, HIDDEN), jnp.float32) * s, 'bo': jax.random.normal(ks[8], (HIDDEN,), jnp.float32) * s}
    _L1_gnn_all = _L1_gnn_setup()
    _L1_gnn_in = {k: v for k, v in _L1_gnn_all.items() if k in ('Wq', 'Wk', 'Wv', 'bv', 'Wo', 'bo')}
    del _L1_gnn_all

    def _L2_gnn_setup():
        import jax, jax.numpy as jnp
        import numpy as np
        LN_EPS = 1e-12

        def _digcn_forward(hidden_state, adjacency_matrix, Wl, bl, Ws, bs, Wr, br, ln_w, ln_b):
            B, S, D = hidden_state.shape
            temper = jnp.asarray(D, jnp.float32) ** 0.5
            i = jnp.arange(S)
            upper = (i[None, :] > i[:, None]).astype(hidden_state.dtype)
            lower = (i[None, :] < i[:, None]).astype(hidden_state.dtype)

            def layer(h, params):
                wl, b_l, ws, b_s, wr, b_r, g, beta = params
                u = jnp.einsum('bid,bjd->bij', h, h) / temper
                a = jax.nn.softmax(u, axis=-1)
                delta = a * adjacency_matrix
                attn = delta / (jnp.sum(delta, axis=-1, keepdims=True) + 1e-10)
                hl = h @ wl.T + b_l
                hs = h @ ws.T + b_s
                hr = h @ wr.T + b_r
                diag_a = jnp.diagonal(attn, axis1=1, axis2=2)
                ctx = jnp.einsum('bij,bjd->bid', attn * upper, hl) + diag_a[..., None] * hs + jnp.einsum('bij,bjd->bid', attn * lower, hr)
                mean = ctx.mean(-1, keepdims=True)
                var = ctx.var(-1, keepdims=True)
                o = (ctx - mean) / jnp.sqrt(var + LN_EPS) * g + beta
                return (jax.nn.relu(o), None)
            out, _ = jax.lax.scan(layer, hidden_state, (Wl, bl, Ws, bs, Wr, br, ln_w, ln_b))
            return out
        key = jax.random.key(seed)
        ks = jax.random.split(key, 6)
        B, S, D, L = (8, 512, 384, 2)
        scale = (1.0 / D) ** 0.5
        hidden_state = jax.random.normal(ks[0], (B, S, D), jnp.float32)
        adjacency_matrix = (jax.random.uniform(ks[1], (B, S, S)) < 0.05).astype(jnp.float32)
        Wl = jax.random.normal(ks[2], (L, D, D), jnp.float32) * scale
        Ws = jax.random.normal(ks[3], (L, D, D), jnp.float32) * scale
        Wr = jax.random.normal(ks[4], (L, D, D), jnp.float32) * scale
        bl = jnp.zeros((L, D), jnp.float32)
        bs = jnp.zeros((L, D), jnp.float32)
        br = jnp.zeros((L, D), jnp.float32)
        ln_w = jnp.ones((L, D), jnp.float32)
        ln_b = jnp.zeros((L, D), jnp.float32)
        return dict(hidden_state=hidden_state, adjacency_matrix=adjacency_matrix, Wl=Wl, bl=bl, Ws=Ws, bs=bs, Wr=Wr, br=br, ln_w=ln_w, ln_b=ln_b)
    _L2_gnn_all = _L2_gnn_setup()
    _L2_gnn_in = {k: v for k, v in _L2_gnn_all.items() if k in ('Wl', 'bl', 'Ws', 'bs', 'Wr', 'br', 'ln_w', 'ln_b')}
    del _L2_gnn_all

    def _L3_gnn_setup():
        import jax, jax.numpy as jnp
        import numpy as np
        NUM_HEADS = 12
        HIDDEN = 384
        HEAD = HIDDEN // NUM_HEADS
        SCALE = HIDDEN ** (-0.5)
        key = jax.random.key(seed)
        ks = jax.random.split(key, 8)
        B, N = (16, 256)
        std = HIDDEN ** (-0.5)
        return {'x': jax.random.normal(ks[0], (B, N, HIDDEN), dtype=jnp.float32), 'encoding_bias': jax.random.normal(ks[1], (B, N, N), dtype=jnp.float32), 'Wq': jax.random.normal(ks[2], (HIDDEN, HIDDEN), dtype=jnp.float32) * std, 'Wk': jax.random.normal(ks[3], (HIDDEN, HIDDEN), dtype=jnp.float32) * std, 'Wv': jax.random.normal(ks[4], (HIDDEN, HIDDEN), dtype=jnp.float32) * std, 'bv': jax.random.normal(ks[5], (HIDDEN,), dtype=jnp.float32) * 0.01, 'Wo': jax.random.normal(ks[6], (HIDDEN, HIDDEN), dtype=jnp.float32) * std, 'bo': jax.random.normal(ks[7], (HIDDEN,), dtype=jnp.float32) * 0.01}
    _L3_gnn_all = _L3_gnn_setup()
    _L3_gnn_in = {k: v for k, v in _L3_gnn_all.items() if k in ('Wq', 'Wk', 'Wv', 'bv', 'Wo', 'bo')}
    del _L3_gnn_all
    return {'x': x, 'adj': adj, 'L0_gnn_W_left': _L0_gnn_in['W_left'], 'L0_gnn_W_right': _L0_gnn_in['W_right'], 'L0_gnn_W_lin': _L0_gnn_in['W_lin'], 'L0_gnn_b_lin': _L0_gnn_in['b_lin'], 'L0_gnn_ln_a': _L0_gnn_in['ln_a'], 'L0_gnn_ln_b': _L0_gnn_in['ln_b'], 'L1_gnn_Wq': _L1_gnn_in['Wq'], 'L1_gnn_Wk': _L1_gnn_in['Wk'], 'L1_gnn_Wv': _L1_gnn_in['Wv'], 'L1_gnn_bv': _L1_gnn_in['bv'], 'L1_gnn_Wo': _L1_gnn_in['Wo'], 'L1_gnn_bo': _L1_gnn_in['bo'], 'L2_gnn_Wl': _L2_gnn_in['Wl'], 'L2_gnn_bl': _L2_gnn_in['bl'], 'L2_gnn_Ws': _L2_gnn_in['Ws'], 'L2_gnn_bs': _L2_gnn_in['bs'], 'L2_gnn_Wr': _L2_gnn_in['Wr'], 'L2_gnn_br': _L2_gnn_in['br'], 'L2_gnn_ln_w': _L2_gnn_in['ln_w'], 'L2_gnn_ln_b': _L2_gnn_in['ln_b'], 'L3_gnn_Wq': _L3_gnn_in['Wq'], 'L3_gnn_Wk': _L3_gnn_in['Wk'], 'L3_gnn_Wv': _L3_gnn_in['Wv'], 'L3_gnn_bv': _L3_gnn_in['bv'], 'L3_gnn_Wo': _L3_gnn_in['Wo'], 'L3_gnn_bo': _L3_gnn_in['bo']}

def reference(x, adj, L0_gnn_W_left, L0_gnn_W_right, L0_gnn_W_lin, L0_gnn_b_lin, L0_gnn_ln_a, L0_gnn_ln_b, L1_gnn_Wq, L1_gnn_Wk, L1_gnn_Wv, L1_gnn_bv, L1_gnn_Wo, L1_gnn_bo, L2_gnn_Wl, L2_gnn_bl, L2_gnn_Ws, L2_gnn_bs, L2_gnn_Wr, L2_gnn_br, L2_gnn_ln_w, L2_gnn_ln_b, L3_gnn_Wq, L3_gnn_Wk, L3_gnn_Wv, L3_gnn_bv, L3_gnn_Wo, L3_gnn_bo):
    import jax
    import jax.numpy as jnp

    def _L0_gnn_ref(hidden_state, adjacency_matrix, W_left, W_right, W_lin, b_lin, ln_a, ln_b):
        import jax, jax.numpy as jnp
        import numpy as np
        B, S, H, L = (32, 256, 384, 2)

        def _layer_norm(z, a, b, eps=0.001):
            mu = jnp.mean(z, axis=-1, keepdims=True)
            sigma = jnp.std(z, axis=-1, keepdims=True, ddof=1)
            return (z - mu) / (sigma + eps) * a + b
        temper = float(np.sqrt(H))
        adj = adjacency_matrix
        adj_tri = jnp.triu(adj, k=1)
        diag_mask = jnp.triu(adj, k=0) - adj_tri
        h = hidden_state
        for l in range(L):
            m_left = jnp.einsum('bsh,oh->bso', h, W_left[l])
            m_right = jnp.einsum('bsh,oh->bso', h, W_right[l])
            u_left = jnp.einsum('bih,bjh->bij', h, m_left) / temper
            u_right = jnp.einsum('bih,bjh->bij', h, m_right) / temper
            u = u_left * adj_tri + u_left * diag_mask + u_right * jnp.swapaxes(adj_tri, 1, 2)
            delta_exp_u = jnp.exp(u) * adj
            attention = delta_exp_u / (jnp.sum(delta_exp_u, axis=2, keepdims=True) + 1e-10)
            h_lin = jnp.einsum('bsh,oh->bso', h, W_lin[l]) + b_lin[l]
            ctx = jnp.matmul(attention, h_lin)
            h = jax.nn.relu(_layer_norm(ctx, ln_a[l], ln_b[l]))
        return h

    def _L1_gnn_ref(x, spatial_encoding, edge_encoding, Wq, Wk, Wv, bv, Wo, bo):
        import jax, jax.numpy as jnp
        import numpy as np
        NUM_HEADS = 12
        HIDDEN = 384
        HEAD = HIDDEN // NUM_HEADS
        B, N = (16, 256)
        b, n, h = x.shape
        scale = jnp.asarray(HIDDEN, x.dtype) ** (-0.5)
        q = (x @ Wq.T).reshape(b, n, NUM_HEADS, HEAD)
        k = (x @ Wk.T).reshape(b, n, NUM_HEADS, HEAD)
        v = (x @ Wv.T + bv).reshape(b, n, NUM_HEADS, HEAD)
        bias = (spatial_encoding + edge_encoding)[:, None]
        scores = jnp.einsum('bqhd,bkhd->bhqk', q, k) * scale + bias
        row_nonzero = jnp.any(scores != 0, axis=-1, keepdims=True)
        scores = jnp.where(row_nonzero, scores, -jnp.inf)
        p = jax.nn.softmax(scores, axis=-1)
        p = jnp.nan_to_num(p)
        out = jnp.einsum('bhqk,bkhd->bqhd', p, v).reshape(b, n, h)
        return out @ Wo.T + bo

    def _L2_gnn_ref(hidden_state, adjacency_matrix, Wl, bl, Ws, bs, Wr, br, ln_w, ln_b):
        import jax, jax.numpy as jnp
        import numpy as np
        LN_EPS = 1e-12

        def _digcn_forward(hidden_state, adjacency_matrix, Wl, bl, Ws, bs, Wr, br, ln_w, ln_b):
            B, S, D = hidden_state.shape
            temper = jnp.asarray(D, jnp.float32) ** 0.5
            i = jnp.arange(S)
            upper = (i[None, :] > i[:, None]).astype(hidden_state.dtype)
            lower = (i[None, :] < i[:, None]).astype(hidden_state.dtype)

            def layer(h, params):
                wl, b_l, ws, b_s, wr, b_r, g, beta = params
                u = jnp.einsum('bid,bjd->bij', h, h) / temper
                a = jax.nn.softmax(u, axis=-1)
                delta = a * adjacency_matrix
                attn = delta / (jnp.sum(delta, axis=-1, keepdims=True) + 1e-10)
                hl = h @ wl.T + b_l
                hs = h @ ws.T + b_s
                hr = h @ wr.T + b_r
                diag_a = jnp.diagonal(attn, axis1=1, axis2=2)
                ctx = jnp.einsum('bij,bjd->bid', attn * upper, hl) + diag_a[..., None] * hs + jnp.einsum('bij,bjd->bid', attn * lower, hr)
                mean = ctx.mean(-1, keepdims=True)
                var = ctx.var(-1, keepdims=True)
                o = (ctx - mean) / jnp.sqrt(var + LN_EPS) * g + beta
                return (jax.nn.relu(o), None)
            out, _ = jax.lax.scan(layer, hidden_state, (Wl, bl, Ws, bs, Wr, br, ln_w, ln_b))
            return out
        return _digcn_forward(hidden_state, adjacency_matrix, Wl, bl, Ws, bs, Wr, br, ln_w, ln_b)

    def _L3_gnn_ref(x, encoding_bias, Wq, Wk, Wv, bv, Wo, bo):
        import jax, jax.numpy as jnp
        import numpy as np
        NUM_HEADS = 12
        HIDDEN = 384
        HEAD = HIDDEN // NUM_HEADS
        SCALE = HIDDEN ** (-0.5)
        B, N, _ = x.shape
        q = (x @ Wq.T).reshape(B, N, NUM_HEADS, HEAD)
        k = (x @ Wk.T).reshape(B, N, NUM_HEADS, HEAD)
        v = (x @ Wv.T + bv).reshape(B, N, NUM_HEADS, HEAD)
        a = jnp.einsum('bnhd,bmhd->bhnm', q, k) * SCALE + encoding_bias[:, None, :, :]
        pad_mask = jnp.all(a == 0, axis=-1)
        a = jnp.where(pad_mask[..., None], -jnp.inf, a)
        a = jax.nn.softmax(a, axis=-1)
        a = jnp.nan_to_num(a)
        o = jnp.einsum('bhnm,bmhd->bnhd', a, v).reshape(B, N, HIDDEN)
        return o @ Wo.T + bo
    x = _layernorm(x + _L0_gnn_ref(x, adj, L0_gnn_W_left, L0_gnn_W_right, L0_gnn_W_lin, L0_gnn_b_lin, L0_gnn_ln_a, L0_gnn_ln_b), axis=-1)
    x = _layernorm(x + _L1_gnn_ref(x, adj, adj, L1_gnn_Wq, L1_gnn_Wk, L1_gnn_Wv, L1_gnn_bv, L1_gnn_Wo, L1_gnn_bo), axis=-1)
    x = _layernorm(x + _L2_gnn_ref(x, adj, L2_gnn_Wl, L2_gnn_bl, L2_gnn_Ws, L2_gnn_bs, L2_gnn_Wr, L2_gnn_br, L2_gnn_ln_w, L2_gnn_ln_b), axis=-1)
    x = _layernorm(x + _L3_gnn_ref(x, adj, L3_gnn_Wq, L3_gnn_Wk, L3_gnn_Wv, L3_gnn_bv, L3_gnn_Wo, L3_gnn_bo), axis=-1)
    return x

_drawn_inputs = setup_inputs


def setup_inputs(seed=0):
    import zlib

    import numpy as np

    out = dict(_drawn_inputs(seed))
    spreads = {'L0_gnn_b_lin': (0.0, 0.1),
     'L0_gnn_ln_a': (1.0, 0.2),
     'L0_gnn_ln_b': (0.0, 0.1),
     'L2_gnn_bl': (0.0, 0.1),
     'L2_gnn_bs': (0.0, 0.39),
     'L2_gnn_br': (0.0, 0.1),
     'L2_gnn_ln_w': (1.0, 0.2),
     'L2_gnn_ln_b': (0.0, 0.1)}
    factors = {'L1_gnn_Wq': 8.0,
     'L1_gnn_Wk': 8.0,
     'L1_gnn_bv': 4.792,
     'L3_gnn_Wq': 2.762,
     'L3_gnn_Wk': 2.767,
     'L3_gnn_bv': 5.823,
     'L3_gnn_bo': 6.423}
    for name, (base, spread) in spreads.items():
        noise = np.random.default_rng([zlib.crc32(name.encode()), seed]).standard_normal(out[name].shape)
        drawn = base * np.exp(spread * noise) if base else spread * noise
        out[name] = jnp.asarray(drawn.astype(out[name].dtype))
    for name, factor in factors.items():
        out[name] = (out[name] * factor).astype(out[name].dtype)
    return out
```

```python
from contextlib import ExitStack

import concourse.bass as bass
from concourse import mybir

P = 128
NG = 64
D = 384
C = D // P
PAIRS = NG // 2
T = 2 * P
HEADS = 12
HD = D // HEADS
HB = HEADS // 2
WSCALE = 64.0
DESCALE = 1.0 / WSCALE
TEMPER = float(D) ** 0.5

F32 = mybir.dt.float32
F16 = mybir.dt.float16
ALU = mybir.AluOpType
ACT = mybir.ActivationFunctionType
AX_X = mybir.AxisListType.X

WEIGHTS = (["L0_left0", "L0_right0", "L0_lin0", "L0_left1", "L0_right1", "L0_lin1"]
           + ["L1_q", "L1_k", "L1_v", "L1_o"]
           + ["L2_l0", "L2_s0", "L2_r0", "L2_l1", "L2_s1", "L2_r1"]
           + ["L3_q", "L3_k", "L3_v", "L3_o"])

JOBS = {
    "L0": ("I", "mL0", "mR0", "U0", "H0", "C0", "T0", "mL1", "mR1", "U1", "H1", "C1"),
    "L2": ("I", "S0", "X0", "hl0", "hr0", "hs0", "C0", "T0", "S1", "X1", "hl1", "hr1", "hs1", "C1"),
    "L1": ("I", "Q", "K", "V", "S0", "S1", "X0", "S2", "X1", "P0", "S3", "X2", "X3", "P1", "T", "Y"),
}
JOBS["L3"] = JOBS["L1"]

LAG = {"L0": 0, "L1": 0, "L2": 1, "L3": 2}
PARTNER = {"L0": "L2", "L2": "L0", "L1": "L3", "L3": "L1"}
FIRST = {"L0": "L0", "L2": "L0", "L1": "L1", "L3": "L1"}
VECTOR_LINKS = 36
LOOP_START = 3

STEPS = {
    "L0": """load masks I I.hi I.lo mL0 mL0.hi mL0.lo mR0 mR0.hi mR0.lo U0 U0.mask U0.add H0 U0.exp U0.adj H0.out
             C0 C0.ctx C0.root C0.shift C0.norm T0 T0.gain T0.relu T0.lo
             mL1 mL1.hi mL1.lo mR1 mR1.hi mR1.lo U1 U1.mask U1.add H1 U1.exp U1.adj H1.out
             C1 C1.ctx C1.root C1.shift C1.norm F.affine F.res F.root F.shift F.norm""",
    "L2": """load I I.hi I.lo S0 S0.max S0.exp S0.delta X0 X0.mask hl0 hl0.out hl0.bias hr0 hr0.out hr0.bias
             hs0 hs0.out C0 C0.ctx C0.root C0.shift C0.norm T0 T0.gain T0.relu T0.lo
             S1 S1.max S1.exp S1.delta X1 X1.mask hl1 hl1.out hl1.bias hr1 hr1.out hr1.bias
             hs1 hs1.out C1 C1.ctx C1.root C1.shift C1.norm F.affine F.res F.root F.shift F.norm""",
    "L1": """load I I.hi I.lo Q Q.hi Q.lo Q.stack K K.hi K.lo K.stack xb V V.out V.hi V.lo
             S0 S0.max S0.center S1 S0.exp S1.max S1.center X0 X0.hi X0.lo S1.exp S2 S2.max S2.center X1 X1.hi X1.lo
             S2.exp P0 P0.out S3 S3.max S3.center X2 X2.hi X2.lo S3.exp X3 X3.hi X3.lo P1 P1.out
             T T.hi T.lo Y Y.res Y.root Y.shift Y.norm store""",
}
STEPS["L3"] = STEPS["L1"]


def merged(a, b):
    x = [((n + 0.5) / len(STEPS[a].split()), a, s) for n, s in enumerate(STEPS[a].split())]
    y = [((n + 0.6) / len(STEPS[b].split()), b, s) for n, s in enumerate(STEPS[b].split())]
    return [(k, 0, s) for _, k, s in sorted(x + y, key=lambda e: e[0])]


ORDER = merged("L0", "L3") + merged("L2", "L1")


class Turn:

    def __init__(self, k, reg=None):
        self.k, self.reg = k, reg

    def before(self):
        return Turn(self.k - 1, self.reg)

    def from_on(self, k):
        return self.reg is not None or self.k >= k

    def index(self, lag):
        return self.k - lag if self.reg is None else self.reg + (self.k - lag)


def blocks_before(kind, turn):
    k = turn.k
    n1, n2 = {"L0": (k, k - 1), "L2": (k + 1, k - 1), "L1": (k, k - 1), "L3": (k, k - 2)}[kind]
    if turn.reg is None:
        n1, n2 = (min(max(n, 0), PAIRS) for n in (n1, n2))
    return n1, n2


class Signal:

    def __init__(self, sem, events, step=1):
        self.sem, self.events, self.step = sem, events, step

    def at(self, kind, event, turn, back=0):
        first = FIRST[kind]
        c1, c2 = len(self.events.get(first, ())), len(self.events.get(PARTNER[first], ()))
        n1, n2 = blocks_before(kind, turn)
        b = (c1 * n1 + c2 * n2 + self.events[kind].index(event) + 1 - back) * self.step
        return b if turn.reg is None else turn.reg * ((c1 + c2) * self.step) + b

    def again(self, kind, event, turn):
        return turn.reg is not None or self.at(kind, event, turn, back=1) > 0


class Slots:

    def __init__(self, full, evacuated, tensors):
        self.full, self.evacuated, self.tensors = full, evacuated, tensors

    def number(self, kind, job, turn):
        first = FIRST[kind]
        c1, c2 = len(JOBS[first]), len(JOBS[PARTNER[first]])
        assert (c1 + c2) % 2 == 0
        n1, n2 = blocks_before(kind, turn)
        return c1 * n1 + c2 * n2 + JOBS[kind].index(job), c1 + c2

    def tile(self, kind, job, turn):
        return self.tensors[self.number(kind, job, turn)[0] % 2]

    def evac(self, kind, job, turn):
        return self.evacuated[self.number(kind, job, turn)[0] % 2]

    def full_at(self, kind, job, turn):
        n, per = self.number(kind, job, turn)
        return n + 1 if turn.reg is None else turn.reg * per + (n + 1)

    def evac_at(self, kind, job, turn, back=0):
        n, per = self.number(kind, job, turn)
        v = n // 2 + 1 - back
        return v if turn.reg is None else turn.reg * (per // 2) + v

    def free_at(self, kind, job, turn):
        return self.evac_at(kind, job, turn, back=1)

    def used(self, kind, job, turn):
        return turn.reg is not None or self.free_at(kind, job, turn) > 0


def graph_stack_kernel(nc, x, adj, adj_t, weights_t, vectors, out):
    ctx = ExitStack()
    with ctx:
        def sb(name, shape, dt=F32):
            return ctx.enter_context(nc.sbuf_tensor(name, shape, dt))

        def sem(name):
            return ctx.enter_context(nc.semaphore(name))

        w_hi = sb("w_hi", [P, len(WEIGHTS), C, D], F16)
        w_lo = sb("w_lo", [P, len(WEIGHTS), C, D], F16)
        rows = {n: sb(f"row_{n}", [P, D]) for n in (
            "L0_b0", "L0_b1", "L0_a", "L0_c", "L1_bv", "L1_bo", "L2_bl0", "L2_bs0", "L2_br0",
            "L2_bl1", "L2_bs1", "L2_br1", "L2_a", "L2_c", "L3_bv", "L3_bo")}
        cols = {n: sb(f"col_{n}", [P, C]) for n in ("L0_a", "L0_c", "L2_a", "L2_c")}
        ident = sb("ident", [P, P])
        tri_scaled = sb("tri_scaled", [P, 2, P])
        tri_strict = sb("tri_strict", [P, 2, P])
        half = sb("half", [P, 2])
        neg_half = sb("neg_half", [P, 2])

        x0 = sb("x0", [P, 2, D])
        x1 = sb("x1", [P, 2, D])
        x2 = sb("x2", [P, 2, D])
        x3 = sb("x3", [P, 2, D])
        x4 = sb("x4", [P, 2, D])
        x_in = {"L0": x0, "L1": x1, "L2": x2, "L3": x3}
        x_out = {"L0": x1, "L1": x2, "L2": x3, "L3": x4}
        adj01 = sb("adj01", [P, 2, P])
        adjt0 = sb("adjt0", [P, 2, P])
        adj2 = sb("adj2", [P, 2, P])
        adj3 = sb("adj3", [P, 2, P])
        adj_of = {"L1": adj01, "L3": adj3}

        g_ht_hi = sb("g_ht_hi", [P, C, T], F16)
        g_ht_lo = sb("g_ht_lo", [P, C, T], F16)
        m_all = sb("m_all", [P, 4 * C * T], F16)
        m_hi = [m_all[:, s * 2 * C * T:s * 2 * C * T + C * T].rearrange("p (c t) -> p c t", c=C) for s in range(2)]
        m_lo = [m_all[:, s * 2 * C * T + C * T:(s + 1) * 2 * C * T].rearrange("p (c t) -> p c t", c=C)
                for s in range(2)]
        h_r = m_all[:, 0:2 * C * T].bitcast(F32).rearrange("p (g d) -> p g d", g=2)
        h_s = m_all[:, 2 * C * T:4 * C * T].bitcast(F32).rearrange("p (g d) -> p g d", g=2)
        h_l = sb("h_l", [P, 2, D + 1])
        masks = sb("masks", [P, 2, 2, P])
        gated = sb("gated", [P, 2, 2, P])
        logits = sb("logits", [P, 2, P])
        expu = sb("expu", [P, 2, P])
        exp_adj = sb("exp_adj", [P, 2, P])
        t32 = sb("t32", [P, C, T])
        g_z = sb("g_z", [P, 2, D])
        g_small = sb("g_small", [P, 64])

        a_ht_hi = sb("a_ht_hi", [P, C, T], F16)
        a_ht_lo = sb("a_ht_lo", [P, C, T], F16)
        qk_hi = [sb(f"qk_hi{n}", [P, C, T], F16) for n in range(2)]
        qk_lo = [sb(f"qk_lo{n}", [P, C, T], F16) for n in range(2)]
        stack = [sb("stack_q", [P, HEADS, T], F16), sb("stack_k", [P, HEADS, T], F16)]
        row_a = sb("row_a", [P, 2, D])
        v_hi = sb("v_hi", [P, 2, HEADS, HD + 1], F16)
        v_lo = sb("v_lo", [P, 2, HEADS, HD], F16)
        sc = sb("sc", [P, 2, HB, P])
        pt_hi = sb("pt_hi", [P, HEADS, P], F16)
        pt_lo = sb("pt_lo", [P, HEADS, P], F16)
        row_max = sb("row_max", [P, 4, HB])
        a_z = sb("a_z", [P, 2, D])
        a_small = sb("a_small", [P, 96])

        def rows_of(tile, width):
            return tile[:, :].rearrange("p (g n) -> p g n", g=2)[:, :, 0:width]

        def both_graphs(row):
            return row[:, :].unsqueeze(1).to_broadcast([P, 2, D])

        def features_of(tile):
            return tile[:, 0:C * T].rearrange("p (c t) -> p c t", c=C)

        def heads_of(tile):
            return tile[:, 0:HB * P].rearrange("p (h n) -> p h n", n=P)

        staging = [sc[:, :, :, :].rearrange("p b h n -> p (b h n)")]
        staging += [s[:, :, :].rearrange("p h t -> p (h t)").bitcast(F32) for s in stack]
        staging = [s[:, 0:C * D].rearrange("p (c o) -> p c o", c=C) for s in staging]

        psum = [ctx.enter_context(nc.psum_tensor(f"ps{n}", [P, 1024], F32)) for n in range(4)]

        load_w = [sem(f"load_w{n}") for n in range(3)]
        weight_split = sem("weight_split")
        weight_hi = sem("weight_hi")
        params_loaded = sem("params_loaded")
        consts_filled = sem("consts_filled")
        consts_ready = sem("consts_ready")
        ones_ready = sem("ones_ready")
        vector_link = sem("vector_link")

        gnn = Slots(sem("gnn_full"), [sem("gnn_evac0"), sem("gnn_evac1")], psum[0:2])
        att = Slots(sem("att_full"), [sem("att_evac0"), sem("att_evac1")], psum[2:4])
        slots = {"L0": gnn, "L2": gnn, "L1": att, "L3": att}

        def signal(name, events, step=1):
            return Signal(sem(name), events, step)

        def both_att(*events):
            return {"L1": events, "L3": events}

        x0_loaded = signal("x0_loaded", {"L0": ("x",)}, 16)
        adj01_loaded = signal("adj01_loaded", {"L0": ("x",)}, 32)
        adj2_loaded = signal("adj2_loaded", {"L2": ("x",)}, 16)
        adj3_loaded = signal("adj3_loaded", {"L3": ("x",)}, 16)
        x4_stored = signal("x4_stored", {"L3": ("x",)}, 16)
        norms = {"L0": ("C0", "C1", "F"), "L2": ("C0", "C1", "F")}
        g_hi = signal("g_hi", {"L0": ("I", "mL0", "mR0", "T0", "mL1", "mR1"), "L2": ("I", "T0")})
        g_masks = signal("g_masks", {"L0": ("x",)})
        g_logits = signal("g_logits", {"L0": ("0", "1")})
        g_expu = signal("g_expu", {"L0": ("0", "1")})
        g_exp_adj = signal("g_exp_adj", {"L0": ("0", "1"), "L2": ("0", "1")})
        g_negmax = signal("g_negmax", {"L2": ("0", "1")})
        g_biased = signal("g_biased", {"L2": ("hl0", "hr0", "hl1", "hr1")})
        g_var = signal("g_var", norms)
        g_root = signal("g_root", norms)
        g_shift = signal("g_shift", norms)
        g_norm = signal("g_norm", norms)
        g_affine = signal("g_affine", {"L0": ("mul", "add"), "L2": ("mul", "add")})
        g_gained = signal("g_gained", {"L0": ("x",), "L2": ("x",)})
        g_resid = signal("g_resid", {"L0": ("x",), "L2": ("x",)})
        a_hi = signal("a_hi", both_att("I", "Q", "K", "V", "X0", "X1", "X2", "X3", "T"))
        a_stacked = signal("a_stacked", both_att("Q", "K"), 12 * 16)
        a_vlo = signal("a_vlo", both_att("x"))
        a_max = signal("a_max", both_att("0", "1", "2", "3"))
        a_centered = signal("a_centered", both_att("0", "1", "2", "3"))
        a_exp = signal("a_exp", both_att("0", "1", "2", "3"))
        a_xb = signal("a_xb", both_att("x"))
        a_var = signal("a_var", both_att("x"))
        a_root = signal("a_root", both_att("x"))
        a_shift = signal("a_shift", both_att("x"))
        a_norm = signal("a_norm", both_att("x"))

        def steps_of(turn):
            for kind, back, step in ORDER:
                if turn.reg is not None or 0 <= turn.k - back - LAG[kind] < PAIRS:
                    job, _, part = step.partition(".")
                    yield kind, job, part, (turn.before() if back else turn)

        links = {"n": 0}
        block = ctx.enter_context(nc.Block())

        @block.sync
        def _(sp):
            for n in range(len(WEIGHTS)):
                if n >= 3:
                    sp.wait_ge(weight_split, n - 2)
                sp.dma_start(staging[n % 3], weights_t[n].rearrange("(c p) o -> p c o", p=P)).then_inc(load_w[n % 3], 16)
                if n == 2:
                    for name, tile in rows.items():
                        sp.dma_start(tile[:, :], vectors[name].unsqueeze(0).to_broadcast([P, D]))\
                          .then_inc(params_loaded, 16)
                    for name, tile in cols.items():
                        sp.dma_start(tile[:, :], vectors["col_" + name]).then_inc(params_loaded, 16)

            x_pairs = x.rearrange("(q g) n d -> q n g d", g=2)
            out_pairs = out.rearrange("(q g) n d -> q n g d", g=2)
            adj_pairs = adj.rearrange("(q g) i j -> q i g j", g=2)
            adjt_pairs = adj_t.rearrange("(q g) i j -> q i g j", g=2)

            def do(kind, job, part, turn):
                pair = turn.index(LAG[kind])
                if (kind, job) == ("L0", "load"):
                    if turn.from_on(1):
                        sp.wait_ge(g_resid.sem, g_resid.at("L0", "x", turn.before()))
                    sp.dma_start(x0[:, :, :], x_pairs[pair]).then_inc(x0_loaded.sem, 16)
                    if turn.from_on(1):
                        sp.wait_ge(att.evac("L1", "S3", turn.before()), att.evac_at("L1", "S3", turn.before()))
                        sp.wait_ge(g_exp_adj.sem, g_exp_adj.at("L0", "1", turn.before()))
                    sp.dma_start(adj01[:, :, :], adj_pairs[pair]).then_inc(adj01_loaded.sem, 16)
                    sp.dma_start(adjt0[:, :, :], adjt_pairs[pair]).then_inc(adj01_loaded.sem, 16)
                elif (kind, job) == ("L2", "load"):
                    if turn.from_on(2):
                        sp.wait_ge(g_exp_adj.sem, g_exp_adj.at("L2", "1", turn.before()))
                    sp.dma_start(adj2[:, :, :], adj_pairs[pair]).then_inc(adj2_loaded.sem, 16)
                elif (kind, job) == ("L3", "load"):
                    if turn.from_on(3):
                        sp.wait_ge(att.evac("L3", "S3", turn.before()), att.evac_at("L3", "S3", turn.before()))
                    sp.dma_start(adj3[:, :, :], adj_pairs[pair]).then_inc(adj3_loaded.sem, 16)
                elif part == "stack":
                    n = "QK".index(job)
                    sp.wait_ge(att.evac(kind, job, turn), att.evac_at(kind, job, turn))
                    for third, src in enumerate((qk_hi, qk_lo if n else qk_hi, qk_hi if n else qk_lo)):
                        for r in range(4):
                            sp.dma_start(stack[n][32 * third:32 * third + 32, r:HEADS:4, :],
                                         src[n][32 * r:32 * r + 32, :, :]).then_inc(a_stacked.sem, 16)
                elif (kind, job) == ("L3", "store"):
                    sp.wait_ge(a_norm.sem, a_norm.at("L3", "x", turn))
                    sp.dma_start(out_pairs[pair], x4[:, :, :]).then_inc(x4_stored.sem, 16)

            for n in range(LOOP_START):
                for step in steps_of(Turn(n)):
                    do(*step)
            with sp.Fori(LOOP_START, PAIRS) as reg:
                for step in steps_of(Turn(0, reg)):
                    do(*step)
            for n in range(PAIRS, PAIRS + 3):
                for step in steps_of(Turn(n)):
                    do(*step)
            sp.wait_ge(x4_stored.sem, 16 * PAIRS)

        @block.tensor
        def _(pe):
            def split_products(tile, stationary, moving, last):
                (a_hi_, a_lo_), (b_hi_, b_lo_) = stationary, moving
                for k in range(C):
                    for n, (a, b) in enumerate(((a_hi_, b_hi_), (a_hi_, b_lo_), (a_lo_, b_hi_))):
                        mm = pe.matmul(tile, a(k), b(k), start=(k == 0 and n == 0), stop=(k == C - 1 and n == 2))
                if last is not None:
                    mm.then_inc(last, 1)

            def feature_projection(tile, weight, ht, full):
                w = WEIGHTS.index(weight)
                for o in range(C):
                    cols_ = slice(o * P, (o + 1) * P)
                    split_products(tile[:, o * T:(o + 1) * T],
                                   [lambda k, m=m: m[:, w, k, cols_] for m in (w_hi, w_lo)],
                                   [lambda k, h=h: h[:, k, :] for h in ht], full if o == C - 1 else None)

            def row_projection(tile, weight, ht, full):
                w = WEIGHTS.index(weight)
                for g in range(2):
                    nodes = slice(g * P, (g + 1) * P)
                    split_products(tile[:, g * 512:g * 512 + D],
                                   [lambda k, h=h: h[:, k, nodes] for h in ht],
                                   [lambda k, m=m: m[:, w, k, :] for m in (w_hi, w_lo)], full if g else None)

            def transpose_rows(tile, source, full):
                for c in range(C):
                    for g in range(2):
                        mm = pe.transpose(tile[:, c * T + g * P:c * T + (g + 1) * P],
                                          source[:, g, c * P:(c + 1) * P], ident[:, :])
                mm.then_inc(full, 1)

            pe.wait_ge(consts_ready, 3)
            pe.wait_ge(weight_split, len(WEIGHTS))
            pe.wait_ge(ones_ready, 2)
            g_ht, a_ht = (g_ht_hi, g_ht_lo), (a_ht_hi, a_ht_lo)

            def do(kind, job, part, turn):
                if part or job not in JOBS[kind]:
                    return
                s = slots[kind]
                tile, full = s.tile(kind, job, turn), s.full
                base, l = job.rstrip("0123"), job[-1]
                if s.used(kind, job, turn):
                    pe.wait_ge(s.evac(kind, job, turn), s.free_at(kind, job, turn))

                if job == "I":
                    if kind == "L0":
                        pe.wait_ge(x0_loaded.sem, x0_loaded.at("L0", "x", turn))
                    elif kind == "L1":
                        pe.wait_ge(g_norm.sem, g_norm.at("L0", "F", turn))
                    elif kind == "L2":
                        pe.wait_ge(a_norm.sem, a_norm.at("L1", "x", turn.before()))
                    else:
                        pe.wait_ge(g_norm.sem, g_norm.at("L2", "F", turn.before()))
                    transpose_rows(tile, x_in[kind], full)

                elif base in ("mL", "mR"):
                    if base == "mL":
                        ready = "I" if l == "0" else "T0"
                        pe.wait_ge(gnn.evac(kind, ready, turn), gnn.evac_at(kind, ready, turn))
                    feature_projection(tile, ("L0_left" if base == "mL" else "L0_right") + l, g_ht, full)

                elif base == "U":
                    pe.wait_ge(gnn.evac(kind, "mL" + l, turn), gnn.evac_at(kind, "mL" + l, turn))
                    pe.wait_ge(gnn.evac(kind, "mR" + l, turn), gnn.evac_at(kind, "mR" + l, turn))
                    for side in range(2):
                        for g in range(2):
                            at, n = (2 * side + g) * P, slice(g * P, (g + 1) * P)
                            split_products(tile[:, at:at + P],
                                           [lambda k, m=m: m[:, k, n] for m in (m_hi[side], m_lo[side])],
                                           [lambda k, h=h: h[:, k, n] for h in g_ht],
                                           full if side and g else None)

                elif base == "H":
                    row_projection(tile, "L0_lin" + l, g_ht, full)

                elif base == "C" and kind == "L0":
                    pe.wait_ge(gnn.evac(kind, "H" + l, turn), gnn.evac_at(kind, "H" + l, turn))
                    pe.wait_ge(g_exp_adj.sem, g_exp_adj.at(kind, l, turn))
                    for g in range(2):
                        mm = pe.matmul(tile[:, g * 512:g * 512 + D + 1], exp_adj[:, g, :], h_l[:, g, :],
                                       start=True, stop=True)
                    mm.then_inc(full, 1)

                elif base == "C":
                    pe.wait_ge(gnn.evac(kind, "X" + l, turn), gnn.evac_at(kind, "X" + l, turn))
                    pe.wait_ge(g_biased.sem, g_biased.at(kind, "hr" + l, turn))
                    for g in range(2):
                        for side, h in enumerate((h_l, h_r)):
                            mm = pe.matmul(tile[:, g * 512:g * 512 + D], gated[:, side, g, :], h[:, g, 0:D],
                                           start=(side == 0), stop=(side == 1))
                    mm.then_inc(full, 1)

                elif kind == "L2" and base == "S":
                    ready = "I" if l == "0" else "T0"
                    pe.wait_ge(gnn.evac(kind, ready, turn), gnn.evac_at(kind, ready, turn))
                    for g in range(2):
                        n = slice(g * P, (g + 1) * P)
                        h_pair = [lambda k, h=h: h[:, k, n] for h in g_ht]
                        split_products(tile[:, n], h_pair, h_pair, full if g else None)

                elif kind == "L2" and base == "X":
                    pe.wait_ge(g_exp_adj.sem, g_exp_adj.at(kind, l, turn))
                    for g in range(2):
                        mm = pe.transpose(tile[:, g * P:(g + 1) * P], exp_adj[:, g, :], ident[:, :])
                    mm.then_inc(full, 1)

                elif base in ("hl", "hr", "hs"):
                    row_projection(tile, f"L2_{base[1]}{l}", g_ht, full)

                elif job == "T0":
                    pe.wait_ge(g_norm.sem, g_norm.at(kind, "C0", turn))
                    transpose_rows(tile, g_z, full)

                elif job in ("Q", "K"):
                    if job == "Q":
                        pe.wait_ge(att.evac(kind, "I", turn), att.evac_at(kind, "I", turn))
                    feature_projection(tile, f"{kind}_{job.lower()}", a_ht, full)

                elif job == "V":
                    row_projection(tile, f"{kind}_v", a_ht, full)

                elif base == "S":
                    b = int(l)
                    if b == 0:
                        pe.wait_ge(a_stacked.sem, a_stacked.at(kind, "K", turn))
                    n = slice(b // 2 * P, (b // 2 + 1) * P)
                    for h in range(HB):
                        head = HB * (b % 2) + h
                        mm = pe.matmul(tile[:, h * P:(h + 1) * P], stack[0][0:96, head, n], stack[1][0:96, head, n],
                                       start=True, stop=True)
                    mm.then_inc(full, 1)

                elif base == "X":
                    pe.wait_ge(a_exp.sem, a_exp.at(kind, l, turn))
                    for h in range(HB):
                        mm = pe.transpose(tile[:, h * P:(h + 1) * P], sc[:, int(l) % 2, h, :], ident[:, :])
                    mm.then_inc(full, 1)

                elif base == "P":
                    g = int(l)
                    if g == 1:
                        pe.wait_ge(att.evac(kind, "X2", turn), att.evac_at(kind, "X2", turn))
                    last_x = f"X{2 * g + 1}"
                    pe.wait_ge(att.evac(kind, last_x, turn), att.evac_at(kind, last_x, turn))
                    if g == 0:
                        pe.wait_ge(a_hi.sem, a_hi.at(kind, "V", turn))
                        pe.wait_ge(a_vlo.sem, a_vlo.at(kind, "x", turn))
                    for h in range(HEADS):
                        at = h * (HD + 1)
                        pe.matmul(tile[:, at:at + HD + 1], pt_hi[:, h, :], v_hi[:, g, h, :], start=True, stop=False)
                        pe.matmul(tile[:, at:at + HD], pt_hi[:, h, :], v_lo[:, g, h, :], start=False, stop=False,
                                  skip_group_check=True)
                        mm = pe.matmul(tile[:, at:at + HD + 1], pt_lo[:, h, :], v_hi[:, g, h, :],
                                       start=False, stop=True)
                    mm.then_inc(full, 1)

                elif job == "T":
                    pe.wait_ge(att.evac(kind, "P1", turn), att.evac_at(kind, "P1", turn))
                    transpose_rows(tile, row_a, full)

                elif job == "Y":
                    pe.wait_ge(att.evac(kind, "T", turn), att.evac_at(kind, "T", turn))
                    row_projection(tile, f"{kind}_o", a_ht, full)

            for n in range(LOOP_START):
                for step in steps_of(Turn(n)):
                    do(*step)
            with pe.Fori(LOOP_START, PAIRS) as reg:
                for step in steps_of(Turn(0, reg)):
                    do(*step)
            for n in range(PAIRS, PAIRS + 3):
                for step in steps_of(Turn(n)):
                    do(*step)

        @block.scalar
        def _(act):
            for n in range(len(WEIGHTS)):
                act.wait_ge(load_w[n % 3], 16 * (n // 3 + 1))
                act.activation(w_hi[:, n], staging[n % 3], ACT.Copy, scale=WSCALE).then_inc(weight_hi, 1)

            def normalise(z, small, dst, norm):
                for g in range(2):
                    a = act.activation(dst[:, g, :], z[:, g, :], ACT.Identity, bias=small[:, 30 + g:31 + g],
                                       scale=small[:, 28 + g:29 + g])
                a.then_inc(norm.sem, 1)

            hi_of = {"mL": (m_hi[0], DESCALE), "mR": (m_hi[1], DESCALE), "Q": (qk_hi[0], DESCALE / TEMPER),
                     "K": (qk_hi[1], DESCALE), "T": (a_ht_hi, 1.0)}

            def do(kind, job, part, turn):
                s = slots[kind]
                base, l = job.rstrip("0123"), job[-1]
                hi = g_hi if s is gnn else a_hi

                if part == "hi" and base in ("I", "mL", "mR", "Q", "K", "T"):
                    dst, scale = ((g_ht_hi if s is gnn else a_ht_hi), 1.0) if base == "I" else hi_of[base]
                    act.wait_ge(s.full, s.full_at(kind, job, turn))
                    act.activation(dst[:, :, :], features_of(s.tile(kind, job, turn)), ACT.Copy, scale=scale)\
                       .then_inc(hi.sem, 1)

                elif part == "hi" and base == "X":
                    act.wait_ge(att.full, att.full_at(kind, job, turn))
                    h0 = HB * (int(l) % 2)
                    act.activation(pt_hi[:, h0:h0 + HB, :], heads_of(att.tile(kind, job, turn)), ACT.Copy)\
                       .then_inc(a_hi.sem, 1)

                elif part == "hi" and job == "V":
                    act.wait_ge(att.evac(kind, "V", turn), att.evac_at(kind, "V", turn))
                    act.activation(v_hi[:, :, :, 0:HD], row_a[:, :, :].rearrange("p g (h d) -> p g h d", d=HD),
                                   ACT.Copy).then_inc(a_hi.sem, 1)

                elif part == "relu":
                    act.wait_ge(g_gained.sem, g_gained.at(kind, "x", turn))
                    act.activation(g_ht_hi[:, :, :], t32[:, :, :], ACT.Relu).then_inc(g_hi.sem, 1)

                elif part == "out" and base in ("H", "hl", "hr"):
                    act.wait_ge(gnn.full, gnn.full_at(kind, job, turn))
                    act.activation((h_r if base == "hr" else h_l)[:, :, 0:D], rows_of(gnn.tile(kind, job, turn), D),
                                   ACT.Copy, scale=DESCALE).then_inc(gnn.evac(kind, job, turn), 1)

                elif kind == "L0" and part == "exp":
                    act.wait_ge(g_logits.sem, g_logits.at("L0", l, turn))
                    act.activation(expu[:, :, :], logits[:, :, :], ACT.Exp).then_inc(g_expu.sem, 1)

                elif kind == "L2" and part == "exp":
                    act.wait_ge(g_negmax.sem, g_negmax.at("L2", l, turn))
                    tile = gnn.tile("L2", job, turn)
                    for g in range(2):
                        e = act.activation(expu[:, g, :], tile[:, g * P:(g + 1) * P], ACT.Exp,
                                           bias=g_small[:, 42 + g:43 + g], scale=1.0 / TEMPER,
                                           accum_out=g_small[:, 44 + g:45 + g])
                    e.then_inc(gnn.evac("L2", job, turn), 1)

                elif part == "exp":
                    act.wait_ge(a_centered.sem, a_centered.at(kind, l, turn))
                    act.activation(sc[:, int(l) % 2], sc[:, int(l) % 2], ACT.Exp).then_inc(a_exp.sem, 1)

                elif part == "norm" and base == "C":
                    act.wait_ge(g_shift.sem, g_shift.at(kind, job, turn))
                    normalise(g_z, g_small, g_z, g_norm)

                elif part == "norm" and base == "F":
                    act.wait_ge(g_shift.sem, g_shift.at(kind, job, turn))
                    if kind == "L0" and turn.from_on(1):
                        act.wait_ge(att.evac("L1", "Y", turn.before()), att.evac_at("L1", "Y", turn.before()))
                    if kind == "L2" and turn.from_on(2):
                        act.wait_ge(att.evac("L3", "Y", turn), att.evac_at("L3", "Y", turn))
                    normalise(g_z, g_small, x_out[kind], g_norm)

                elif part == "norm":
                    act.wait_ge(a_shift.sem, a_shift.at(kind, "x", turn))
                    if kind == "L1" and turn.from_on(1):
                        act.wait_ge(g_resid.sem, g_resid.at("L2", "x", turn))
                    if kind == "L3" and turn.from_on(3):
                        act.wait_ge(x4_stored.sem, x4_stored.at("L3", "x", turn, back=1))
                    normalise(a_z, a_small, x_out[kind], a_norm)

            for n in range(LOOP_START):
                for step in steps_of(Turn(n)):
                    do(*step)
            with act.Fori(LOOP_START, PAIRS) as reg:
                for step in steps_of(Turn(0, reg)):
                    do(*step)
            for n in range(PAIRS, PAIRS + 3):
                for step in steps_of(Turn(n)):
                    do(*step)

        @block.vector
        def _(dve):
            def linked(turn):
                links["n"] += 1
                if turn.reg is None:
                    return links["n"]
                return turn.reg * VECTOR_LINKS + (links["n"] - LOOP_START * VECTOR_LINKS)

            dve.memset(h_l[:, :, :], 1.0).then_inc(ones_ready, 1)
            dve.memset(v_hi[:, :, :, :], 1.0).then_inc(ones_ready, 1)
            for n in range(len(WEIGHTS)):
                dve.wait_ge(weight_hi, n + 1)
                dve.scalar_tensor_tensor(w_lo[:, n], staging[n % 3], WSCALE, w_hi[:, n], ALU.mult, ALU.subtract)\
                   .then_inc(weight_split, 1)
            dve.wait_ge(params_loaded, 16 * (len(rows) + len(cols)))
            dve.wait_ge(consts_ready, 3)

            def stats(z, small, turn):
                dve.bn_stats(small[:, 0:6], z[:, 0, :])
                dve.bn_stats(small[:, 6:12], z[:, 1, :])
                dve.drain()
                dve.bn_aggr(small[:, 16:18], small[:, 0:6])
                dve.bn_aggr(small[:, 18:20], small[:, 6:12]).then_inc(vector_link, 1)
                dve.wait_ge(vector_link, linked(turn))

            def means(small):
                return small[:, 16:20].rearrange("p (g s) -> p g s", s=2)[:, :, 0]

            def variances(small):
                return small[:, 16:20].rearrange("p (g s) -> p g s", s=2)[:, :, 1]

            lo_of = {"mL": (m_hi[0], m_lo[0], DESCALE), "mR": (m_hi[1], m_lo[1], DESCALE),
                     "Q": (qk_hi[0], qk_lo[0], DESCALE / TEMPER), "K": (qk_hi[1], qk_lo[1], DESCALE),
                     "T": (a_ht_hi, a_ht_lo, 1.0)}

            def do(kind, job, part, turn):
                s = slots[kind]
                base, l = job.rstrip("0123"), job[-1]

                if part == "lo" and base in ("I", "mL", "mR", "Q", "K") or (part == "lo" and job == "T"):
                    hi = g_hi if s is gnn else a_hi
                    dst_hi, dst_lo, scale = lo_of[base] if base != "I" else (
                        (g_ht_hi, g_ht_lo, 1.0) if s is gnn else (a_ht_hi, a_ht_lo, 1.0))
                    dve.wait_ge(hi.sem, hi.at(kind, job, turn))
                    dve.scalar_tensor_tensor(dst_lo[:, :, :], features_of(s.tile(kind, job, turn)), scale,
                                             dst_hi[:, :, :], ALU.mult, ALU.subtract)\
                       .then_inc(s.evac(kind, job, turn), 1)

                elif part == "lo" and job == "T0":
                    dve.wait_ge(g_hi.sem, g_hi.at(kind, "T0", turn))
                    dve.scalar_tensor_tensor(g_ht_lo[:, :, :], t32[:, :, :], 0.0, g_ht_hi[:, :, :],
                                             ALU.max, ALU.subtract).then_inc(gnn.evac(kind, "T0", turn), 1)

                elif part == "gain":
                    dve.wait_ge(gnn.full, gnn.full_at(kind, job, turn))
                    tile = gnn.tile(kind, job, turn)
                    for c in range(C):
                        t = dve.tensor_scalar(t32[:, c, :], tile[:, c * T:(c + 1) * T], cols[f"{kind}_a"][:, c:c + 1],
                                              cols[f"{kind}_c"][:, c:c + 1], ALU.mult, ALU.add)
                    t.then_inc(g_gained.sem, 1)
                    dve.wait_ge(g_gained.sem, g_gained.at(kind, "x", turn))

                elif kind == "L0" and part == "mask":
                    dve.wait_ge(gnn.full, gnn.full_at(kind, job, turn))
                    if l == "0":
                        dve.wait_ge(g_masks.sem, g_masks.at("L0", "x", turn))
                    dve.tensor_tensor(gated[:, :, :, :].rearrange("p s g n -> p (s g n)"),
                                      gnn.tile(kind, job, turn)[:, 0:4 * P],
                                      masks[:, :, :, :].rearrange("p s g n -> p (s g n)"), ALU.mult)\
                       .then_inc(gnn.evac(kind, job, turn), 1)

                elif kind == "L0" and part == "ctx":
                    dve.wait_ge(gnn.full, gnn.full_at(kind, job, turn))
                    if g_norm.again(kind, job, turn):
                        dve.wait_ge(g_norm.sem, g_norm.at(kind, job, turn, back=1))
                    tile = gnn.tile(kind, job, turn)
                    sums = rows_of(tile, D + 1)[:, :, D]
                    dve.tensor_scalar(g_small[:, 20:22], sums, 1e-10, 1e-3, ALU.add, ALU.mult)
                    dve.tensor_copy(g_small[:, 46:48], sums).then_inc(vector_link, 1)
                    dve.wait_ge(vector_link, linked(turn))
                    for g in range(2):
                        z = dve.scalar_tensor_tensor(g_z[:, g, :], rows[f"L0_b{l}"][:, :], g_small[:, 46 + g:47 + g],
                                                     tile[:, g * 512:g * 512 + D], ALU.mult, ALU.add)
                    z.then_inc(gnn.evac(kind, job, turn), 1)
                    dve.wait_ge(gnn.evac(kind, job, turn), gnn.evac_at(kind, job, turn))
                    stats(g_z, g_small, turn)
                    dve.tensor_scalar(g_small[:, 22:24], variances(g_small), D / (D - 1.0), None, ALU.mult)\
                       .then_inc(g_var.sem, 1)

                elif kind == "L0" and base == "C" and part == "shift":
                    dve.wait_ge(g_root.sem, g_root.at("L0", job, turn))
                    dve.tensor_tensor(g_small[:, 26:28], g_small[:, 24:26], g_small[:, 20:22], ALU.add)\
                       .then_inc(vector_link, 1)
                    dve.wait_ge(vector_link, linked(turn))
                    dve.reciprocal(g_small[:, 28:30], g_small[:, 26:28]).then_inc(vector_link, 1)
                    dve.wait_ge(vector_link, linked(turn))
                    dve.scalar_tensor_tensor(g_small[:, 30:32], means(g_small), -1.0, g_small[:, 28:30],
                                             ALU.mult, ALU.mult).then_inc(g_shift.sem, 1)

                elif part == "shift":
                    root, shift, small = (g_root, g_shift, g_small) if s is gnn else (a_root, a_shift, a_small)
                    event = job if s is gnn else "x"
                    dve.wait_ge(root.sem, root.at(kind, event, turn))
                    dve.scalar_tensor_tensor(small[:, 30:32], means(small), -1.0, small[:, 28:30],
                                             ALU.mult, ALU.mult).then_inc(shift.sem, 1)

                elif base == "F" and part == "res":
                    dve.wait_ge(g_affine.sem, g_affine.at(kind, "add", turn))
                    dve.scalar_tensor_tensor(g_z[:, :, :], g_z[:, :, :], 0.0, x_in[kind][:, :, :],
                                             ALU.max, ALU.add).then_inc(g_resid.sem, 1)
                    dve.wait_ge(g_resid.sem, g_resid.at(kind, "x", turn))
                    stats(g_z, g_small, turn)
                    dve.tensor_scalar(g_small[:, 22:24], variances(g_small), 1e-5, None, ALU.add)\
                       .then_inc(g_var.sem, 1)

                elif kind == "L2" and part == "max":
                    dve.wait_ge(gnn.full, gnn.full_at(kind, job, turn))
                    dve.tensor_reduce(g_small[:, 40:42], gnn.tile(kind, job, turn)[:, 0:T]
                                      .rearrange("p (g n) -> p g n", n=P), AX_X, ALU.max).then_inc(vector_link, 1)
                    dve.wait_ge(vector_link, linked(turn))
                    dve.tensor_scalar(g_small[:, 42:44], g_small[:, 40:42], -1.0 / TEMPER, None, ALU.mult)\
                       .then_inc(g_negmax.sem, 1)

                elif kind == "L2" and part == "delta":
                    dve.wait_ge(gnn.evac(kind, job, turn), gnn.evac_at(kind, job, turn))
                    if l == "0":
                        dve.wait_ge(adj2_loaded.sem, adj2_loaded.at("L2", "x", turn))
                    for g in range(2):
                        e = dve.scalar_tensor_tensor(exp_adj[:, g, :], expu[:, g, :], 1.0, adj2[:, g, :],
                                                     ALU.mult, ALU.mult, accum_out=g_small[:, 46 + g:47 + g])
                    e.then_inc(g_exp_adj.sem, 1)
                    dve.wait_ge(g_exp_adj.sem, g_exp_adj.at("L2", l, turn))
                    for g in range(2):
                        dve.scalar_tensor_tensor(logits[:, g, :], exp_adj[:, g, :], 1.0, ident[:, :],
                                                 ALU.mult, ALU.mult, accum_out=g_small[:, 48 + g:49 + g])
                    dve.scalar_tensor_tensor(g_small[:, 50:52], g_small[:, 44:46], 1e-10, g_small[:, 46:48],
                                             ALU.mult, ALU.add).then_inc(vector_link, 1)
                    dve.wait_ge(vector_link, linked(turn))
                    dve.scalar_tensor_tensor(g_small[:, 52:54], g_small[:, 50:52], 1e-12, g_small[:, 50:52],
                                             ALU.mult, ALU.mult).then_inc(vector_link, 1)
                    dve.wait_ge(vector_link, linked(turn))

                elif kind == "L2" and part == "mask":
                    dve.wait_ge(gnn.full, gnn.full_at(kind, job, turn))
                    tile = gnn.tile(kind, job, turn)[:, 0:T].rearrange("p (s g n) -> p s g n", s=1, g=2)
                    dve.tensor_tensor(gated[:, :, :, :], tile.to_broadcast([P, 2, 2, P]),
                                      tri_strict[:, :, :].unsqueeze(2).to_broadcast([P, 2, 2, P]), ALU.mult)\
                       .then_inc(gnn.evac(kind, job, turn), 1)

                elif base == "hs" and part == "out":
                    dve.wait_ge(gnn.full, gnn.full_at(kind, job, turn))
                    dve.scalar_tensor_tensor(h_s, rows_of(gnn.tile(kind, job, turn), D), DESCALE,
                                             both_graphs(rows[f"L2_bs{l}"]), ALU.mult, ALU.add)\
                       .then_inc(gnn.evac(kind, job, turn), 1)

                elif kind == "L2" and part == "ctx":
                    dve.wait_ge(gnn.full, gnn.full_at(kind, job, turn))
                    dve.wait_ge(gnn.evac(kind, "hs" + l, turn), gnn.evac_at(kind, "hs" + l, turn))
                    if g_norm.again(kind, job, turn):
                        dve.wait_ge(g_norm.sem, g_norm.at(kind, job, turn, back=1))
                    tile = gnn.tile(kind, job, turn)
                    for g in range(2):
                        z = dve.scalar_tensor_tensor(g_z[:, g, :], h_s[:, g, :], g_small[:, 48 + g:49 + g],
                                                     tile[:, g * 512:g * 512 + D], ALU.mult, ALU.add)
                    z.then_inc(gnn.evac(kind, job, turn), 1)
                    dve.wait_ge(gnn.evac(kind, job, turn), gnn.evac_at(kind, job, turn))
                    stats(g_z, g_small, turn)
                    dve.tensor_tensor(g_small[:, 22:24], variances(g_small), g_small[:, 52:54], ALU.add)\
                       .then_inc(g_var.sem, 1)

                elif job == "V" and part == "out":
                    dve.wait_ge(att.full, att.full_at(kind, job, turn))
                    dve.scalar_tensor_tensor(row_a[:, :, :], rows_of(att.tile(kind, job, turn), D), DESCALE,
                                             both_graphs(rows[f"{kind}_bv"]), ALU.mult, ALU.add)\
                       .then_inc(att.evac(kind, job, turn), 1)

                elif part == "max":
                    b = int(l)
                    dve.wait_ge(att.full, att.full_at(kind, job, turn))
                    if b == 0 and kind == "L1":
                        dve.wait_ge(adj01_loaded.sem, adj01_loaded.at("L0", "x", turn))
                    if b == 0 and kind == "L3":
                        dve.wait_ge(adj3_loaded.sem, adj3_loaded.at("L3", "x", turn))
                    if b >= 2:
                        dve.wait_ge(att.full, att.full_at(kind, f"X{b - 2}", turn))
                    edges = adj_of[kind][:, b // 2:b // 2 + 1, :].to_broadcast([P, HB, P])
                    dve.scalar_tensor_tensor(sc[:, b % 2], edges, 2.0 if kind == "L1" else 1.0,
                                             heads_of(att.tile(kind, job, turn)), ALU.mult, ALU.add)\
                       .then_inc(att.evac(kind, job, turn), 1)
                    dve.wait_ge(att.evac(kind, job, turn), att.evac_at(kind, job, turn))
                    dve.tensor_reduce(row_max[:, b, :], sc[:, b % 2], AX_X, ALU.max).then_inc(a_max.sem, 1)

                elif base == "X" and part == "lo":
                    dve.wait_ge(a_hi.sem, a_hi.at(kind, job, turn))
                    h0 = HB * (int(l) % 2)
                    dve.tensor_tensor(pt_lo[:, h0:h0 + HB, :], heads_of(att.tile(kind, job, turn)),
                                      pt_hi[:, h0:h0 + HB, :], ALU.subtract)\
                       .then_inc(att.evac(kind, job, turn), 1)

                elif base == "P" and part == "out":
                    g = int(l)
                    dve.wait_ge(att.full, att.full_at(kind, job, turn))
                    if g == 0:
                        dve.wait_ge(a_vlo.sem, a_vlo.at(kind, "x", turn))
                        dve.wait_ge(a_hi.sem, a_hi.at(kind, "V", turn))
                    dve.wait_ge(a_max.sem, a_max.at(kind, str(2 * g + 1), turn))
                    tile = att.tile(kind, job, turn)[:, 0:HEADS * (HD + 1)].rearrange("p (h d) -> p h d", d=HD + 1)
                    sums = tile[:, :, HD]
                    is_zero, keep, recip = a_small[:, 32:44], a_small[:, 44:56], a_small[:, 56:68]
                    dve.reciprocal(recip, sums)
                    dve.tensor_scalar(is_zero, row_max[:, 2 * g:2 * g + 2, :].rearrange("p b h -> p (b h)"),
                                      0.0, None, ALU.is_equal).then_inc(vector_link, 1)
                    dve.wait_ge(vector_link, linked(turn))
                    dve.scalar_tensor_tensor(keep, sums, float(P), is_zero, ALU.is_ge, ALU.mult)\
                       .then_inc(vector_link, 1)
                    dve.wait_ge(vector_link, linked(turn))
                    dve.tensor_scalar(keep, keep, -1.0, 1.0, ALU.mult, ALU.add).then_inc(vector_link, 1)
                    dve.wait_ge(vector_link, linked(turn))
                    dve.tensor_tensor(recip, recip, keep, ALU.mult).then_inc(vector_link, 1)
                    dve.wait_ge(vector_link, linked(turn))
                    dve.tensor_tensor(row_a[:, g, :].rearrange("p (h d) -> p h d", d=HD), tile[:, :, 0:HD],
                                      recip.unsqueeze(2).to_broadcast([P, HEADS, HD]), ALU.mult)\
                       .then_inc(att.evac(kind, job, turn), 1)

                elif job == "Y" and part == "res":
                    dve.wait_ge(att.full, att.full_at(kind, job, turn))
                    dve.wait_ge(a_xb.sem, a_xb.at(kind, "x", turn))
                    if a_norm.again(kind, "x", turn):
                        dve.wait_ge(a_norm.sem, a_norm.at(kind, "x", turn, back=1))
                    dve.scalar_tensor_tensor(a_z[:, :, :], rows_of(att.tile(kind, job, turn), D), DESCALE,
                                             x_in[kind][:, :, :], ALU.mult, ALU.add)\
                       .then_inc(att.evac(kind, job, turn), 1)
                    dve.wait_ge(att.evac(kind, job, turn), att.evac_at(kind, job, turn))
                    stats(a_z, a_small, turn)
                    dve.tensor_scalar(a_small[:, 22:24], variances(a_small), 1e-5, None, ALU.add)\
                       .then_inc(a_var.sem, 1)

            for n in range(LOOP_START):
                for step in steps_of(Turn(n)):
                    do(*step)
            before_loop = links["n"]
            with dve.Fori(LOOP_START, PAIRS) as reg:
                for step in steps_of(Turn(0, reg)):
                    do(*step)
            assert links["n"] - before_loop == VECTOR_LINKS, links["n"] - before_loop
            links["n"] = before_loop + (PAIRS - LOOP_START) * VECTOR_LINKS
            for n in range(PAIRS, PAIRS + 3):
                for step in steps_of(Turn(n)):
                    do(*step)

        @block.gpsimd
        def _(pool):
            pool.memset(ident[:, :], 0.0).then_inc(consts_filled, 1)
            pool.memset(tri_scaled[:, :, :], 1.0 / TEMPER).then_inc(consts_filled, 1)
            pool.memset(tri_strict[:, :, :], 1.0).then_inc(consts_filled, 1)
            pool.memset(half[:, :], 0.5).then_inc(consts_filled, 1)
            pool.memset(neg_half[:, :], -0.5).then_inc(consts_filled, 1)
            pool.wait_ge(consts_filled, 5)
            pool.affine_select(out=ident[:, :], in_=ident[:, :], compare_op=ALU.not_equal, fill=1.0, base=0,
                               pattern=[[-1, P]], channel_multiplier=1).then_inc(consts_ready, 1)
            pool.affine_select(out=tri_scaled[:, 0, :], in_=tri_scaled[:, 0, :], compare_op=ALU.is_ge, fill=0.0,
                               base=0, pattern=[[-1, P]], channel_multiplier=1)
            pool.affine_select(out=tri_scaled[:, 1, :], in_=tri_scaled[:, 1, :], compare_op=ALU.is_ge, fill=0.0,
                               base=-1, pattern=[[1, P]], channel_multiplier=-1).then_inc(consts_ready, 1)
            pool.affine_select(out=tri_strict[:, 0, :], in_=tri_strict[:, 0, :], compare_op=ALU.is_ge, fill=0.0,
                               base=-1, pattern=[[-1, P]], channel_multiplier=1)
            pool.affine_select(out=tri_strict[:, 1, :], in_=tri_strict[:, 1, :], compare_op=ALU.is_ge, fill=0.0,
                               base=-1, pattern=[[1, P]], channel_multiplier=-1).then_inc(consts_ready, 1)
            pool.wait_ge(consts_ready, 3)
            pool.wait_ge(params_loaded, 16 * (len(rows) + len(cols)))

            def do(kind, job, part, turn):
                s = slots[kind]
                base, l = job.rstrip("0123"), job[-1]

                if (kind, job) == ("L0", "masks"):
                    pool.wait_ge(adj01_loaded.sem, adj01_loaded.at("L0", "x", turn))
                    if turn.from_on(1):
                        pool.wait_ge(gnn.evac("L0", "U1", turn.before()), gnn.evac_at("L0", "U1", turn.before()))
                    for side, edges in enumerate((adjt0, adj01)):
                        m = pool.tensor_tensor(masks[:, side], edges[:, :, :],
                                               tri_scaled[:, side:side + 1, :].to_broadcast([P, 2, P]), ALU.mult)
                    m.then_inc(g_masks.sem, 1)

                elif part == "add":
                    pool.wait_ge(gnn.evac(kind, job, turn), gnn.evac_at(kind, job, turn))
                    pool.tensor_tensor(logits[:, :, :], gated[:, 0], gated[:, 1], ALU.add).then_inc(g_logits.sem, 1)

                elif part == "adj":
                    pool.wait_ge(g_expu.sem, g_expu.at("L0", l, turn))
                    pool.tensor_tensor(exp_adj[:, :, :], expu[:, :, :], adjt0[:, :, :], ALU.mult)\
                        .then_inc(g_exp_adj.sem, 1)

                elif part == "root":
                    var, rt, small = (g_var, g_root, g_small) if s is gnn else (a_var, a_root, a_small)
                    event = job if s is gnn else "x"
                    power, at = (half, 24) if kind == "L0" and base == "C" else (neg_half, 28)
                    pool.wait_ge(var.sem, var.at(kind, event, turn))
                    pool.tensor_tensor(small[:, at:at + 2], small[:, 22:24], power[:, :], ALU.pow).then_inc(rt.sem, 1)

                elif part == "affine":
                    pool.wait_ge(g_norm.sem, g_norm.at(kind, "C1", turn))
                    pool.tensor_tensor(g_z[:, :, :], g_z[:, :, :], both_graphs(rows[f"{kind}_a"]), ALU.mult)\
                        .then_inc(g_affine.sem, 1)
                    pool.wait_ge(g_affine.sem, g_affine.at(kind, "mul", turn))
                    pool.tensor_tensor(g_z[:, :, :], g_z[:, :, :], both_graphs(rows[f"{kind}_c"]), ALU.add)\
                        .then_inc(g_affine.sem, 1)

                elif part == "bias":
                    pool.wait_ge(gnn.evac(kind, job, turn), gnn.evac_at(kind, job, turn))
                    h = h_l if base == "hl" else h_r
                    pool.tensor_tensor(h[:, :, 0:D], h[:, :, 0:D], both_graphs(rows[f"L2_b{base[1]}{l}"]), ALU.add)\
                        .then_inc(g_biased.sem, 1)

                elif job == "V" and part == "lo":
                    pool.wait_ge(a_hi.sem, a_hi.at(kind, "V", turn))
                    pool.tensor_tensor(v_lo[:, :, :, :], row_a[:, :, :].rearrange("p g (h d) -> p g h d", d=HD),
                                       v_hi[:, :, :, 0:HD], ALU.subtract).then_inc(a_vlo.sem, 1)

                elif part == "center":
                    b = int(l)
                    pool.wait_ge(a_max.sem, a_max.at(kind, l, turn))
                    pool.tensor_tensor(sc[:, b % 2], sc[:, b % 2],
                                       row_max[:, b, :].unsqueeze(2).to_broadcast([P, HB, P]), ALU.subtract)\
                        .then_inc(a_centered.sem, 1)

                elif job == "xb":
                    pool.wait_ge(att.full, att.full_at(kind, "I", turn))
                    pool.tensor_tensor(x_in[kind][:, :, :], x_in[kind][:, :, :], both_graphs(rows[f"{kind}_bo"]),
                                       ALU.add).then_inc(a_xb.sem, 1)

            for n in range(LOOP_START):
                for step in steps_of(Turn(n)):
                    do(*step)
            with pool.Fori(LOOP_START, PAIRS) as reg:
                for step in steps_of(Turn(0, reg)):
                    do(*step)
            for n in range(PAIRS, PAIRS + 3):
                for step in steps_of(Turn(n)):
                    do(*step)


def kernel(**inputs):
    import numpy as _np
    import concourse.bacc as _bacc
    from concourse import mybir as _mybir
    from concourse.bass_utils import run_bass_kernel_spmd as _run

    a = {k: _np.asarray(v) for k, v in inputs.items()}
    weights = {
        "L0_left0": a["L0_gnn_W_left"][0], "L0_right0": a["L0_gnn_W_right"][0], "L0_lin0": a["L0_gnn_W_lin"][0],
        "L0_left1": a["L0_gnn_W_left"][1], "L0_right1": a["L0_gnn_W_right"][1], "L0_lin1": a["L0_gnn_W_lin"][1],
        "L1_q": a["L1_gnn_Wq"], "L1_k": a["L1_gnn_Wk"], "L1_v": a["L1_gnn_Wv"], "L1_o": a["L1_gnn_Wo"],
        "L2_l0": a["L2_gnn_Wl"][0], "L2_s0": a["L2_gnn_Ws"][0], "L2_r0": a["L2_gnn_Wr"][0],
        "L2_l1": a["L2_gnn_Wl"][1], "L2_s1": a["L2_gnn_Ws"][1], "L2_r1": a["L2_gnn_Wr"][1],
        "L3_q": a["L3_gnn_Wq"], "L3_k": a["L3_gnn_Wk"], "L3_v": a["L3_gnn_Wv"], "L3_o": a["L3_gnn_Wo"],
    }
    vectors = {
        "L0_b0": a["L0_gnn_b_lin"][0], "L0_b1": a["L0_gnn_b_lin"][1],
        "L0_a": a["L0_gnn_ln_a"][1], "L0_c": a["L0_gnn_ln_b"][1],
        "col_L0_a": a["L0_gnn_ln_a"][0].reshape(C, P).T, "col_L0_c": a["L0_gnn_ln_b"][0].reshape(C, P).T,
        "L1_bv": a["L1_gnn_bv"], "L1_bo": a["L1_gnn_bo"],
        "L2_bl0": a["L2_gnn_bl"][0], "L2_bs0": a["L2_gnn_bs"][0], "L2_br0": a["L2_gnn_br"][0],
        "L2_bl1": a["L2_gnn_bl"][1], "L2_bs1": a["L2_gnn_bs"][1], "L2_br1": a["L2_gnn_br"][1],
        "L2_a": a["L2_gnn_ln_w"][1], "L2_c": a["L2_gnn_ln_b"][1],
        "col_L2_a": a["L2_gnn_ln_w"][0].reshape(C, P).T, "col_L2_c": a["L2_gnn_ln_b"][0].reshape(C, P).T,
        "L3_bv": a["L3_gnn_bv"], "L3_bo": a["L3_gnn_bo"],
    }
    arrays = {
        "x": _np.ascontiguousarray(a["x"]),
        "adj": _np.ascontiguousarray(a["adj"]),
        "adj_t": _np.ascontiguousarray(a["adj"].transpose(0, 2, 1)),
        "weights_t": _np.ascontiguousarray(_np.stack([weights[n].T for n in WEIGHTS])),
        **{f"vec_{n}": _np.ascontiguousarray(v) for n, v in vectors.items()},
    }
    nc = _bacc.Bacc("TRN2", target_bir_lowering=False, num_devices=1)
    dram = {n: nc.dram_tensor(n, v.shape, _mybir.dt.from_np(v.dtype), kind="ExternalInput").ap()
            for n, v in arrays.items()}
    out = nc.dram_tensor("out", (NG, P, D), _mybir.dt.float32, kind="ExternalOutput").ap()
    graph_stack_kernel(nc, dram["x"], dram["adj"], dram["adj_t"], dram["weights_t"],
                       {n: dram[f"vec_{n}"] for n in vectors}, out)
    r = _run(nc, [arrays], core_ids=[0])
    return r.results[0]["out"]
```

```python
from contextlib import ExitStack

import concourse.bass as bass
from concourse import mybir

P = 128
NG = 64
D = 384
C = D // P
PAIRS = NG // 2
T = 2 * P
HEADS = 12
HD = D // HEADS
HB = HEADS // 2
WSCALE = 64.0
DESCALE = 1.0 / WSCALE
TEMPER = float(D) ** 0.5

F32 = mybir.dt.float32
F16 = mybir.dt.float16
ALU = mybir.AluOpType
ACT = mybir.ActivationFunctionType
AX_X = mybir.AxisListType.X

WEIGHTS = (["L0_left0", "L0_right0", "L0_lin0", "L0_left1", "L0_right1", "L0_lin1"]
           + ["L1_q", "L1_k", "L1_v", "L1_o"]
           + ["L2_l0", "L2_s0", "L2_r0", "L2_l1", "L2_s1", "L2_r1"]
           + ["L3_q", "L3_k", "L3_v", "L3_o"])

JOBS = {
    "L0": ("I", "mL0", "mR0", "U0", "H0", "C0", "T0", "mL1", "mR1", "U1", "H1", "C1"),
    "L2": ("I", "S0", "X0", "hl0", "hr0", "hs0", "C0", "T0", "S1", "X1", "hl1", "hr1", "hs1", "C1"),
    "L1": ("I", "Q", "K", "V", "S0", "S1", "X0", "S2", "X1", "P0", "S3", "X2", "X3", "P1", "T", "Y"),
}
JOBS["L3"] = JOBS["L1"]

LAG = {"L0": 0, "L1": 0, "L2": 1, "L3": 2}
VECTOR_LINKS = 38

WALK = """
    -L2:hl1.out -L2:hr1 -L2:S1.delta -L2:X1 -L1:Q.stack_lo -L1:K.stack_hi -L1:K.stack_lo L0:edges -L2:hr1.out
    -L1:S0 -L1:S1 -L2:X1.mask -L1:store -L1:V.hi -L1:S0.max -L1:S0.exp -L1:S1.max L2:load L0:load -L2:hr1.bias
    -L2:hs1 -L2:hs1.out L0:I L0:I.hi -L1:xb -L1:X0 -L1:V.lo -L1:X0.hi L0:I.lo L0:masks -L1:X0.lo -L1:S2
    -L1:S2.max -L1:S1.exp -L2:C1 L0:mL0 -L1:X1 -L2:C1.ctx L0:mL0.hi L0:mR0 -L1:X1.hi L0:mL0.lo -L1:X1.lo
    -L2:C1.root -L2:C1.apply -L1:S2.exp -L1:P0 L0:mR0.hi -L1:P0.out -L1:S3 L0:mR0.lo -L3:Y.root -L1:S3.max
    -L1:X2 -L1:X2.hi -L1:S3.exp -L2:F.res L0:U0 -L1:X3 -L1:X3.hi -L3:Y.shift L0:U0.mask -L1:X2.lo -L2:F.root
    L0:U0.add -L2:F.shift L0:H0 -L2:F.norm L0:U0.exp L0:U0.adj L0:H0.out -L1:X3.lo -L1:P1 L3:I L3:I.hi
    -L1:P1.out L0:C0 L3:I.lo L0:C0.ctx -L1:T -L3:Y.norm -L1:T.hi L0:C0.root -L1:T.lo L3:Q L0:C0.shift L3:Q.hi
    L3:Q.lo L3:load -L1:Y L3:Q.stack_hi -L1:Y.res -L1:Y.root L0:C0.norm L0:T0 L0:T0.relu L3:K L0:T0.lo L3:xb
    L0:mL1 L0:mR1 L3:V L3:Q.stack_lo L3:K.hi L3:K.lo L3:K.stack_hi L0:mL1.hi L0:mL1.lo L0:mR1.hi L0:mR1.lo L0:U1
    L3:K.stack_lo -L1:Y.shift L3:V.out L3:V.hi -L1:Y.norm L3:V.lo L0:U1.mask L0:U1.add L0:U1.exp L3:S0 L3:S0.max
    L3:S1 L0:H1 L2:I L3:S1.max L0:H1.out L2:I.hi L0:U1.adj L0:C1 L3:S0.exp L2:I.lo L0:C1.ctx L3:X0 L3:X0.hi
    L2:S0 L3:X0.lo L3:S1.exp L3:S2 L3:S2.max L3:X1 L0:C1.root L3:X1.hi L2:S0.max L3:X1.lo L0:C1.apply L2:hl0
    L3:P0 L3:S2.exp L3:P0.out L2:S0.exp L3:S3 L3:X2 L3:X2.hi L3:S3.max L2:hl0.out L1:load L3:S3.exp L2:S0.delta
    L2:hr0 L2:hr0.out L3:X3 L0:F.res L3:X3.hi L2:X0 L0:F.root L3:X2.lo L0:F.shift L3:X3.lo L2:hr0.bias L2:hs0
    L2:X0.mask L0:F.norm L3:P1 L1:I L3:P1.out L1:I.hi L2:C0 L3:T -L3:store L1:I.lo L2:hs0.out L2:C0.ctx
    L2:C0.root L1:Q L3:T.hi L1:Q.hi L3:T.lo L3:Y L2:C0.shift L2:C0.norm L1:Q.lo L2:T0 L2:T0.relu L3:Y.res L1:K
    L1:V L1:Q.stack_hi L1:K.hi L2:T0.lo L2:S1 L2:S1.max L1:K.lo L1:V.out L2:hl1 L2:S1.exp
"""


def steps_in(walk):
    for name in walk.split():
        kind, step = name.lstrip("-").split(":")
        yield kind, name.count("-"), step


ORDER = list(steps_in(WALK))
MOST_BACK = max(back for _, back, _ in ORDER)
LOOP_START = 3 + MOST_BACK
TURNS = PAIRS + 2 + MOST_BACK


class Turn:

    def __init__(self, k, reg=None):
        self.k, self.reg = k, reg

    def before(self):
        return Turn(self.k - 1, self.reg)

    def from_on(self, k):
        return self.reg is not None or self.k >= k

    def index(self, lag):
        return self.k - lag if self.reg is None else self.reg + (self.k - lag)


class Counter:

    def __init__(self, events):
        self.places = []
        for kind, listed in events.items():
            for n, (event, step, amount) in enumerate(listed):
                at = [i for i, (k, _, s) in enumerate(ORDER) if (k, s) == (kind, step)][0]
                self.places.append((kind, event, (at, n), ORDER[at][1] + LAG[kind], amount))

    def per_turn(self):
        return sum(amount for *_, amount in self.places)

    def until(self, kind, event, turn):
        place, late = [(p, lt) for k, e, p, lt, _ in self.places if (k, e) == (kind, event)][0]
        walked = turn.k + late - LAG[kind]
        total = 0
        for _, _, other, other_late, amount in self.places:
            pairs = walked - other_late + (other <= place)
            total += amount * (pairs if turn.reg is not None else min(max(pairs, 0), PAIRS))
        return total


class Signal(Counter):

    def __init__(self, sem, events):
        super().__init__(events)
        self.sem = sem

    def at(self, kind, event, turn, back=0):
        v = self.until(kind, event, turn) - back * self.places[0][4]
        return v if turn.reg is None else turn.reg * self.per_turn() + v

    def again(self, kind, event, turn):
        return turn.reg is not None or self.at(kind, event, turn, back=1) > 0


class Slots(Counter):

    def __init__(self, full, evacuated, tensors, kinds):
        super().__init__({kind: [(job, job, 1) for job in JOBS[kind]] for kind in kinds})
        self.full, self.evacuated, self.tensors = full, evacuated, tensors
        assert self.per_turn() % 2 == 0

    def number(self, kind, job, turn):
        return self.until(kind, job, turn) - 1

    def tile(self, kind, job, turn):
        return self.tensors[self.number(kind, job, turn) % 2]

    def evac(self, kind, job, turn):
        return self.evacuated[self.number(kind, job, turn) % 2]

    def full_at(self, kind, job, turn):
        n = self.number(kind, job, turn) + 1
        return n if turn.reg is None else turn.reg * self.per_turn() + n

    def evac_at(self, kind, job, turn, back=0):
        v = self.number(kind, job, turn) // 2 + 1 - back
        return v if turn.reg is None else turn.reg * (self.per_turn() // 2) + v

    def free_at(self, kind, job, turn):
        return self.evac_at(kind, job, turn, back=1)

    def used(self, kind, job, turn):
        return turn.reg is not None or self.free_at(kind, job, turn) > 0


def graph_stack_kernel(nc, x, adj, adj_t, weights_t, vectors, out):
    ctx = ExitStack()
    with ctx:
        def sb(name, shape, dt=F32):
            return ctx.enter_context(nc.sbuf_tensor(name, shape, dt))

        def sem(name):
            return ctx.enter_context(nc.semaphore(name))

        w_hi = sb("w_hi", [P, len(WEIGHTS), C, D], F16)
        w_lo = sb("w_lo", [P, len(WEIGHTS), C, D], F16)
        rows = {n: sb(f"row_{n}", [P, D]) for n in (
            "L0_b0", "L0_b1", "L0_a", "L0_c", "L1_bv", "L1_bo", "L2_bl0", "L2_bs0", "L2_br0",
            "L2_bl1", "L2_bs1", "L2_br1", "L2_a", "L2_c", "L3_bv", "L3_bo")}
        cols = {n: sb(f"col_{n}", [P, C]) for n in ("L0_a", "L0_c", "L2_a", "L2_c")}
        ident = sb("ident", [P, P])
        tri_scaled = sb("tri_scaled", [P, 2, P])
        tri_strict = sb("tri_strict", [P, 2, P])
        half = sb("half", [P, 2])
        neg_half = sb("neg_half", [P, 2])

        x0 = sb("x0", [P, 2, D])
        x1 = sb("x1", [P, 2, D])
        x2 = sb("x2", [P, 2, D])
        x3 = sb("x3", [P, 2, D])
        x4 = sb("x4", [P, 2, D])
        x_in = {"L0": x0, "L1": x1, "L2": x2, "L3": x3}
        x_out = {"L0": x1, "L1": x2, "L2": x3, "L3": x4}
        adj0 = sb("adj0", [P, 2, P])
        adj1 = sb("adj1", [P, 2, P])
        adjt0 = sb("adjt0", [P, 2, P])
        adj2 = sb("adj2", [P, 2, P])
        adj3 = sb("adj3", [P, 2, P])
        adj_of = {"L1": adj1, "L3": adj3}

        g_ht_hi = sb("g_ht_hi", [P, C, T], F16)
        g_ht_lo = sb("g_ht_lo", [P, C, T], F16)
        m_all = sb("m_all", [P, 4 * C * T], F16)
        m_hi = [m_all[:, s * 2 * C * T:s * 2 * C * T + C * T].rearrange("p (c t) -> p c t", c=C) for s in range(2)]
        m_lo = [m_all[:, s * 2 * C * T + C * T:(s + 1) * 2 * C * T].rearrange("p (c t) -> p c t", c=C)
                for s in range(2)]
        h_r = m_all[:, 0:2 * C * T].bitcast(F32).rearrange("p (g d) -> p g d", g=2)
        h_s = m_all[:, 2 * C * T:4 * C * T].bitcast(F32).rearrange("p (g d) -> p g d", g=2)
        h_l = sb("h_l", [P, 2, D + 1])
        masks = sb("masks", [P, 2, 2, P])
        gated = sb("gated", [P, 2, 2, P])
        logits = sb("logits", [P, 2, P])
        expu = sb("expu", [P, 2, P])
        exp_adj = sb("exp_adj", [P, 2, P])
        t32 = sb("t32", [P, C, T])
        g_z = sb("g_z", [P, 2, D])
        g_small = sb("g_small", [P, 64])

        a_ht_hi = sb("a_ht_hi", [P, C, T], F16)
        a_ht_lo = sb("a_ht_lo", [P, C, T], F16)
        qk_hi = [sb(f"qk_hi{n}", [P, C, T], F16) for n in range(2)]
        qk_lo = [sb(f"qk_lo{n}", [P, C, T], F16) for n in range(2)]
        stack = [sb("stack_q", [P, HEADS, T], F16), sb("stack_k", [P, HEADS, T], F16)]
        row_a = sb("row_a", [P, 2, D])
        v_hi = sb("v_hi", [P, 2, HEADS, HD + 1], F16)
        v_lo = sb("v_lo", [P, 2, HEADS, HD], F16)
        sc = sb("sc", [P, 2, HB, P])
        pt_hi = sb("pt_hi", [P, HEADS, P], F16)
        pt_lo = sb("pt_lo", [P, HEADS, P], F16)
        t_hi, t_lo = (p[:, 0:C * T // P, :].rearrange("p (c g) n -> p c (g n)", c=C) for p in (pt_hi, pt_lo))
        neg_max = sb("neg_max", [P, 4, HB])
        a_z = sb("a_z", [P, 2, D])
        a_small = sb("a_small", [P, 96])

        def rows_of(tile, width):
            return tile[:, :].rearrange("p (g n) -> p g n", g=2)[:, :, 0:width]

        def both_graphs(row):
            return row[:, :].unsqueeze(1).to_broadcast([P, 2, D])

        def features_of(tile):
            return tile[:, 0:C * T].rearrange("p (c t) -> p c t", c=C)

        def heads_of(tile):
            return tile[:, 0:HB * P].rearrange("p (h n) -> p h n", n=P)

        staging = [sc[:, :, :, :].rearrange("p b h n -> p (b h n)")]
        staging += [s[:, :, :].rearrange("p h t -> p (h t)").bitcast(F32) for s in stack]
        staging = [s[:, 0:C * D].rearrange("p (c o) -> p c o", c=C) for s in staging]

        psum = [ctx.enter_context(nc.psum_tensor(f"ps{n}", [P, 1024], F32)) for n in range(4)]

        load_w = [sem(f"load_w{n}") for n in range(3)]
        weight_split = sem("weight_split")
        weight_hi = sem("weight_hi")
        params_loaded = sem("params_loaded")
        consts_filled = sem("consts_filled")
        consts_ready = sem("consts_ready")
        ones_ready = sem("ones_ready")
        vector_link = sem("vector_link")

        gnn = Slots(sem("gnn_full"), [sem("gnn_evac0"), sem("gnn_evac1")], psum[0:2], ("L0", "L2"))
        att = Slots(sem("att_full"), [sem("att_evac0"), sem("att_evac1")], psum[2:4], ("L1", "L3"))
        slots = {"L0": gnn, "L2": gnn, "L1": att, "L3": att}

        def signal(name, events, amount=1):
            listed = {kind: {"x": e} if isinstance(e, str) else e for kind, e in events.items()}
            return Signal(sem(name), {kind: [(event, step, amount) for event, step in e.items()]
                                      for kind, e in listed.items()})

        def parts(part, *jobs):
            return {job: f"{job}.{part}" for job in jobs}

        def both(events, kinds=("L1", "L3")):
            return {kind: events for kind in kinds}

        x0_loaded = signal("x0_loaded", {"L0": "load"}, 16)
        adj0_loaded = signal("adj0_loaded", {"L0": "edges"}, 32)
        adj1_loaded = signal("adj1_loaded", {"L1": "load"}, 16)
        adj2_loaded = signal("adj2_loaded", {"L2": "load"}, 16)
        adj3_loaded = signal("adj3_loaded", {"L3": "load"}, 16)
        x4_stored = signal("x4_stored", {"L3": "store"}, 16)
        g_kinds = ("L0", "L2")
        g_hi = signal("g_hi", {"L0": parts("hi", "I", "mL0", "mR0", "mL1", "mR1") | {"T0": "T0.relu"},
                               "L2": {"I": "I.hi", "T0": "T0.relu"}})
        g_masks = signal("g_masks", {"L0": "masks"})
        g_logits = signal("g_logits", {"L0": {"0": "U0.add", "1": "U1.add"}})
        g_expu = signal("g_expu", {"L0": {"0": "U0.exp", "1": "U1.exp"}})
        g_exp_adj = signal("g_exp_adj", {"L0": {"0": "U0.adj", "1": "U1.adj"}, "L2": {"0": "S0.delta", "1": "S1.delta"}})
        g_negmax = signal("g_negmax", {"L2": {"0": "S0.max", "1": "S1.max"}})
        g_biased = signal("g_biased", {"L2": parts("bias", "hr0", "hr1")})
        g_var = signal("g_var", both({"C0": "C0.ctx", "C1": "C1.ctx", "F": "F.res"}, g_kinds))
        g_root = signal("g_root", both(parts("root", "C0", "C1", "F"), g_kinds))
        g_shift = signal("g_shift", both(parts("shift", "C0", "F"), g_kinds))
        g_norm = signal("g_norm", both(parts("norm", "C0", "F"), g_kinds))
        g_affine = signal("g_affine", both("C1.apply", g_kinds))
        g_lo = signal("g_lo", both("T0.lo", g_kinds))
        g_resid = signal("g_resid", both("F.res", g_kinds))
        a_hi = signal("a_hi", both(parts("hi", "I", "Q", "K", "V", "X0", "X1", "X2", "X3", "T")))
        a_stacked = Signal(sem("a_stacked"), both([(step, step, 16 * (8 if "hi" in step else 4)) for step in (
            "Q.stack_hi", "Q.stack_lo", "K.stack_hi", "K.stack_lo")]))
        a_vlo = signal("a_vlo", both("V.lo"))
        a_max = signal("a_max", both({b: f"S{b}.max" for b in "0123"}))
        a_exp = signal("a_exp", both({b: f"S{b}.exp" for b in "0123"}))
        a_xb = signal("a_xb", both("xb"))
        a_var = signal("a_var", both("Y.res"))
        a_root = signal("a_root", both("Y.root"))
        a_shift = signal("a_shift", both("Y.shift"))
        a_norm = signal("a_norm", both("Y.norm"))

        def steps_of(turn):
            for kind, back, step in ORDER:
                if turn.reg is not None or 0 <= turn.k - back - LAG[kind] < PAIRS:
                    job, _, part = step.partition(".")
                    yield kind, job, part, Turn(turn.k - back, turn.reg)

        links = {"n": 0}
        block = ctx.enter_context(nc.Block())

        @block.sync
        def _(sp):
            for n in range(len(WEIGHTS)):
                if n >= 3:
                    sp.wait_ge(weight_split, n - 2)
                sp.dma_start(staging[n % 3], weights_t[n].rearrange("(c p) o -> p c o", p=P)).then_inc(load_w[n % 3], 16)
                if n == 2:
                    for name, tile in rows.items():
                        sp.dma_start(tile[:, :], vectors[name].unsqueeze(0).to_broadcast([P, D]))\
                          .then_inc(params_loaded, 16)
                    for name, tile in cols.items():
                        sp.dma_start(tile[:, :], vectors["col_" + name]).then_inc(params_loaded, 16)

            x_pairs = x.rearrange("(q g) n d -> q n g d", g=2)
            out_pairs = out.rearrange("(q g) n d -> q n g d", g=2)
            adj_pairs = adj.rearrange("(q g) i j -> q i g j", g=2)
            adjt_pairs = adj_t.rearrange("(q g) i j -> q i g j", g=2)

            def do(kind, job, part, turn):
                pair = turn.index(LAG[kind])
                if (kind, job) == ("L0", "load"):
                    if turn.from_on(1):
                        sp.wait_ge(g_resid.sem, g_resid.at("L0", "x", turn.before()))
                    sp.dma_start(x0[:, :, :], x_pairs[pair]).then_inc(x0_loaded.sem, 16)
                elif (kind, job) == ("L0", "edges"):
                    if turn.from_on(1):
                        sp.wait_ge(g_exp_adj.sem, g_exp_adj.at("L0", "1", turn.before()))
                        sp.wait_ge(g_masks.sem, g_masks.at("L0", "x", turn.before()))
                    sp.dma_start(adj0[:, :, :], adj_pairs[pair]).then_inc(adj0_loaded.sem, 16)
                    sp.dma_start(adjt0[:, :, :], adjt_pairs[pair]).then_inc(adj0_loaded.sem, 16)
                elif (kind, job) == ("L1", "load"):
                    if turn.from_on(1):
                        sp.wait_ge(att.evac("L1", "S3", turn.before()), att.evac_at("L1", "S3", turn.before()))
                    sp.dma_start(adj1[:, :, :], adj_pairs[pair]).then_inc(adj1_loaded.sem, 16)
                elif (kind, job) == ("L2", "load"):
                    if turn.from_on(2):
                        sp.wait_ge(g_exp_adj.sem, g_exp_adj.at("L2", "1", turn.before()))
                    sp.dma_start(adj2[:, :, :], adj_pairs[pair]).then_inc(adj2_loaded.sem, 16)
                elif (kind, job) == ("L3", "load"):
                    if turn.from_on(3):
                        sp.wait_ge(att.evac("L3", "S3", turn.before()), att.evac_at("L3", "S3", turn.before()))
                    sp.dma_start(adj3[:, :, :], adj_pairs[pair]).then_inc(adj3_loaded.sem, 16)
                elif part in ("stack_hi", "stack_lo"):
                    n = "QK".index(job)
                    if part == "stack_hi":
                        sp.wait_ge(a_hi.sem, a_hi.at(kind, job, turn))
                        src, thirds = qk_hi[n], ((0, 1), (0, 2))[n]
                    else:
                        sp.wait_ge(att.evac(kind, job, turn), att.evac_at(kind, job, turn))
                        src, thirds = qk_lo[n], ((2,), (1,))[n]
                    for third in thirds:
                        for r in range(4):
                            sp.dma_start(stack[n][32 * third:32 * third + 32, r:HEADS:4, :],
                                         src[32 * r:32 * r + 32, :, :]).then_inc(a_stacked.sem, 16)
                elif (kind, job) == ("L3", "store"):
                    sp.wait_ge(a_norm.sem, a_norm.at("L3", "x", turn))
                    sp.dma_start(out_pairs[pair], x4[:, :, :]).then_inc(x4_stored.sem, 16)

            for n in range(LOOP_START):
                for step in steps_of(Turn(n)):
                    do(*step)
            with sp.Fori(LOOP_START, PAIRS) as reg:
                for step in steps_of(Turn(0, reg)):
                    do(*step)
            for n in range(PAIRS, TURNS):
                for step in steps_of(Turn(n)):
                    do(*step)
            sp.wait_ge(x4_stored.sem, 16 * PAIRS)

        @block.tensor
        def _(pe):
            def split_products(tile, stationary, moving, last):
                (a_hi_, a_lo_), (b_hi_, b_lo_) = stationary, moving
                for k in range(C):
                    for n, (a, b) in enumerate(((a_hi_, b_hi_), (a_hi_, b_lo_), (a_lo_, b_hi_))):
                        mm = pe.matmul(tile, a(k), b(k), start=(k == 0 and n == 0), stop=(k == C - 1 and n == 2))
                if last is not None:
                    mm.then_inc(last, 1)

            def feature_projection(tile, weight, ht, full):
                w = WEIGHTS.index(weight)
                for o in range(C):
                    cols_ = slice(o * P, (o + 1) * P)
                    split_products(tile[:, o * T:(o + 1) * T],
                                   [lambda k, m=m: m[:, w, k, cols_] for m in (w_hi, w_lo)],
                                   [lambda k, h=h: h[:, k, :] for h in ht], full if o == C - 1 else None)

            def row_projection(tile, weight, ht, full):
                w = WEIGHTS.index(weight)
                for g in range(2):
                    nodes = slice(g * P, (g + 1) * P)
                    split_products(tile[:, g * 512:g * 512 + D],
                                   [lambda k, h=h: h[:, k, nodes] for h in ht],
                                   [lambda k, m=m: m[:, w, k, :] for m in (w_hi, w_lo)], full if g else None)

            def transpose_rows(tile, source, full):
                for c in range(C):
                    for g in range(2):
                        mm = pe.transpose(tile[:, c * T + g * P:c * T + (g + 1) * P],
                                          source[:, g, c * P:(c + 1) * P], ident[:, :])
                mm.then_inc(full, 1)

            pe.wait_ge(consts_ready, 3)
            pe.wait_ge(weight_split, len(WEIGHTS))
            pe.wait_ge(ones_ready, 2)
            g_ht, a_ht = (g_ht_hi, g_ht_lo), (a_ht_hi, a_ht_lo)

            def do(kind, job, part, turn):
                if part or job not in JOBS[kind]:
                    return
                s = slots[kind]
                tile, full = s.tile(kind, job, turn), s.full
                base, l = job.rstrip("0123"), job[-1]
                if s.used(kind, job, turn):
                    pe.wait_ge(s.evac(kind, job, turn), s.free_at(kind, job, turn))

                if job == "I":
                    if kind == "L0":
                        pe.wait_ge(x0_loaded.sem, x0_loaded.at("L0", "x", turn))
                    elif kind == "L1":
                        pe.wait_ge(g_norm.sem, g_norm.at("L0", "F", turn))
                    elif kind == "L2":
                        pe.wait_ge(a_norm.sem, a_norm.at("L1", "x", turn.before()))
                    else:
                        pe.wait_ge(g_norm.sem, g_norm.at("L2", "F", turn.before()))
                    transpose_rows(tile, x_in[kind], full)

                elif base in ("mL", "mR"):
                    if base == "mL":
                        if l == "0":
                            pe.wait_ge(gnn.evac(kind, "I", turn), gnn.evac_at(kind, "I", turn))
                        else:
                            pe.wait_ge(g_lo.sem, g_lo.at(kind, "x", turn))
                    feature_projection(tile, ("L0_left" if base == "mL" else "L0_right") + l, g_ht, full)

                elif base == "U":
                    pe.wait_ge(gnn.evac(kind, "mL" + l, turn), gnn.evac_at(kind, "mL" + l, turn))
                    pe.wait_ge(gnn.evac(kind, "mR" + l, turn), gnn.evac_at(kind, "mR" + l, turn))
                    for side in range(2):
                        for g in range(2):
                            at, n = (2 * side + g) * P, slice(g * P, (g + 1) * P)
                            split_products(tile[:, at:at + P],
                                           [lambda k, m=m: m[:, k, n] for m in (m_hi[side], m_lo[side])],
                                           [lambda k, h=h: h[:, k, n] for h in g_ht],
                                           full if side and g else None)

                elif base == "H":
                    row_projection(tile, "L0_lin" + l, g_ht, full)

                elif base == "C" and kind == "L0":
                    pe.wait_ge(gnn.evac(kind, "H" + l, turn), gnn.evac_at(kind, "H" + l, turn))
                    pe.wait_ge(g_exp_adj.sem, g_exp_adj.at(kind, l, turn))
                    for g in range(2):
                        mm = pe.matmul(tile[:, g * 512:g * 512 + D + 1], exp_adj[:, g, :], h_l[:, g, :],
                                       start=True, stop=True)
                    mm.then_inc(full, 1)

                elif base == "C":
                    pe.wait_ge(gnn.evac(kind, "X" + l, turn), gnn.evac_at(kind, "X" + l, turn))
                    if gnn.evac(kind, "hl" + l, turn) is not gnn.evac(kind, "X" + l, turn):
                        pe.wait_ge(gnn.evac(kind, "hl" + l, turn), gnn.evac_at(kind, "hl" + l, turn))
                    pe.wait_ge(g_biased.sem, g_biased.at(kind, "hr" + l, turn))
                    for g in range(2):
                        for side, h in enumerate((h_l, h_r)):
                            mm = pe.matmul(tile[:, g * 512:g * 512 + D], gated[:, side, g, :], h[:, g, 0:D],
                                           start=(side == 0), stop=(side == 1))
                    mm.then_inc(full, 1)

                elif kind == "L2" and base == "S":
                    if l == "0":
                        pe.wait_ge(gnn.evac(kind, "I", turn), gnn.evac_at(kind, "I", turn))
                    else:
                        pe.wait_ge(g_lo.sem, g_lo.at(kind, "x", turn))
                    for g in range(2):
                        n = slice(g * P, (g + 1) * P)
                        h_pair = [lambda k, h=h: h[:, k, n] for h in g_ht]
                        split_products(tile[:, n], h_pair, h_pair, full if g else None)

                elif kind == "L2" and base == "X":
                    pe.wait_ge(g_exp_adj.sem, g_exp_adj.at(kind, l, turn))
                    for g in range(2):
                        mm = pe.transpose(tile[:, g * P:(g + 1) * P], exp_adj[:, g, :], ident[:, :])
                    mm.then_inc(full, 1)

                elif base in ("hl", "hr", "hs"):
                    row_projection(tile, f"L2_{base[1]}{l}", g_ht, full)

                elif job == "T0":
                    pe.wait_ge(g_norm.sem, g_norm.at(kind, "C0", turn))
                    transpose_rows(tile, g_z, full)

                elif job in ("Q", "K"):
                    if job == "Q":
                        pe.wait_ge(att.evac(kind, "I", turn), att.evac_at(kind, "I", turn))
                    feature_projection(tile, f"{kind}_{job.lower()}", a_ht, full)

                elif job == "V":
                    row_projection(tile, f"{kind}_v", a_ht, full)

                elif base == "S":
                    b = int(l)
                    if b == 0:
                        pe.wait_ge(a_stacked.sem, a_stacked.at(kind, "K.stack_lo", turn))
                    n = slice(b // 2 * P, (b // 2 + 1) * P)
                    for h in range(HB):
                        head = HB * (b % 2) + h
                        mm = pe.matmul(tile[:, h * P:(h + 1) * P], stack[0][0:96, head, n], stack[1][0:96, head, n],
                                       start=True, stop=True)
                    mm.then_inc(full, 1)

                elif base == "X":
                    pe.wait_ge(a_exp.sem, a_exp.at(kind, l, turn))
                    for h in range(HB):
                        mm = pe.transpose(tile[:, h * P:(h + 1) * P], sc[:, int(l) % 2, h, :], ident[:, :])
                    mm.then_inc(full, 1)

                elif base == "P":
                    g = int(l)
                    if g == 1:
                        pe.wait_ge(att.evac(kind, "X2", turn), att.evac_at(kind, "X2", turn))
                    last_x = f"X{2 * g + 1}"
                    pe.wait_ge(att.evac(kind, last_x, turn), att.evac_at(kind, last_x, turn))
                    if g == 0:
                        pe.wait_ge(a_hi.sem, a_hi.at(kind, "V", turn))
                        pe.wait_ge(a_vlo.sem, a_vlo.at(kind, "x", turn))
                    for h in range(HEADS):
                        at = h * (HD + 1)
                        pe.matmul(tile[:, at:at + HD + 1], pt_hi[:, h, :], v_hi[:, g, h, :], start=True, stop=False)
                        pe.matmul(tile[:, at:at + HD], pt_hi[:, h, :], v_lo[:, g, h, :], start=False, stop=False,
                                  skip_group_check=True)
                        mm = pe.matmul(tile[:, at:at + HD + 1], pt_lo[:, h, :], v_hi[:, g, h, :],
                                       start=False, stop=True)
                    mm.then_inc(full, 1)

                elif job == "T":
                    pe.wait_ge(att.evac(kind, "P1", turn), att.evac_at(kind, "P1", turn))
                    transpose_rows(tile, row_a, full)

                elif job == "Y":
                    pe.wait_ge(att.evac(kind, "T", turn), att.evac_at(kind, "T", turn))
                    row_projection(tile, f"{kind}_o", (t_hi, t_lo), full)

            for n in range(LOOP_START):
                for step in steps_of(Turn(n)):
                    do(*step)
            with pe.Fori(LOOP_START, PAIRS) as reg:
                for step in steps_of(Turn(0, reg)):
                    do(*step)
            for n in range(PAIRS, TURNS):
                for step in steps_of(Turn(n)):
                    do(*step)

        @block.scalar
        def _(act):
            for n in range(len(WEIGHTS)):
                act.wait_ge(load_w[n % 3], 16 * (n // 3 + 1))
                act.activation(w_hi[:, n], staging[n % 3], ACT.Copy, scale=WSCALE).then_inc(weight_hi, 1)

            def normalise(z, small, dst, norm):
                for g in range(2):
                    a = act.activation(dst[:, g, :], z[:, g, :], ACT.Identity, bias=small[:, 30 + g:31 + g],
                                       scale=small[:, 28 + g:29 + g])
                a.then_inc(norm.sem, 1)

            hi_of = {"mL": (m_hi[0], DESCALE), "mR": (m_hi[1], DESCALE), "Q": (qk_hi[0], DESCALE / TEMPER),
                     "K": (qk_hi[1], DESCALE), "T": (t_hi, 1.0)}

            def do(kind, job, part, turn):
                s = slots[kind]
                base, l = job.rstrip("0123"), job[-1]
                hi = g_hi if s is gnn else a_hi

                if part == "hi" and base in ("I", "mL", "mR", "Q", "K", "T"):
                    dst, scale = ((g_ht_hi if s is gnn else a_ht_hi), 1.0) if base == "I" else hi_of[base]
                    act.wait_ge(s.full, s.full_at(kind, job, turn))
                    act.activation(dst[:, :, :], features_of(s.tile(kind, job, turn)), ACT.Copy, scale=scale)\
                       .then_inc(hi.sem, 1)

                elif part == "hi" and base == "X":
                    act.wait_ge(att.full, att.full_at(kind, job, turn))
                    h0 = HB * (int(l) % 2)
                    act.activation(pt_hi[:, h0:h0 + HB, :], heads_of(att.tile(kind, job, turn)), ACT.Copy)\
                       .then_inc(a_hi.sem, 1)

                elif part == "hi" and job == "V":
                    act.wait_ge(att.evac(kind, "V", turn), att.evac_at(kind, "V", turn))
                    act.activation(v_hi[:, :, :, 0:HD], row_a[:, :, :].rearrange("p g (h d) -> p g h d", d=HD),
                                   ACT.Copy).then_inc(a_hi.sem, 1)

                elif part == "relu":
                    act.wait_ge(gnn.full, gnn.full_at(kind, job, turn))
                    tile = gnn.tile(kind, job, turn)
                    for c in range(C):
                        t = act.activation(t32[:, c, :], tile[:, c * T:(c + 1) * T], ACT.Relu,
                                           bias=cols[f"{kind}_c"][:, c:c + 1], scale=cols[f"{kind}_a"][:, c:c + 1])
                    t.then_inc(gnn.evac(kind, job, turn), 1)
                    act.wait_ge(gnn.evac(kind, job, turn), gnn.evac_at(kind, job, turn))
                    act.activation(g_ht_hi[:, :, :], t32[:, :, :], ACT.Copy).then_inc(g_hi.sem, 1)

                elif part == "out" and base in ("H", "hr"):
                    act.wait_ge(gnn.full, gnn.full_at(kind, job, turn))
                    act.activation((h_r if base == "hr" else h_l)[:, :, 0:D], rows_of(gnn.tile(kind, job, turn), D),
                                   ACT.Copy, scale=DESCALE).then_inc(gnn.evac(kind, job, turn), 1)

                elif kind == "L0" and part == "exp":
                    act.wait_ge(g_logits.sem, g_logits.at("L0", l, turn))
                    act.activation(expu[:, :, :], logits[:, :, :], ACT.Exp).then_inc(g_expu.sem, 1)

                elif kind == "L2" and part == "exp":
                    act.wait_ge(g_negmax.sem, g_negmax.at("L2", l, turn))
                    tile = gnn.tile("L2", job, turn)
                    for g in range(2):
                        e = act.activation(expu[:, g, :], tile[:, g * P:(g + 1) * P], ACT.Exp,
                                           bias=g_small[:, 42 + g:43 + g], scale=1.0 / TEMPER,
                                           accum_out=g_small[:, 44 + g:45 + g])
                    e.then_inc(gnn.evac("L2", job, turn), 1)

                elif part == "exp":
                    b = int(l)
                    act.wait_ge(a_max.sem, a_max.at(kind, l, turn))
                    for h in range(HB):
                        e = act.activation(sc[:, b % 2, h, :], sc[:, b % 2, h, :], ACT.Exp,
                                           bias=neg_max[:, b, h:h + 1])
                    e.then_inc(a_exp.sem, 1)

                elif part == "norm" and base == "C":
                    act.wait_ge(g_shift.sem, g_shift.at(kind, job, turn))
                    normalise(g_z, g_small, g_z, g_norm)

                elif part == "norm" and base == "F":
                    act.wait_ge(g_shift.sem, g_shift.at(kind, job, turn))
                    if kind == "L0" and turn.from_on(1):
                        act.wait_ge(att.evac("L1", "Y", turn.before()), att.evac_at("L1", "Y", turn.before()))
                    if kind == "L2" and turn.from_on(2):
                        act.wait_ge(att.evac("L3", "Y", turn), att.evac_at("L3", "Y", turn))
                    normalise(g_z, g_small, x_out[kind], g_norm)

                elif part == "norm":
                    act.wait_ge(a_shift.sem, a_shift.at(kind, "x", turn))
                    if kind == "L1" and turn.from_on(1):
                        act.wait_ge(g_resid.sem, g_resid.at("L2", "x", turn))
                    if kind == "L3" and turn.from_on(3):
                        act.wait_ge(x4_stored.sem, x4_stored.at("L3", "x", turn, back=1))
                    normalise(a_z, a_small, x_out[kind], a_norm)

            for n in range(LOOP_START):
                for step in steps_of(Turn(n)):
                    do(*step)
            with act.Fori(LOOP_START, PAIRS) as reg:
                for step in steps_of(Turn(0, reg)):
                    do(*step)
            for n in range(PAIRS, TURNS):
                for step in steps_of(Turn(n)):
                    do(*step)

        @block.vector
        def _(dve):
            def linked(turn):
                links["n"] += 1
                if turn.reg is None:
                    return links["n"]
                return turn.reg * VECTOR_LINKS + (links["n"] - LOOP_START * VECTOR_LINKS)

            dve.memset(h_l[:, :, :], 1.0).then_inc(ones_ready, 1)
            dve.memset(v_hi[:, :, :, :], 1.0).then_inc(ones_ready, 1)
            for n in range(len(WEIGHTS)):
                dve.wait_ge(weight_hi, n + 1)
                dve.scalar_tensor_tensor(w_lo[:, n], staging[n % 3], WSCALE, w_hi[:, n], ALU.mult, ALU.subtract)\
                   .then_inc(weight_split, 1)
            dve.wait_ge(params_loaded, 16 * (len(rows) + len(cols)))
            dve.wait_ge(consts_ready, 3)

            def stats(z, small, turn):
                dve.bn_stats(small[:, 0:6], z[:, 0, :])
                dve.bn_stats(small[:, 6:12], z[:, 1, :])
                dve.drain()
                dve.bn_aggr(small[:, 16:18], small[:, 0:6])
                dve.bn_aggr(small[:, 18:20], small[:, 6:12]).then_inc(vector_link, 1)
                dve.wait_ge(vector_link, linked(turn))

            def center_and_gain(kind, turn):
                for g in range(2):
                    z = dve.scalar_tensor_tensor(g_z[:, g, :], g_z[:, g, :], g_small[:, 16 + 2 * g:17 + 2 * g],
                                                 rows[f"{kind}_a"][:, :], ALU.subtract, ALU.mult)
                z.then_inc(vector_link, 1)
                dve.wait_ge(vector_link, linked(turn))

            def means(small):
                return small[:, 16:20].rearrange("p (g s) -> p g s", s=2)[:, :, 0]

            def variances(small):
                return small[:, 16:20].rearrange("p (g s) -> p g s", s=2)[:, :, 1]

            lo_of = {"mL": (m_hi[0], m_lo[0], DESCALE), "mR": (m_hi[1], m_lo[1], DESCALE),
                     "Q": (qk_hi[0], qk_lo[0], DESCALE / TEMPER), "K": (qk_hi[1], qk_lo[1], DESCALE),
                     "T": (t_hi, t_lo, 1.0)}

            def do(kind, job, part, turn):
                s = slots[kind]
                base, l = job.rstrip("0123"), job[-1]

                if part == "lo" and base in ("I", "mL", "mR", "Q", "K") or (part == "lo" and job == "T"):
                    hi = g_hi if s is gnn else a_hi
                    dst_hi, dst_lo, scale = lo_of[base] if base != "I" else (
                        (g_ht_hi, g_ht_lo, 1.0) if s is gnn else (a_ht_hi, a_ht_lo, 1.0))
                    dve.wait_ge(hi.sem, hi.at(kind, job, turn))
                    dve.scalar_tensor_tensor(dst_lo[:, :, :], features_of(s.tile(kind, job, turn)), scale,
                                             dst_hi[:, :, :], ALU.mult, ALU.subtract)\
                       .then_inc(s.evac(kind, job, turn), 1)

                elif part == "lo" and job == "T0":
                    dve.wait_ge(g_hi.sem, g_hi.at(kind, "T0", turn))
                    dve.tensor_tensor(g_ht_lo[:, :, :], t32[:, :, :], g_ht_hi[:, :, :], ALU.subtract)\
                       .then_inc(g_lo.sem, 1)

                elif kind == "L0" and part == "mask":
                    dve.wait_ge(gnn.full, gnn.full_at(kind, job, turn))
                    if l == "0":
                        dve.wait_ge(g_masks.sem, g_masks.at("L0", "x", turn))
                    dve.tensor_tensor(gated[:, :, :, :].rearrange("p s g n -> p (s g n)"),
                                      gnn.tile(kind, job, turn)[:, 0:4 * P],
                                      masks[:, :, :, :].rearrange("p s g n -> p (s g n)"), ALU.mult)\
                       .then_inc(gnn.evac(kind, job, turn), 1)

                elif kind == "L0" and part == "ctx":
                    dve.wait_ge(gnn.full, gnn.full_at(kind, job, turn))
                    if l == "0" and g_norm.again(kind, job, turn):
                        dve.wait_ge(g_norm.sem, g_norm.at(kind, job, turn, back=1))
                    tile = gnn.tile(kind, job, turn)
                    sums = rows_of(tile, D + 1)[:, :, D]
                    dve.tensor_scalar(g_small[:, 20:22], sums, 1e-10, 1e-3, ALU.add, ALU.mult)
                    dve.tensor_copy(g_small[:, 46:48], sums).then_inc(vector_link, 1)
                    dve.wait_ge(vector_link, linked(turn))
                    for g in range(2):
                        z = dve.scalar_tensor_tensor(g_z[:, g, :], rows[f"L0_b{l}"][:, :], g_small[:, 46 + g:47 + g],
                                                     tile[:, g * 512:g * 512 + D], ALU.mult, ALU.add)
                    z.then_inc(gnn.evac(kind, job, turn), 1)
                    dve.wait_ge(gnn.evac(kind, job, turn), gnn.evac_at(kind, job, turn))
                    stats(g_z, g_small, turn)
                    dve.tensor_scalar(g_small[:, 22:24], variances(g_small), D / (D - 1.0), None, ALU.mult)\
                       .then_inc(g_var.sem, 1)
                    if l == "1":
                        center_and_gain(kind, turn)

                elif part == "apply":
                    dve.wait_ge(g_root.sem, g_root.at(kind, job, turn))
                    if kind == "L0":
                        dve.tensor_tensor(g_small[:, 26:28], g_small[:, 24:26], g_small[:, 20:22], ALU.add)\
                           .then_inc(vector_link, 1)
                        dve.wait_ge(vector_link, linked(turn))
                        dve.reciprocal(g_small[:, 28:30], g_small[:, 26:28]).then_inc(vector_link, 1)
                        dve.wait_ge(vector_link, linked(turn))
                    for g in range(2):
                        z = dve.scalar_tensor_tensor(g_z[:, g, :], g_z[:, g, :], g_small[:, 28 + g:29 + g],
                                                     rows[f"{kind}_c"][:, :], ALU.mult, ALU.add)
                    z.then_inc(g_affine.sem, 1)

                elif kind == "L0" and base == "C" and part == "shift":
                    dve.wait_ge(g_root.sem, g_root.at("L0", job, turn))
                    dve.tensor_tensor(g_small[:, 26:28], g_small[:, 24:26], g_small[:, 20:22], ALU.add)\
                       .then_inc(vector_link, 1)
                    dve.wait_ge(vector_link, linked(turn))
                    dve.reciprocal(g_small[:, 28:30], g_small[:, 26:28]).then_inc(vector_link, 1)
                    dve.wait_ge(vector_link, linked(turn))
                    dve.scalar_tensor_tensor(g_small[:, 30:32], means(g_small), -1.0, g_small[:, 28:30],
                                             ALU.mult, ALU.mult).then_inc(g_shift.sem, 1)

                elif part == "shift":
                    root, shift, small = (g_root, g_shift, g_small) if s is gnn else (a_root, a_shift, a_small)
                    event = job if s is gnn else "x"
                    dve.wait_ge(root.sem, root.at(kind, event, turn))
                    dve.scalar_tensor_tensor(small[:, 30:32], means(small), -1.0, small[:, 28:30],
                                             ALU.mult, ALU.mult).then_inc(shift.sem, 1)

                elif base == "F" and part == "res":
                    dve.wait_ge(g_affine.sem, g_affine.at(kind, "x", turn))
                    dve.scalar_tensor_tensor(g_z[:, :, :], g_z[:, :, :], 0.0, x_in[kind][:, :, :],
                                             ALU.max, ALU.add).then_inc(g_resid.sem, 1)
                    dve.wait_ge(g_resid.sem, g_resid.at(kind, "x", turn))
                    stats(g_z, g_small, turn)
                    dve.tensor_scalar(g_small[:, 22:24], variances(g_small), 1e-5, None, ALU.add)\
                       .then_inc(g_var.sem, 1)

                elif kind == "L2" and part == "max":
                    dve.wait_ge(gnn.full, gnn.full_at(kind, job, turn))
                    dve.tensor_reduce(g_small[:, 40:42], gnn.tile(kind, job, turn)[:, 0:T]
                                      .rearrange("p (g n) -> p g n", n=P), AX_X, ALU.max).then_inc(vector_link, 1)
                    dve.wait_ge(vector_link, linked(turn))
                    dve.tensor_scalar(g_small[:, 42:44], g_small[:, 40:42], -1.0 / TEMPER, None, ALU.mult)\
                       .then_inc(g_negmax.sem, 1)

                elif kind == "L2" and part == "delta":
                    dve.wait_ge(gnn.evac(kind, job, turn), gnn.evac_at(kind, job, turn))
                    if l == "0":
                        dve.wait_ge(adj2_loaded.sem, adj2_loaded.at("L2", "x", turn))
                    for g in range(2):
                        e = dve.scalar_tensor_tensor(exp_adj[:, g, :], expu[:, g, :], 1.0, adj2[:, g, :],
                                                     ALU.mult, ALU.mult, accum_out=g_small[:, 46 + g:47 + g])
                    e.then_inc(g_exp_adj.sem, 1)
                    dve.wait_ge(g_exp_adj.sem, g_exp_adj.at("L2", l, turn))
                    for g in range(2):
                        dve.scalar_tensor_tensor(logits[:, g, :], exp_adj[:, g, :], 1.0, ident[:, :],
                                                 ALU.mult, ALU.mult, accum_out=g_small[:, 48 + g:49 + g])
                    dve.scalar_tensor_tensor(g_small[:, 50:52], g_small[:, 44:46], 1e-10, g_small[:, 46:48],
                                             ALU.mult, ALU.add).then_inc(vector_link, 1)
                    dve.wait_ge(vector_link, linked(turn))
                    dve.scalar_tensor_tensor(g_small[:, 52:54], g_small[:, 50:52], 1e-12, g_small[:, 50:52],
                                             ALU.mult, ALU.mult).then_inc(vector_link, 1)
                    dve.wait_ge(vector_link, linked(turn))

                elif kind == "L2" and part == "mask":
                    dve.wait_ge(gnn.full, gnn.full_at(kind, job, turn))
                    tile = gnn.tile(kind, job, turn)[:, 0:T].rearrange("p (s g n) -> p s g n", s=1, g=2)
                    dve.tensor_tensor(gated[:, :, :, :], tile.to_broadcast([P, 2, 2, P]),
                                      tri_strict[:, :, :].unsqueeze(2).to_broadcast([P, 2, 2, P]), ALU.mult)\
                       .then_inc(gnn.evac(kind, job, turn), 1)

                elif base in ("hl", "hs") and part == "out":
                    dve.wait_ge(gnn.full, gnn.full_at(kind, job, turn))
                    dve.scalar_tensor_tensor(h_s if base == "hs" else h_l[:, :, 0:D],
                                             rows_of(gnn.tile(kind, job, turn), D), DESCALE,
                                             both_graphs(rows[f"L2_b{base[1]}{l}"]), ALU.mult, ALU.add)\
                       .then_inc(gnn.evac(kind, job, turn), 1)

                elif kind == "L2" and part == "ctx":
                    dve.wait_ge(gnn.full, gnn.full_at(kind, job, turn))
                    dve.wait_ge(gnn.evac(kind, "hs" + l, turn), gnn.evac_at(kind, "hs" + l, turn))
                    if l == "0" and g_norm.again(kind, job, turn):
                        dve.wait_ge(g_norm.sem, g_norm.at(kind, job, turn, back=1))
                    tile = gnn.tile(kind, job, turn)
                    for g in range(2):
                        z = dve.scalar_tensor_tensor(g_z[:, g, :], h_s[:, g, :], g_small[:, 48 + g:49 + g],
                                                     tile[:, g * 512:g * 512 + D], ALU.mult, ALU.add)
                    z.then_inc(gnn.evac(kind, job, turn), 1)
                    dve.wait_ge(gnn.evac(kind, job, turn), gnn.evac_at(kind, job, turn))
                    stats(g_z, g_small, turn)
                    dve.tensor_tensor(g_small[:, 22:24], variances(g_small), g_small[:, 52:54], ALU.add)\
                       .then_inc(g_var.sem, 1)
                    if l == "1":
                        center_and_gain(kind, turn)

                elif job == "V" and part == "out":
                    dve.wait_ge(att.full, att.full_at(kind, job, turn))
                    dve.scalar_tensor_tensor(row_a[:, :, :], rows_of(att.tile(kind, job, turn), D), DESCALE,
                                             both_graphs(rows[f"{kind}_bv"]), ALU.mult, ALU.add)\
                       .then_inc(att.evac(kind, job, turn), 1)

                elif part == "max":
                    b = int(l)
                    dve.wait_ge(att.full, att.full_at(kind, job, turn))
                    if b == 0 and kind == "L1":
                        dve.wait_ge(adj1_loaded.sem, adj1_loaded.at("L1", "x", turn))
                    if b == 0 and kind == "L3":
                        dve.wait_ge(adj3_loaded.sem, adj3_loaded.at("L3", "x", turn))
                    if b >= 2:
                        dve.wait_ge(att.full, att.full_at(kind, f"X{b - 2}", turn))
                    edges = adj_of[kind][:, b // 2:b // 2 + 1, :].to_broadcast([P, HB, P])
                    dve.scalar_tensor_tensor(sc[:, b % 2], edges, 2.0 if kind == "L1" else 1.0,
                                             heads_of(att.tile(kind, job, turn)), ALU.mult, ALU.add)\
                       .then_inc(att.evac(kind, job, turn), 1)
                    dve.wait_ge(att.evac(kind, job, turn), att.evac_at(kind, job, turn))
                    dve.tensor_reduce(neg_max[:, b, :], sc[:, b % 2], AX_X, ALU.max, negate=True)\
                        .then_inc(a_max.sem, 1)

                elif base == "X" and part == "lo":
                    dve.wait_ge(a_hi.sem, a_hi.at(kind, job, turn))
                    h0 = HB * (int(l) % 2)
                    dve.tensor_tensor(pt_lo[:, h0:h0 + HB, :], heads_of(att.tile(kind, job, turn)),
                                      pt_hi[:, h0:h0 + HB, :], ALU.subtract)\
                       .then_inc(att.evac(kind, job, turn), 1)

                elif base == "P" and part == "out":
                    g = int(l)
                    dve.wait_ge(att.full, att.full_at(kind, job, turn))
                    if g == 0:
                        dve.wait_ge(a_vlo.sem, a_vlo.at(kind, "x", turn))
                        dve.wait_ge(a_hi.sem, a_hi.at(kind, "V", turn))
                    dve.wait_ge(a_max.sem, a_max.at(kind, str(2 * g + 1), turn))
                    tile = att.tile(kind, job, turn)[:, 0:HEADS * (HD + 1)].rearrange("p (h d) -> p h d", d=HD + 1)
                    sums = tile[:, :, HD]
                    is_zero, keep, recip = a_small[:, 32:44], a_small[:, 44:56], a_small[:, 56:68]
                    dve.reciprocal(recip, sums)
                    dve.tensor_scalar(is_zero, neg_max[:, 2 * g:2 * g + 2, :].rearrange("p b h -> p (b h)"),
                                      0.0, None, ALU.is_equal).then_inc(vector_link, 1)
                    dve.wait_ge(vector_link, linked(turn))
                    dve.scalar_tensor_tensor(keep, sums, float(P), is_zero, ALU.is_ge, ALU.mult)\
                       .then_inc(vector_link, 1)
                    dve.wait_ge(vector_link, linked(turn))
                    dve.tensor_scalar(keep, keep, -1.0, 1.0, ALU.mult, ALU.add).then_inc(vector_link, 1)
                    dve.wait_ge(vector_link, linked(turn))
                    dve.tensor_tensor(recip, recip, keep, ALU.mult).then_inc(vector_link, 1)
                    dve.wait_ge(vector_link, linked(turn))
                    dve.tensor_tensor(row_a[:, g, :].rearrange("p (h d) -> p h d", d=HD), tile[:, :, 0:HD],
                                      recip.unsqueeze(2).to_broadcast([P, HEADS, HD]), ALU.mult)\
                       .then_inc(att.evac(kind, job, turn), 1)

                elif job == "Y" and part == "res":
                    dve.wait_ge(att.full, att.full_at(kind, job, turn))
                    dve.wait_ge(a_xb.sem, a_xb.at(kind, "x", turn))
                    if a_norm.again(kind, "x", turn):
                        dve.wait_ge(a_norm.sem, a_norm.at(kind, "x", turn, back=1))
                    dve.scalar_tensor_tensor(a_z[:, :, :], rows_of(att.tile(kind, job, turn), D), DESCALE,
                                             x_in[kind][:, :, :], ALU.mult, ALU.add)\
                       .then_inc(att.evac(kind, job, turn), 1)
                    dve.wait_ge(att.evac(kind, job, turn), att.evac_at(kind, job, turn))
                    stats(a_z, a_small, turn)
                    dve.tensor_scalar(a_small[:, 22:24], variances(a_small), 1e-5, None, ALU.add)\
                       .then_inc(a_var.sem, 1)

            for n in range(LOOP_START):
                for step in steps_of(Turn(n)):
                    do(*step)
            before_loop = links["n"]
            with dve.Fori(LOOP_START, PAIRS) as reg:
                for step in steps_of(Turn(0, reg)):
                    do(*step)
            assert links["n"] - before_loop == VECTOR_LINKS, links["n"] - before_loop
            links["n"] = before_loop + (PAIRS - LOOP_START) * VECTOR_LINKS
            for n in range(PAIRS, TURNS):
                for step in steps_of(Turn(n)):
                    do(*step)

        @block.gpsimd
        def _(pool):
            pool.memset(ident[:, :], 0.0).then_inc(consts_filled, 1)
            pool.memset(tri_scaled[:, :, :], 1.0 / TEMPER).then_inc(consts_filled, 1)
            pool.memset(tri_strict[:, :, :], 1.0).then_inc(consts_filled, 1)
            pool.memset(half[:, :], 0.5).then_inc(consts_filled, 1)
            pool.memset(neg_half[:, :], -0.5).then_inc(consts_filled, 1)
            pool.wait_ge(consts_filled, 5)
            pool.affine_select(out=ident[:, :], in_=ident[:, :], compare_op=ALU.not_equal, fill=1.0, base=0,
                               pattern=[[-1, P]], channel_multiplier=1).then_inc(consts_ready, 1)
            pool.affine_select(out=tri_scaled[:, 0, :], in_=tri_scaled[:, 0, :], compare_op=ALU.is_ge, fill=0.0,
                               base=0, pattern=[[-1, P]], channel_multiplier=1)
            pool.affine_select(out=tri_scaled[:, 1, :], in_=tri_scaled[:, 1, :], compare_op=ALU.is_ge, fill=0.0,
                               base=-1, pattern=[[1, P]], channel_multiplier=-1).then_inc(consts_ready, 1)
            pool.affine_select(out=tri_strict[:, 0, :], in_=tri_strict[:, 0, :], compare_op=ALU.is_ge, fill=0.0,
                               base=-1, pattern=[[-1, P]], channel_multiplier=1)
            pool.affine_select(out=tri_strict[:, 1, :], in_=tri_strict[:, 1, :], compare_op=ALU.is_ge, fill=0.0,
                               base=-1, pattern=[[1, P]], channel_multiplier=-1).then_inc(consts_ready, 1)
            pool.wait_ge(consts_ready, 3)
            pool.wait_ge(params_loaded, 16 * (len(rows) + len(cols)))

            def do(kind, job, part, turn):
                s = slots[kind]
                base, l = job.rstrip("0123"), job[-1]

                if (kind, job) == ("L0", "masks"):
                    pool.wait_ge(adj0_loaded.sem, adj0_loaded.at("L0", "x", turn))
                    if turn.from_on(1):
                        pool.wait_ge(gnn.evac("L0", "U1", turn.before()), gnn.evac_at("L0", "U1", turn.before()))
                    for side, edges in enumerate((adjt0, adj0)):
                        m = pool.tensor_tensor(masks[:, side], edges[:, :, :],
                                               tri_scaled[:, side:side + 1, :].to_broadcast([P, 2, P]), ALU.mult)
                    m.then_inc(g_masks.sem, 1)

                elif part == "add":
                    pool.wait_ge(gnn.evac(kind, job, turn), gnn.evac_at(kind, job, turn))
                    pool.tensor_tensor(logits[:, :, :], gated[:, 0], gated[:, 1], ALU.add).then_inc(g_logits.sem, 1)

                elif part == "adj":
                    pool.wait_ge(g_expu.sem, g_expu.at("L0", l, turn))
                    pool.tensor_tensor(exp_adj[:, :, :], expu[:, :, :], adjt0[:, :, :], ALU.mult)\
                        .then_inc(g_exp_adj.sem, 1)

                elif part == "root":
                    var, rt, small = (g_var, g_root, g_small) if s is gnn else (a_var, a_root, a_small)
                    event = job if s is gnn else "x"
                    power, at = (half, 24) if kind == "L0" and base == "C" else (neg_half, 28)
                    pool.wait_ge(var.sem, var.at(kind, event, turn))
                    pool.tensor_tensor(small[:, at:at + 2], small[:, 22:24], power[:, :], ALU.pow).then_inc(rt.sem, 1)

                elif part == "bias":
                    pool.wait_ge(gnn.evac(kind, job, turn), gnn.evac_at(kind, job, turn))
                    pool.tensor_tensor(h_r, h_r, both_graphs(rows[f"L2_br{l}"]), ALU.add)\
                        .then_inc(g_biased.sem, 1)

                elif job == "V" and part == "lo":
                    pool.wait_ge(a_hi.sem, a_hi.at(kind, "V", turn))
                    pool.tensor_tensor(v_lo[:, :, :, :], row_a[:, :, :].rearrange("p g (h d) -> p g h d", d=HD),
                                       v_hi[:, :, :, 0:HD], ALU.subtract).then_inc(a_vlo.sem, 1)

                elif job == "xb":
                    pool.wait_ge(att.full, att.full_at(kind, "I", turn))
                    pool.tensor_tensor(x_in[kind][:, :, :], x_in[kind][:, :, :], both_graphs(rows[f"{kind}_bo"]),
                                       ALU.add).then_inc(a_xb.sem, 1)

            for n in range(LOOP_START):
                for step in steps_of(Turn(n)):
                    do(*step)
            with pool.Fori(LOOP_START, PAIRS) as reg:
                for step in steps_of(Turn(0, reg)):
                    do(*step)
            for n in range(PAIRS, TURNS):
                for step in steps_of(Turn(n)):
                    do(*step)


def kernel(**inputs):
    import numpy as _np
    import concourse.bacc as _bacc
    from concourse import mybir as _mybir
    from concourse.bass_utils import run_bass_kernel_spmd as _run

    a = {k: _np.asarray(v) for k, v in inputs.items()}
    weights = {
        "L0_left0": a["L0_gnn_W_left"][0], "L0_right0": a["L0_gnn_W_right"][0], "L0_lin0": a["L0_gnn_W_lin"][0],
        "L0_left1": a["L0_gnn_W_left"][1], "L0_right1": a["L0_gnn_W_right"][1], "L0_lin1": a["L0_gnn_W_lin"][1],
        "L1_q": a["L1_gnn_Wq"], "L1_k": a["L1_gnn_Wk"], "L1_v": a["L1_gnn_Wv"], "L1_o": a["L1_gnn_Wo"],
        "L2_l0": a["L2_gnn_Wl"][0], "L2_s0": a["L2_gnn_Ws"][0], "L2_r0": a["L2_gnn_Wr"][0],
        "L2_l1": a["L2_gnn_Wl"][1], "L2_s1": a["L2_gnn_Ws"][1], "L2_r1": a["L2_gnn_Wr"][1],
        "L3_q": a["L3_gnn_Wq"], "L3_k": a["L3_gnn_Wk"], "L3_v": a["L3_gnn_Wv"], "L3_o": a["L3_gnn_Wo"],
    }
    vectors = {
        "L0_b0": a["L0_gnn_b_lin"][0], "L0_b1": a["L0_gnn_b_lin"][1],
        "L0_a": a["L0_gnn_ln_a"][1], "L0_c": a["L0_gnn_ln_b"][1],
        "col_L0_a": a["L0_gnn_ln_a"][0].reshape(C, P).T, "col_L0_c": a["L0_gnn_ln_b"][0].reshape(C, P).T,
        "L1_bv": a["L1_gnn_bv"], "L1_bo": a["L1_gnn_bo"],
        "L2_bl0": a["L2_gnn_bl"][0], "L2_bs0": a["L2_gnn_bs"][0], "L2_br0": a["L2_gnn_br"][0],
        "L2_bl1": a["L2_gnn_bl"][1], "L2_bs1": a["L2_gnn_bs"][1], "L2_br1": a["L2_gnn_br"][1],
        "L2_a": a["L2_gnn_ln_w"][1], "L2_c": a["L2_gnn_ln_b"][1],
        "col_L2_a": a["L2_gnn_ln_w"][0].reshape(C, P).T, "col_L2_c": a["L2_gnn_ln_b"][0].reshape(C, P).T,
        "L3_bv": a["L3_gnn_bv"], "L3_bo": a["L3_gnn_bo"],
    }
    arrays = {
        "x": _np.ascontiguousarray(a["x"]),
        "adj": _np.ascontiguousarray(a["adj"]),
        "adj_t": _np.ascontiguousarray(a["adj"].transpose(0, 2, 1)),
        "weights_t": _np.ascontiguousarray(_np.stack([weights[n].T for n in WEIGHTS])),
        **{f"vec_{n}": _np.ascontiguousarray(v) for n, v in vectors.items()},
    }
    nc = _bacc.Bacc("TRN2", target_bir_lowering=False, num_devices=1)
    dram = {n: nc.dram_tensor(n, v.shape, _mybir.dt.from_np(v.dtype), kind="ExternalInput").ap()
            for n, v in arrays.items()}
    out = nc.dram_tensor("out", (NG, P, D), _mybir.dt.float32, kind="ExternalOutput").ap()
    graph_stack_kernel(nc, dram["x"], dram["adj"], dram["adj_t"], dram["weights_t"],
                       {n: dram[f"vec_{n}"] for n in vectors}, out)
    r = _run(nc, [arrays], core_ids=[0])
    return r.results[0]["out"]
```

```python
from contextlib import ExitStack

import concourse.bass as bass
from concourse import mybir

P = 128
NG = 64
D = 384
C = D // P
PAIRS = NG // 2
T = 2 * P
HEADS = 12
HD = D // HEADS
HB = HEADS // 2
WSCALE = 64.0
DESCALE = 1.0 / WSCALE
TEMPER = float(D) ** 0.5

F32 = mybir.dt.float32
F16 = mybir.dt.float16
ALU = mybir.AluOpType
ACT = mybir.ActivationFunctionType
AX_X = mybir.AxisListType.X

WEIGHTS = (["L0_left0", "L0_right0", "L0_lin0", "L0_left1", "L0_right1", "L0_lin1"]
           + ["L1_q", "L1_k", "L1_v", "L1_o"]
           + ["L2_l0", "L2_s0", "L2_r0", "L2_l1", "L2_s1", "L2_r1"]
           + ["L3_q", "L3_k", "L3_v", "L3_o"])
L0_WEIGHTS = 6

JOBS = {
    "L0": ("I", "mL0", "mR0", "U0", "H0", "C0", "T0", "mL1", "mR1", "U1", "H1", "C1"),
    "L2": ("I", "S0", "X0", "hl0", "hr0", "hs0", "C0", "T0", "S1", "X1", "hl1", "hr1", "hs1", "C1"),
    "L1": ("I", "Q", "K", "V", "S0", "S1", "X0", "S2", "X1", "P0", "S3", "X2", "X3", "P1", "T", "Y"),
}
JOBS["L3"] = JOBS["L1"]

LAG = {"L0": 0, "L1": 0, "L2": 1, "L3": 2}
VECTOR_LINKS = 32

WALK = """
    -L2:C0.norm -L2:T0 -L1:Q.lo -L2:T0.relu -L3:P1.out -L2:T0.hi -L1:K -L3:T -L1:K.hi -L2:T0.lo -L1:Q.stack_hi
    -L3:T.hi -L1:K.lo -L1:Q.stack_lo -L2:S1 -L3:T.lo -L2:hl1 -L2:S1.max -L2:S1.exp -L2:hl1.out -L3:Y -L1:V
    -L3:Y.res -L1:K.stack_hi -L2:hr1 -L2:hr1.out -L2:S1.delta -L3:Y.stats -L1:K.stack_lo -L1:S0 -L3:Y.root
    -L1:V.out -L2:S1.diag -L1:S0.add -L1:S0.max L2:load -L1:S1 L0:edges -L1:V.hi -L2:X1 -L2:hs1 -L2:hr1.bias
    L0:load -L2:X1.mask L0:I -L1:S0.exp L0:masks -L1:X0 -L1:S1.add -L2:hs1.out -L1:S2 -L1:S1.max -L2:C1 L0:I.hi
    -L1:X0.hi L0:I.lo -L1:X0.lo -L1:S2.add L0:mL0 -L2:C1.ctx --L3:store -L1:S2.max -L1:S1.exp -L2:C1.stats
    -L2:C1.center -L1:X1 -L1:V.lo -L1:X1.hi -L1:X1.lo L0:mL0.hi L0:mR0 L0:mR0.hi L0:mL0.lo -L2:C1.root
    -L1:S2.exp -L2:C1.apply -L1:P0 -L1:S3 L0:mR0.lo -L2:F.res L0:U0 -L2:F.stats -L2:F.root L0:U0.mask L0:U0.add
    -L2:F.shift -L2:F.norm L0:U0.exp L0:H0 L0:H0.out L0:U0.adj L3:load -L1:P0.out L3:I -L1:S3.add -L3:Y.shift
    L3:I.hi -L1:S3.max L0:C0 -L1:xb L3:I.lo -L3:Y.norm -L1:X2 L0:C0.ctx -L1:X2.hi -L1:S3.exp L0:C0.stats L3:Q
    L0:C0.root L3:Q.hi -L1:X2.lo -L1:X3 L0:C0.shift L0:C0.norm L0:T0 L3:Q.lo -L1:X3.hi L0:T0.relu L0:T0.hi L3:K
    L3:K.hi -L1:X3.lo L3:Q.stack_hi -L1:P1 L0:T0.lo L3:Q.stack_lo L3:K.stack_hi L1:load -L1:P1.out L0:mL1
    L3:K.lo -L1:T -L1:T.hi -L1:T.lo L0:mL1.hi L0:mR1 L0:mL1.lo L0:mR1.hi L3:K.stack_lo L0:mR1.lo L3:xb -L1:Y
    L3:V -L1:Y.res L3:S0 -L1:Y.stats L3:V.out L0:U1 -L1:Y.root -L1:Y.shift L3:S0.add -L1:Y.norm L3:V.hi
    L3:S0.max -L1:store L0:U1.mask L3:S1 L0:H1 L3:S0.exp L0:U1.add L3:S1.add L2:I L0:U1.exp L3:S1.max L3:V.lo
    L0:H1.out L3:X0 L2:I.hi L2:I.lo L3:S2 L3:X0.hi L0:U1.adj L3:X0.lo L3:S1.exp L0:C1 L0:C1.ctx L2:S0 L3:S2.add
    L2:S0.max L0:C1.stats L0:C1.center L3:S2.max L0:C1.root L2:S0.exp L2:hl0 L3:X1 L0:C1.apply L2:hr0 L3:X1.hi
    L3:S2.exp L3:X1.lo L0:F.res L3:P0 L2:hl0.out L3:S3 L2:S0.delta L0:F.stats L3:P0.out L2:hr0.out L2:X0
    L0:F.root L0:F.shift L0:F.norm L3:S3.add L2:S0.diag L2:X0.mask L2:hs0 L3:X2 L1:I L2:hr0.bias L2:C0 L3:S3.max
    L2:hs0.out L3:X2.hi L1:I.hi L3:X2.lo L1:I.lo L3:S3.exp L2:C0.ctx L2:C0.stats L3:X3 L1:Q L3:X3.hi L1:Q.hi
    L3:X3.lo L3:P1 L2:C0.root L2:C0.shift
"""


def steps_in(walk):
    for name in walk.split():
        kind, step = name.lstrip("-").split(":")
        yield kind, name.count("-"), step


ORDER = list(steps_in(WALK))
MOST_BACK = max(back for _, back, _ in ORDER)
LOOP_TURNS = 2
LOOP_START = 3 + MOST_BACK + (PAIRS - 3 - MOST_BACK) % LOOP_TURNS
TURNS = PAIRS + 2 + MOST_BACK


class Turn:

    def __init__(self, k, reg=None):
        self.k, self.reg = k, reg

    def before(self):
        return Turn(self.k - 1, self.reg)

    def from_on(self, k):
        return self.reg is not None or self.k >= k

    def index(self, lag):
        return self.k - lag if self.reg is None else self.reg + (self.k - lag)


class Counter:

    def __init__(self, events):
        self.places = []
        for kind, listed in events.items():
            for n, (event, step, amount) in enumerate(listed):
                at = [i for i, (k, _, s) in enumerate(ORDER) if (k, s) == (kind, step)][0]
                self.places.append((kind, event, (at, n), ORDER[at][1] + LAG[kind], amount))

    def per_turn(self):
        return sum(amount for *_, amount in self.places)

    def until(self, kind, event, turn):
        place, late = [(p, lt) for k, e, p, lt, _ in self.places if (k, e) == (kind, event)][0]
        walked = turn.k + late - LAG[kind]
        total = 0
        for _, _, other, other_late, amount in self.places:
            pairs = walked - other_late + (other <= place)
            total += amount * (pairs if turn.reg is not None else min(max(pairs, 0), PAIRS))
        return total


class Signal(Counter):

    def __init__(self, sem, events):
        super().__init__(events)
        self.sem = sem

    def at(self, kind, event, turn, back=0):
        v = self.until(kind, event, turn) - back * self.places[0][4]
        return v if turn.reg is None else turn.reg * self.per_turn() + v

    def again(self, kind, event, turn):
        return turn.reg is not None or self.at(kind, event, turn, back=1) > 0


class Slots(Counter):

    def __init__(self, full, evacuated, tensors, kinds):
        super().__init__({kind: [(job, job, 1) for job in JOBS[kind]] for kind in kinds})
        self.full, self.evacuated, self.tensors = full, evacuated, tensors
        assert self.per_turn() % 2 == 0

    def number(self, kind, job, turn):
        return self.until(kind, job, turn) - 1

    def tile(self, kind, job, turn):
        return self.tensors[self.number(kind, job, turn) % 2]

    def evac(self, kind, job, turn):
        return self.evacuated[self.number(kind, job, turn) % 2]

    def full_at(self, kind, job, turn):
        n = self.number(kind, job, turn) + 1
        return n if turn.reg is None else turn.reg * self.per_turn() + n

    def evac_at(self, kind, job, turn, back=0):
        v = self.number(kind, job, turn) // 2 + 1 - back
        return v if turn.reg is None else turn.reg * (self.per_turn() // 2) + v

    def free_at(self, kind, job, turn):
        return self.evac_at(kind, job, turn, back=1)

    def used(self, kind, job, turn):
        return turn.reg is not None or self.free_at(kind, job, turn) > 0


def graph_stack_kernel(nc, x, adj, adj_t, weights_t, vectors, out):
    ctx = ExitStack()
    with ctx:
        def sb(name, shape, dt=F32):
            return ctx.enter_context(nc.sbuf_tensor(name, shape, dt))

        def sem(name):
            return ctx.enter_context(nc.semaphore(name))

        w_hi = sb("w_hi", [P, len(WEIGHTS), C, D], F16)
        w_lo = sb("w_lo", [P, len(WEIGHTS), C, D], F16)
        rows = {n: sb(f"row_{n}", [P, D]) for n in (
            "L0_b0", "L0_b1", "L0_a", "L0_c", "L1_bv", "L1_bo", "L2_bl0", "L2_bs0", "L2_br0",
            "L2_bl1", "L2_bs1", "L2_br1", "L2_a", "L2_c", "L3_bv", "L3_bo")}
        cols = {n: sb(f"col_{n}", [P, C]) for n in ("L0_a", "L0_c", "L2_a", "L2_c")}
        ident = sb("ident", [P, P])
        tri_scaled = sb("tri_scaled", [P, 2, P])
        tri_strict = sb("tri_strict", [P, 2, P])
        half = sb("half", [P, 2])
        neg_half = sb("neg_half", [P, 2])

        x0 = sb("x0", [P, 2, D])
        x1 = sb("x1", [P, 2, D])
        x2 = sb("x2", [P, 2, D])
        x3 = sb("x3", [P, 2, D])
        x4 = sb("x4", [P, 2, D])
        x_in = {"L0": x0, "L1": x1, "L2": x2, "L3": x3}
        x_out = {"L0": x1, "L1": x2, "L2": x3, "L3": x4}
        adj0 = sb("adj0", [P, 2, P])
        adj1 = sb("adj1", [P, 2, P])
        adjt0 = sb("adjt0", [P, 2, P])
        adj2 = sb("adj2", [P, 2, P])
        adj3 = sb("adj3", [P, 2, P])
        adj_of = {"L1": adj1, "L3": adj3}

        g_ht_hi = sb("g_ht_hi", [P, C, T], F16)
        g_ht_lo = sb("g_ht_lo", [P, C, T], F16)
        m_all = sb("m_all", [P, 4 * C * T], F16)
        m_hi = [m_all[:, s * 2 * C * T:s * 2 * C * T + C * T].rearrange("p (c t) -> p c t", c=C) for s in range(2)]
        m_lo = [m_all[:, s * 2 * C * T + C * T:(s + 1) * 2 * C * T].rearrange("p (c t) -> p c t", c=C)
                for s in range(2)]
        h_r = m_all[:, 0:2 * C * T].bitcast(F32).rearrange("p (g d) -> p g d", g=2)
        h_s = m_all[:, 2 * C * T:4 * C * T].bitcast(F32).rearrange("p (g d) -> p g d", g=2)
        h_l = sb("h_l", [P, 2, D + 1])
        masks = sb("masks", [P, 2, 2, P])
        gated = sb("gated", [P, 2, 2, P])
        logits = sb("logits", [P, 2, P])
        expu = sb("expu", [P, 2, P])
        exp_adj = sb("exp_adj", [P, 2, P])
        t32 = sb("t32", [P, C, T])
        g_z = sb("g_z", [P, 2, D])
        g_small = sb("g_small", [P, 64])

        a_ht_hi = sb("a_ht_hi", [P, C, T], F16)
        a_ht_lo = sb("a_ht_lo", [P, C, T], F16)
        qk_hi = [sb(f"qk_hi{n}", [P, C, T], F16) for n in range(2)]
        qk_lo = [sb(f"qk_lo{n}", [P, C, T], F16) for n in range(2)]
        stack = [sb("stack_q", [P, HEADS, T], F16), sb("stack_k", [P, HEADS, T], F16)]
        row_a = sb("row_a", [P, 2, D])
        v_hi = sb("v_hi", [P, 2, HEADS, HD + 1], F16)
        v_lo = sb("v_lo", [P, 2, HEADS, HD], F16)
        sc = sb("sc", [P, 2, HB, P])
        pt_hi = sb("pt_hi", [P, HEADS, P], F16)
        pt_lo = sb("pt_lo", [P, HEADS, P], F16)
        t_hi, t_lo = (p[:, 0:C * T // P, :].rearrange("p (c g) n -> p c (g n)", c=C) for p in (pt_hi, pt_lo))
        neg_max = sb("neg_max", [P, 4, HB])
        a_z = sb("a_z", [P, 2, D])
        a_small = sb("a_small", [P, 96])

        def rows_of(tile, width):
            return tile[:, :].rearrange("p (g n) -> p g n", g=2)[:, :, 0:width]

        def both_graphs(row):
            return row[:, :].unsqueeze(1).to_broadcast([P, 2, D])

        def features_of(tile):
            return tile[:, 0:C * T].rearrange("p (c t) -> p c t", c=C)

        def heads_of(tile):
            return tile[:, 0:HB * P].rearrange("p (h n) -> p h n", n=P)

        staging = [sc[:, :, :, :].rearrange("p b h n -> p (b h n)")]
        staging += [s[:, :, :].rearrange("p h t -> p (h t)").bitcast(F32) for s in stack]
        staging = [s[:, 0:C * D].rearrange("p (c o) -> p c o", c=C) for s in staging]

        psum = [ctx.enter_context(nc.psum_tensor(f"ps{n}", [P, 1024], F32)) for n in range(4)]

        load_w = [sem(f"load_w{n}") for n in range(3)]
        weight_split = sem("weight_split")
        weight_hi = sem("weight_hi")
        params_loaded = sem("params_loaded")
        consts_filled = sem("consts_filled")
        consts_ready = sem("consts_ready")
        ones_ready = sem("ones_ready")
        vector_link = sem("vector_link")

        gnn = Slots(sem("gnn_full"), [sem("gnn_evac0"), sem("gnn_evac1")], psum[0:2], ("L0", "L2"))
        att = Slots(sem("att_full"), [sem("att_evac0"), sem("att_evac1")], psum[2:4], ("L1", "L3"))
        slots = {"L0": gnn, "L2": gnn, "L1": att, "L3": att}

        def signal(name, events, amount=1):
            listed = {kind: {"x": e} if isinstance(e, str) else e for kind, e in events.items()}
            return Signal(sem(name), {kind: [(event, step, amount) for event, step in e.items()]
                                      for kind, e in listed.items()})

        def parts(part, *jobs):
            return {job: f"{job}.{part}" for job in jobs}

        def both(events, kinds=("L1", "L3")):
            return {kind: events for kind in kinds}

        x0_loaded = signal("x0_loaded", {"L0": "load"}, 16)
        adj0_loaded = signal("adj0_loaded", {"L0": "edges"}, 32)
        adj1_loaded = signal("adj1_loaded", {"L1": "load"}, 16)
        adj2_loaded = signal("adj2_loaded", {"L2": "load"}, 16)
        adj3_loaded = signal("adj3_loaded", {"L3": "load"}, 16)
        x4_stored = signal("x4_stored", {"L3": "store"}, 16)
        g_kinds = ("L0", "L2")
        g_hi = signal("g_hi", {"L0": parts("hi", "I", "mL0", "mR0", "T0", "mL1", "mR1"),
                               "L2": parts("hi", "I", "T0")})
        g_masks = signal("g_masks", {"L0": "masks"})
        g_logits = signal("g_logits", {"L0": {"0": "U0.add", "1": "U1.add"}})
        g_expu = signal("g_expu", {"L0": {"0": "U0.exp", "1": "U1.exp"}})
        g_exp_adj = signal("g_exp_adj", {"L0": {"0": "U0.adj", "1": "U1.adj"}, "L2": {"0": "S0.delta", "1": "S1.delta"}})
        g_negmax = signal("g_negmax", {"L2": {"0": "S0.max", "1": "S1.max"}})
        g_biased = signal("g_biased", {"L2": parts("bias", "hr0", "hr1")})
        g_var = signal("g_var", both({"C0": "C0.stats", "C1": "C1.stats", "F": "F.stats"}, g_kinds))
        g_root = signal("g_root", both(parts("root", "C0", "C1", "F"), g_kinds))
        g_shift = signal("g_shift", both(parts("shift", "C0", "F"), g_kinds))
        g_norm = signal("g_norm", both(parts("norm", "C0", "F"), g_kinds))
        g_centered = signal("g_centered", both("C1.center", g_kinds))
        g_affine = signal("g_affine", both("C1.apply", g_kinds))
        g_lo = signal("g_lo", both("T0.lo", g_kinds))
        g_resid = signal("g_resid", both("F.res", g_kinds))
        a_hi = signal("a_hi", both(parts("hi", "I", "Q", "K", "V", "X0", "X1", "X2", "X3", "T")))
        a_stacked = Signal(sem("a_stacked"), both([(step, step, 16 * (8 if "hi" in step else 4)) for step in (
            "Q.stack_hi", "Q.stack_lo", "K.stack_hi", "K.stack_lo")]))
        a_vlo = signal("a_vlo", both("V.lo"))
        a_max = signal("a_max", both({b: f"S{b}.max" for b in "0123"}))
        a_exp = signal("a_exp", both({b: f"S{b}.exp" for b in "0123"}))
        a_xb = signal("a_xb", both("xb"))
        a_var = signal("a_var", both("Y.stats"))
        a_root = signal("a_root", both("Y.root"))
        a_shift = signal("a_shift", both("Y.shift"))
        a_norm = signal("a_norm", both("Y.norm"))

        def steps_of(turn):
            walk = []
            for kind, back, step in ORDER:
                if turn.reg is not None or 0 <= turn.k - back - LAG[kind] < PAIRS:
                    job, _, part = step.partition(".")
                    walk.append((kind, job, part, Turn(turn.k - back, turn.reg)))
            return with_weights(walk) if turn.reg is None and turn.k == 0 else walk

        def with_weights(walk):
            loads = [step for step in walk if step[:2] in (("L0", "load"), ("L0", "edges"))]
            weights = [("W", str(n), "", None) for n in range(len(WEIGHTS))]
            first, others = weights[:L0_WEIGHTS], weights[L0_WEIGHTS:]
            mixed = loads + first
            for step in walk:
                if step not in loads:
                    mixed.append(step)
                    if step[0] == "L0" and step[1] not in ("masks", "I") and others:
                        mixed.append(others.pop(0))
            assert not others
            return mixed

        links = {"n": 0}
        block = ctx.enter_context(nc.Block())

        @block.sync
        def _(sp):
            def load_weight(n):
                sp.dma_start(staging[n % 3], weights_t[n].rearrange("(c p) o -> p c o", p=P)).then_inc(load_w[n % 3], 16)

            for n in range(3):
                load_weight(n)

            x_pairs = x.rearrange("(q g) n d -> q n g d", g=2)
            out_pairs = out.rearrange("(q g) n d -> q n g d", g=2)
            adj_pairs = adj.rearrange("(q g) i j -> q i g j", g=2)
            adjt_pairs = adj_t.rearrange("(q g) i j -> q i g j", g=2)

            def do(kind, job, part, turn):
                if kind == "W":
                    n = int(job)
                    if n + 3 < len(WEIGHTS):
                        sp.wait_ge(weight_split, n + 1)
                        load_weight(n + 3)
                    if n == L0_WEIGHTS - 3:
                        for name, tile in rows.items():
                            sp.dma_start(tile[:, :], vectors[name].unsqueeze(0).to_broadcast([P, D]))\
                              .then_inc(params_loaded, 16)
                        for name, tile in cols.items():
                            sp.dma_start(tile[:, :], vectors["col_" + name]).then_inc(params_loaded, 16)
                    return
                pair = turn.index(LAG[kind])
                if (kind, job) == ("L0", "load"):
                    if turn.from_on(1):
                        sp.wait_ge(g_resid.sem, g_resid.at("L0", "x", turn.before()))
                    sp.dma_start(x0[:, :, :], x_pairs[pair]).then_inc(x0_loaded.sem, 16)
                elif (kind, job) == ("L0", "edges"):
                    if turn.from_on(1):
                        sp.wait_ge(g_exp_adj.sem, g_exp_adj.at("L0", "1", turn.before()))
                    sp.dma_start(adj0[:, :, :], adj_pairs[pair]).then_inc(adj0_loaded.sem, 16)
                    sp.dma_start(adjt0[:, :, :], adjt_pairs[pair]).then_inc(adj0_loaded.sem, 16)
                elif (kind, job) == ("L1", "load"):
                    if turn.from_on(1):
                        sp.wait_ge(att.evac("L1", "S3", turn.before()), att.evac_at("L1", "S3", turn.before()))
                    sp.dma_start(adj1[:, :, :], adj_pairs[pair]).then_inc(adj1_loaded.sem, 16)
                elif (kind, job) == ("L2", "load"):
                    if turn.from_on(2):
                        sp.wait_ge(g_exp_adj.sem, g_exp_adj.at("L2", "1", turn.before()))
                    sp.dma_start(adj2[:, :, :], adj_pairs[pair]).then_inc(adj2_loaded.sem, 16)
                elif (kind, job) == ("L3", "load"):
                    if turn.from_on(3):
                        sp.wait_ge(att.evac("L3", "S3", turn.before()), att.evac_at("L3", "S3", turn.before()))
                    sp.dma_start(adj3[:, :, :], adj_pairs[pair]).then_inc(adj3_loaded.sem, 16)
                elif part in ("stack_hi", "stack_lo"):
                    n = "QK".index(job)
                    if part == "stack_hi":
                        sp.wait_ge(a_hi.sem, a_hi.at(kind, job, turn))
                        src, thirds = qk_hi[n], ((0, 1), (0, 2))[n]
                    else:
                        sp.wait_ge(att.evac(kind, job, turn), att.evac_at(kind, job, turn))
                        src, thirds = qk_lo[n], ((2,), (1,))[n]
                    for third in thirds:
                        for r in range(4):
                            sp.dma_start(stack[n][32 * third:32 * third + 32, r:HEADS:4, :],
                                         src[32 * r:32 * r + 32, :, :]).then_inc(a_stacked.sem, 16)
                elif (kind, job) == ("L3", "store"):
                    sp.wait_ge(a_norm.sem, a_norm.at("L3", "x", turn))
                    sp.dma_start(out_pairs[pair], x4[:, :, :]).then_inc(x4_stored.sem, 16)

            for n in range(LOOP_START):
                for step in steps_of(Turn(n)):
                    do(*step)
            with sp.Fori(LOOP_START, PAIRS - LOOP_TURNS + 1, LOOP_TURNS) as reg:
                for n in range(LOOP_TURNS):
                    for step in steps_of(Turn(n, reg)):
                        do(*step)
            for n in range(PAIRS, TURNS):
                for step in steps_of(Turn(n)):
                    do(*step)
            sp.wait_ge(x4_stored.sem, 16 * PAIRS)

        @block.tensor
        def _(pe):
            def split_products(tile, stationary, moving, last):
                (a_hi_, a_lo_), (b_hi_, b_lo_) = stationary, moving
                for k in range(C):
                    for n, (a, b) in enumerate(((a_hi_, b_hi_), (a_hi_, b_lo_), (a_lo_, b_hi_))):
                        mm = pe.matmul(tile, a(k), b(k), start=(k == 0 and n == 0), stop=(k == C - 1 and n == 2))
                if last is not None:
                    mm.then_inc(last, 1)

            def feature_projection(tile, weight, ht, full):
                w = WEIGHTS.index(weight)
                for o in range(C):
                    cols_ = slice(o * P, (o + 1) * P)
                    split_products(tile[:, o * T:(o + 1) * T],
                                   [lambda k, m=m: m[:, w, k, cols_] for m in (w_hi, w_lo)],
                                   [lambda k, h=h: h[:, k, :] for h in ht], full if o == C - 1 else None)

            def row_projection(tile, weight, ht, full):
                w = WEIGHTS.index(weight)
                for g in range(2):
                    nodes = slice(g * P, (g + 1) * P)
                    split_products(tile[:, g * 512:g * 512 + D],
                                   [lambda k, h=h: h[:, k, nodes] for h in ht],
                                   [lambda k, m=m: m[:, w, k, :] for m in (w_hi, w_lo)], full if g else None)

            def transpose_rows(tile, source, full):
                for c in range(C):
                    for g in range(2):
                        mm = pe.transpose(tile[:, c * T + g * P:c * T + (g + 1) * P],
                                          source[:, g, c * P:(c + 1) * P], ident[:, :])
                mm.then_inc(full, 1)

            pe.wait_ge(consts_ready, 3)
            pe.wait_ge(weight_split, L0_WEIGHTS)
            pe.wait_ge(ones_ready, 2)
            g_ht, a_ht = (g_ht_hi, g_ht_lo), (a_ht_hi, a_ht_lo)

            def evacuated(kind, job, turn, *sources):
                s = slots[kind]
                other = [j for j in sources if s.evac(kind, j, turn) is not s.evac(kind, job, turn)]
                if not other:
                    return s.evac(kind, job, turn), s.free_at(kind, job, turn)
                last = max(other, key=lambda j: s.number(kind, j, turn))
                return s.evac(kind, last, turn), s.evac_at(kind, last, turn)

            def do(kind, job, part, turn):
                if kind == "W" or part or job not in JOBS[kind]:
                    return
                if (kind, job) == ("L1", "I") and not turn.from_on(1):
                    pe.wait_ge(weight_split, len(WEIGHTS))
                s = slots[kind]
                tile, full = s.tile(kind, job, turn), s.full
                base, l = job.rstrip("0123"), job[-1]
                if s.used(kind, job, turn):
                    pe.wait_ge(s.evac(kind, job, turn), s.free_at(kind, job, turn))

                if job == "I":
                    if kind == "L0":
                        pe.wait_ge(x0_loaded.sem, x0_loaded.at("L0", "x", turn))
                    elif kind == "L1":
                        pe.wait_ge(g_norm.sem, g_norm.at("L0", "F", turn))
                    elif kind == "L2":
                        pe.wait_ge(a_norm.sem, a_norm.at("L1", "x", turn.before()))
                    else:
                        pe.wait_ge(g_norm.sem, g_norm.at("L2", "F", turn.before()))
                    transpose_rows(tile, x_in[kind], full)

                elif base in ("mL", "mR"):
                    if base == "mL":
                        if l == "0":
                            pe.wait_ge(*evacuated(kind, job, turn, "I"))
                        else:
                            pe.wait_ge(g_lo.sem, g_lo.at(kind, "x", turn))
                    feature_projection(tile, ("L0_left" if base == "mL" else "L0_right") + l, g_ht, full)

                elif base == "U":
                    pe.wait_ge(*evacuated(kind, job, turn, "mL" + l, "mR" + l))
                    for side in range(2):
                        for g in range(2):
                            at, n = (2 * side + g) * P, slice(g * P, (g + 1) * P)
                            split_products(tile[:, at:at + P],
                                           [lambda k, m=m: m[:, k, n] for m in (m_hi[side], m_lo[side])],
                                           [lambda k, h=h: h[:, k, n] for h in g_ht],
                                           full if side and g else None)

                elif base == "H":
                    row_projection(tile, "L0_lin" + l, g_ht, full)

                elif base == "C" and kind == "L0":
                    pe.wait_ge(*evacuated(kind, job, turn, "H" + l))
                    pe.wait_ge(g_exp_adj.sem, g_exp_adj.at(kind, l, turn))
                    for g in range(2):
                        mm = pe.matmul(tile[:, g * 512:g * 512 + D + 1], exp_adj[:, g, :], h_l[:, g, :],
                                       start=True, stop=True)
                    mm.then_inc(full, 1)

                elif base == "C":
                    pe.wait_ge(*evacuated(kind, job, turn, "X" + l, "hl" + l))
                    pe.wait_ge(g_biased.sem, g_biased.at(kind, "hr" + l, turn))
                    for g in range(2):
                        for side, h in enumerate((h_l, h_r)):
                            mm = pe.matmul(tile[:, g * 512:g * 512 + D], gated[:, side, g, :], h[:, g, 0:D],
                                           start=(side == 0), stop=(side == 1))
                    mm.then_inc(full, 1)

                elif kind == "L2" and base == "S":
                    if l == "0":
                        pe.wait_ge(*evacuated(kind, job, turn, "I"))
                    else:
                        pe.wait_ge(g_lo.sem, g_lo.at(kind, "x", turn))
                    for g in range(2):
                        n = slice(g * P, (g + 1) * P)
                        h_pair = [lambda k, h=h: h[:, k, n] for h in g_ht]
                        split_products(tile[:, n], h_pair, h_pair, full if g else None)

                elif kind == "L2" and base == "X":
                    pe.wait_ge(g_exp_adj.sem, g_exp_adj.at(kind, l, turn))
                    for g in range(2):
                        mm = pe.transpose(tile[:, g * P:(g + 1) * P], exp_adj[:, g, :], ident[:, :])
                    mm.then_inc(full, 1)

                elif base in ("hl", "hr", "hs"):
                    row_projection(tile, f"L2_{base[1]}{l}", g_ht, full)

                elif job == "T0":
                    pe.wait_ge(g_norm.sem, g_norm.at(kind, "C0", turn))
                    transpose_rows(tile, g_z, full)

                elif job in ("Q", "K"):
                    if job == "Q":
                        pe.wait_ge(*evacuated(kind, job, turn, "I"))
                    feature_projection(tile, f"{kind}_{job.lower()}", a_ht, full)

                elif job == "V":
                    row_projection(tile, f"{kind}_v", a_ht, full)

                elif base == "S":
                    b = int(l)
                    if b == 0:
                        pe.wait_ge(a_stacked.sem, a_stacked.at(kind, "K.stack_lo", turn))
                    n = slice(b // 2 * P, (b // 2 + 1) * P)
                    for h in range(HB):
                        head = HB * (b % 2) + h
                        mm = pe.matmul(tile[:, h * P:(h + 1) * P], stack[0][0:96, head, n], stack[1][0:96, head, n],
                                       start=True, stop=True)
                    mm.then_inc(full, 1)

                elif base == "X":
                    pe.wait_ge(a_exp.sem, a_exp.at(kind, l, turn))
                    for h in range(HB):
                        mm = pe.transpose(tile[:, h * P:(h + 1) * P], sc[:, int(l) % 2, h, :], ident[:, :])
                    mm.then_inc(full, 1)

                elif base == "P":
                    g = int(l)
                    pe.wait_ge(*evacuated(kind, job, turn, f"X{2 * g}", f"X{2 * g + 1}"))
                    if g == 0:
                        pe.wait_ge(a_hi.sem, a_hi.at(kind, "V", turn))
                        pe.wait_ge(a_vlo.sem, a_vlo.at(kind, "x", turn))
                    for h in range(HEADS):
                        at = h * (HD + 1)
                        pe.matmul(tile[:, at:at + HD + 1], pt_hi[:, h, :], v_hi[:, g, h, :], start=True, stop=False)
                        pe.matmul(tile[:, at:at + HD], pt_hi[:, h, :], v_lo[:, g, h, :], start=False, stop=False,
                                  skip_group_check=True)
                        mm = pe.matmul(tile[:, at:at + HD + 1], pt_lo[:, h, :], v_hi[:, g, h, :],
                                       start=False, stop=True)
                    mm.then_inc(full, 1)

                elif job == "T":
                    pe.wait_ge(*evacuated(kind, job, turn, "P0", "P1"))
                    transpose_rows(tile, row_a, full)

                elif job == "Y":
                    pe.wait_ge(*evacuated(kind, job, turn, "T"))
                    row_projection(tile, f"{kind}_o", (t_hi, t_lo), full)

            for n in range(LOOP_START):
                for step in steps_of(Turn(n)):
                    do(*step)
            with pe.Fori(LOOP_START, PAIRS - LOOP_TURNS + 1, LOOP_TURNS) as reg:
                for n in range(LOOP_TURNS):
                    for step in steps_of(Turn(n, reg)):
                        do(*step)
            for n in range(PAIRS, TURNS):
                for step in steps_of(Turn(n)):
                    do(*step)

        @block.scalar
        def _(act):
            def normalise(z, small, dst, norm):
                for g in range(2):
                    a = act.activation(dst[:, g, :], z[:, g, :], ACT.Identity, bias=small[:, 30 + g:31 + g],
                                       scale=small[:, 28 + g:29 + g])
                a.then_inc(norm.sem, 1)

            hi_of = {"mL": (m_hi[0], DESCALE), "mR": (m_hi[1], DESCALE), "Q": (qk_hi[0], DESCALE / TEMPER),
                     "K": (qk_hi[1], DESCALE), "T": (t_hi, 1.0)}

            def do(kind, job, part, turn):
                if kind == "W":
                    n = int(job)
                    act.wait_ge(load_w[n % 3], 16 * (n // 3 + 1))
                    act.activation(w_hi[:, n], staging[n % 3], ACT.Copy, scale=WSCALE).then_inc(weight_hi, 1)
                    return
                s = slots[kind]
                base, l = job.rstrip("0123"), job[-1]
                hi = g_hi if s is gnn else a_hi

                if part == "hi" and (base in ("I", "mL", "mR", "Q", "K") or job == "T"):
                    dst, scale = ((g_ht_hi if s is gnn else a_ht_hi), 1.0) if base == "I" else hi_of[base]
                    act.wait_ge(s.full, s.full_at(kind, job, turn))
                    act.activation(dst[:, :, :], features_of(s.tile(kind, job, turn)), ACT.Copy, scale=scale)\
                       .then_inc(hi.sem, 1)

                elif part == "hi" and base == "X":
                    act.wait_ge(att.full, att.full_at(kind, job, turn))
                    h0 = HB * (int(l) % 2)
                    act.activation(pt_hi[:, h0:h0 + HB, :], heads_of(att.tile(kind, job, turn)), ACT.Copy)\
                       .then_inc(a_hi.sem, 1)

                elif part == "hi" and job == "V":
                    act.wait_ge(att.evac(kind, "V", turn), att.evac_at(kind, "V", turn))
                    act.activation(v_hi[:, :, :, 0:HD], row_a[:, :, :].rearrange("p g (h d) -> p g h d", d=HD),
                                   ACT.Copy).then_inc(a_hi.sem, 1)

                elif part == "relu":
                    act.wait_ge(gnn.full, gnn.full_at(kind, job, turn))
                    tile = gnn.tile(kind, job, turn)
                    for c in range(C):
                        t = act.activation(t32[:, c, :], tile[:, c * T:(c + 1) * T], ACT.Relu,
                                           bias=cols[f"{kind}_c"][:, c:c + 1], scale=cols[f"{kind}_a"][:, c:c + 1])
                    t.then_inc(gnn.evac(kind, job, turn), 1)

                elif part == "hi" and job == "T0":
                    act.wait_ge(gnn.evac(kind, job, turn), gnn.evac_at(kind, job, turn))
                    act.activation(g_ht_hi[:, :, :], t32[:, :, :], ACT.Copy).then_inc(g_hi.sem, 1)

                elif part == "out" and base in ("H", "hr"):
                    act.wait_ge(gnn.full, gnn.full_at(kind, job, turn))
                    act.activation((h_r if base == "hr" else h_l)[:, :, 0:D], rows_of(gnn.tile(kind, job, turn), D),
                                   ACT.Copy, scale=DESCALE).then_inc(gnn.evac(kind, job, turn), 1)

                elif kind == "L0" and part == "exp":
                    act.wait_ge(g_logits.sem, g_logits.at("L0", l, turn))
                    act.activation(expu[:, :, :], logits[:, :, :], ACT.Exp).then_inc(g_expu.sem, 1)

                elif kind == "L2" and part == "exp":
                    act.wait_ge(g_negmax.sem, g_negmax.at("L2", l, turn))
                    tile = gnn.tile("L2", job, turn)
                    for g in range(2):
                        e = act.activation(expu[:, g, :], tile[:, g * P:(g + 1) * P], ACT.Exp,
                                           bias=g_small[:, 42 + g:43 + g], scale=1.0 / TEMPER,
                                           accum_out=g_small[:, 44 + g:45 + g])
                    e.then_inc(gnn.evac("L2", job, turn), 1)

                elif part == "exp":
                    b = int(l)
                    act.wait_ge(a_max.sem, a_max.at(kind, l, turn))
                    for h in range(HB):
                        e = act.activation(sc[:, b % 2, h, :], sc[:, b % 2, h, :], ACT.Exp,
                                           bias=neg_max[:, b, h:h + 1])
                    e.then_inc(a_exp.sem, 1)

                elif part == "norm" and base == "C":
                    act.wait_ge(g_shift.sem, g_shift.at(kind, job, turn))
                    normalise(g_z, g_small, g_z, g_norm)

                elif part == "norm" and base == "F":
                    act.wait_ge(g_shift.sem, g_shift.at(kind, job, turn))
                    if kind == "L0" and turn.from_on(1):
                        act.wait_ge(att.evac("L1", "Y", turn.before()), att.evac_at("L1", "Y", turn.before()))
                    if kind == "L2" and turn.from_on(2):
                        act.wait_ge(att.evac("L3", "Y", turn), att.evac_at("L3", "Y", turn))
                    normalise(g_z, g_small, x_out[kind], g_norm)

                elif part == "norm":
                    act.wait_ge(a_shift.sem, a_shift.at(kind, "x", turn))
                    if kind == "L1" and turn.from_on(1):
                        act.wait_ge(g_resid.sem, g_resid.at("L2", "x", turn))
                    if kind == "L3" and turn.from_on(3):
                        act.wait_ge(x4_stored.sem, x4_stored.at("L3", "x", turn, back=1))
                    normalise(a_z, a_small, x_out[kind], a_norm)

            for n in range(LOOP_START):
                for step in steps_of(Turn(n)):
                    do(*step)
            with act.Fori(LOOP_START, PAIRS - LOOP_TURNS + 1, LOOP_TURNS) as reg:
                for n in range(LOOP_TURNS):
                    for step in steps_of(Turn(n, reg)):
                        do(*step)
            for n in range(PAIRS, TURNS):
                for step in steps_of(Turn(n)):
                    do(*step)

        @block.vector
        def _(dve):
            def linked(turn):
                links["n"] += 1
                if turn.reg is None:
                    return links["n"]
                return turn.reg * VECTOR_LINKS + (links["n"] - LOOP_START * VECTOR_LINKS)

            dve.memset(h_l[:, :, :], 1.0).then_inc(ones_ready, 1)
            dve.memset(v_hi[:, :, :, :], 1.0).then_inc(ones_ready, 1)
            dve.wait_ge(consts_ready, 3)

            def stats(z, small, turn):
                dve.bn_stats(small[:, 0:6], z[:, 0, :])
                dve.bn_stats(small[:, 6:12], z[:, 1, :])
                dve.drain()
                dve.bn_aggr(small[:, 16:18], small[:, 0:6])
                dve.bn_aggr(small[:, 18:20], small[:, 6:12]).then_inc(vector_link, 1)
                dve.wait_ge(vector_link, linked(turn))

            def means(small):
                return small[:, 16:20].rearrange("p (g s) -> p g s", s=2)[:, :, 0]

            def variances(small):
                return small[:, 16:20].rearrange("p (g s) -> p g s", s=2)[:, :, 1]

            lo_of = {"mL": (m_hi[0], m_lo[0], DESCALE), "mR": (m_hi[1], m_lo[1], DESCALE),
                     "Q": (qk_hi[0], qk_lo[0], DESCALE / TEMPER), "K": (qk_hi[1], qk_lo[1], DESCALE),
                     "T": (t_hi, t_lo, 1.0)}

            def do(kind, job, part, turn):
                if kind == "W":
                    n = int(job)
                    dve.wait_ge(weight_hi, n + 1)
                    dve.scalar_tensor_tensor(w_lo[:, n], staging[n % 3], WSCALE, w_hi[:, n], ALU.mult, ALU.subtract)\
                       .then_inc(weight_split, 1)
                    if n == L0_WEIGHTS + 2:
                        dve.wait_ge(params_loaded, 16 * (len(rows) + len(cols)))
                    return
                s = slots[kind]
                base, l = job.rstrip("0123"), job[-1]

                if part == "lo" and base in ("I", "mL", "mR", "Q", "K") or (part == "lo" and job == "T"):
                    hi = g_hi if s is gnn else a_hi
                    dst_hi, dst_lo, scale = lo_of[base] if base != "I" else (
                        (g_ht_hi, g_ht_lo, 1.0) if s is gnn else (a_ht_hi, a_ht_lo, 1.0))
                    dve.wait_ge(hi.sem, hi.at(kind, job, turn))
                    dve.scalar_tensor_tensor(dst_lo[:, :, :], features_of(s.tile(kind, job, turn)), scale,
                                             dst_hi[:, :, :], ALU.mult, ALU.subtract)\
                       .then_inc(s.evac(kind, job, turn), 1)

                elif part == "lo" and job == "T0":
                    dve.wait_ge(g_hi.sem, g_hi.at(kind, "T0", turn))
                    dve.tensor_tensor(g_ht_lo[:, :, :], t32[:, :, :], g_ht_hi[:, :, :], ALU.subtract)\
                       .then_inc(g_lo.sem, 1)

                elif kind == "L0" and part == "mask":
                    dve.wait_ge(gnn.full, gnn.full_at(kind, job, turn))
                    if l == "0":
                        dve.wait_ge(g_masks.sem, g_masks.at("L0", "x", turn))
                    dve.tensor_tensor(gated[:, :, :, :].rearrange("p s g n -> p (s g n)"),
                                      gnn.tile(kind, job, turn)[:, 0:4 * P],
                                      masks[:, :, :, :].rearrange("p s g n -> p (s g n)"), ALU.mult)\
                       .then_inc(gnn.evac(kind, job, turn), 1)

                elif kind == "L0" and part == "ctx":
                    dve.wait_ge(gnn.full, gnn.full_at(kind, job, turn))
                    if l == "0" and g_norm.again(kind, job, turn):
                        dve.wait_ge(g_norm.sem, g_norm.at(kind, job, turn, back=1))
                    tile = gnn.tile(kind, job, turn)
                    sums = rows_of(tile, D + 1)[:, :, D]
                    dve.tensor_copy(g_small[:, 46:48], sums).then_inc(vector_link, 1)
                    dve.tensor_scalar(g_small[:, 20:22], sums, 1e-10, 1e-3, ALU.add, ALU.mult)
                    dve.wait_ge(vector_link, linked(turn))
                    for g in range(2):
                        z = dve.scalar_tensor_tensor(g_z[:, g, :], rows[f"L0_b{l}"][:, :], g_small[:, 46 + g:47 + g],
                                                     tile[:, g * 512:g * 512 + D], ALU.mult, ALU.add)
                    z.then_inc(gnn.evac(kind, job, turn), 1)

                elif base == "C" and part == "stats":
                    dve.wait_ge(gnn.evac(kind, job, turn), gnn.evac_at(kind, job, turn))
                    stats(g_z, g_small, turn)
                    if kind == "L0":
                        dve.tensor_scalar(g_small[:, 22:24], variances(g_small), D / (D - 1.0), None, ALU.mult)\
                           .then_inc(g_var.sem, 1)
                    else:
                        dve.tensor_tensor(g_small[:, 22:24], variances(g_small), g_small[:, 52:54], ALU.add)\
                           .then_inc(g_var.sem, 1)

                elif part == "center":
                    for g in range(2):
                        z = dve.scalar_tensor_tensor(g_z[:, g, :], g_z[:, g, :], g_small[:, 16 + 2 * g:17 + 2 * g],
                                                     rows[f"{kind}_a"][:, :], ALU.subtract, ALU.mult)
                    z.then_inc(g_centered.sem, 1)

                elif part == "apply":
                    dve.wait_ge(g_root.sem, g_root.at(kind, job, turn))
                    dve.wait_ge(g_centered.sem, g_centered.at(kind, "x", turn))
                    if kind == "L0":
                        dve.tensor_tensor(g_small[:, 26:28], g_small[:, 24:26], g_small[:, 20:22], ALU.add)\
                           .then_inc(vector_link, 1)
                        dve.wait_ge(vector_link, linked(turn))
                        dve.reciprocal(g_small[:, 28:30], g_small[:, 26:28]).then_inc(vector_link, 1)
                        dve.wait_ge(vector_link, linked(turn))
                    for g in range(2):
                        z = dve.scalar_tensor_tensor(g_z[:, g, :], g_z[:, g, :], g_small[:, 28 + g:29 + g],
                                                     rows[f"{kind}_c"][:, :], ALU.mult, ALU.add)
                    z.then_inc(g_affine.sem, 1)

                elif kind == "L0" and base == "C" and part == "shift":
                    dve.wait_ge(g_root.sem, g_root.at("L0", job, turn))
                    dve.tensor_tensor(g_small[:, 26:28], g_small[:, 24:26], g_small[:, 20:22], ALU.add)\
                       .then_inc(vector_link, 1)
                    dve.wait_ge(vector_link, linked(turn))
                    dve.reciprocal(g_small[:, 28:30], g_small[:, 26:28]).then_inc(vector_link, 1)
                    dve.wait_ge(vector_link, linked(turn))
                    dve.scalar_tensor_tensor(g_small[:, 30:32], means(g_small), -1.0, g_small[:, 28:30],
                                             ALU.mult, ALU.mult).then_inc(g_shift.sem, 1)

                elif part == "shift":
                    root, shift, small = (g_root, g_shift, g_small) if s is gnn else (a_root, a_shift, a_small)
                    event = job if s is gnn else "x"
                    dve.wait_ge(root.sem, root.at(kind, event, turn))
                    dve.scalar_tensor_tensor(small[:, 30:32], means(small), -1.0, small[:, 28:30],
                                             ALU.mult, ALU.mult).then_inc(shift.sem, 1)

                elif base == "F" and part == "res":
                    dve.wait_ge(g_affine.sem, g_affine.at(kind, "x", turn))
                    dve.scalar_tensor_tensor(g_z[:, :, :], g_z[:, :, :], 0.0, x_in[kind][:, :, :],
                                             ALU.max, ALU.add).then_inc(g_resid.sem, 1)

                elif base == "F" and part == "stats":
                    dve.wait_ge(g_resid.sem, g_resid.at(kind, "x", turn))
                    stats(g_z, g_small, turn)
                    dve.tensor_scalar(g_small[:, 22:24], variances(g_small), 1e-5, None, ALU.add)\
                       .then_inc(g_var.sem, 1)

                elif kind == "L2" and part == "max":
                    dve.wait_ge(gnn.full, gnn.full_at(kind, job, turn))
                    dve.tensor_reduce(g_small[:, 40:42], gnn.tile(kind, job, turn)[:, 0:T]
                                      .rearrange("p (g n) -> p g n", n=P), AX_X, ALU.max).then_inc(vector_link, 1)
                    dve.wait_ge(vector_link, linked(turn))
                    dve.tensor_scalar(g_small[:, 42:44], g_small[:, 40:42], -1.0 / TEMPER, None, ALU.mult)\
                       .then_inc(g_negmax.sem, 1)

                elif kind == "L2" and part == "delta":
                    dve.wait_ge(gnn.evac(kind, job, turn), gnn.evac_at(kind, job, turn))
                    if l == "0":
                        dve.wait_ge(adj2_loaded.sem, adj2_loaded.at("L2", "x", turn))
                    for g in range(2):
                        e = dve.scalar_tensor_tensor(exp_adj[:, g, :], expu[:, g, :], 1.0, adj2[:, g, :],
                                                     ALU.mult, ALU.mult, accum_out=g_small[:, 46 + g:47 + g])
                    e.then_inc(g_exp_adj.sem, 1)

                elif part == "diag":
                    dve.wait_ge(g_exp_adj.sem, g_exp_adj.at("L2", l, turn))
                    for g in range(2):
                        dve.scalar_tensor_tensor(logits[:, g, :], exp_adj[:, g, :], 1.0, ident[:, :],
                                                 ALU.mult, ALU.mult, accum_out=g_small[:, 48 + g:49 + g])
                    dve.scalar_tensor_tensor(g_small[:, 50:52], g_small[:, 44:46], 1e-10, g_small[:, 46:48],
                                             ALU.mult, ALU.add).then_inc(vector_link, 1)
                    dve.wait_ge(vector_link, linked(turn))
                    dve.scalar_tensor_tensor(g_small[:, 52:54], g_small[:, 50:52], 1e-12, g_small[:, 50:52],
                                             ALU.mult, ALU.mult).then_inc(vector_link, 1)
                    dve.wait_ge(vector_link, linked(turn))

                elif kind == "L2" and part == "mask":
                    dve.wait_ge(gnn.full, gnn.full_at(kind, job, turn))
                    tile = gnn.tile(kind, job, turn)[:, 0:T].rearrange("p (s g n) -> p s g n", s=1, g=2)
                    dve.tensor_tensor(gated[:, :, :, :], tile.to_broadcast([P, 2, 2, P]),
                                      tri_strict[:, :, :].unsqueeze(2).to_broadcast([P, 2, 2, P]), ALU.mult)\
                       .then_inc(gnn.evac(kind, job, turn), 1)

                elif base in ("hl", "hs") and part == "out":
                    dve.wait_ge(gnn.full, gnn.full_at(kind, job, turn))
                    dve.scalar_tensor_tensor(h_s if base == "hs" else h_l[:, :, 0:D],
                                             rows_of(gnn.tile(kind, job, turn), D), DESCALE,
                                             both_graphs(rows[f"L2_b{base[1]}{l}"]), ALU.mult, ALU.add)\
                       .then_inc(gnn.evac(kind, job, turn), 1)

                elif kind == "L2" and part == "ctx":
                    dve.wait_ge(gnn.full, gnn.full_at(kind, job, turn))
                    dve.wait_ge(gnn.evac(kind, "hs" + l, turn), gnn.evac_at(kind, "hs" + l, turn))
                    if l == "0" and g_norm.again(kind, job, turn):
                        dve.wait_ge(g_norm.sem, g_norm.at(kind, job, turn, back=1))
                    tile = gnn.tile(kind, job, turn)
                    for g in range(2):
                        z = dve.scalar_tensor_tensor(g_z[:, g, :], h_s[:, g, :], g_small[:, 48 + g:49 + g],
                                                     tile[:, g * 512:g * 512 + D], ALU.mult, ALU.add)
                    z.then_inc(gnn.evac(kind, job, turn), 1)

                elif job == "V" and part == "out":
                    dve.wait_ge(att.full, att.full_at(kind, job, turn))
                    dve.scalar_tensor_tensor(row_a[:, :, :], rows_of(att.tile(kind, job, turn), D), DESCALE,
                                             both_graphs(rows[f"{kind}_bv"]), ALU.mult, ALU.add)\
                       .then_inc(att.evac(kind, job, turn), 1)

                elif part == "max":
                    b = int(l)
                    dve.wait_ge(att.evac(kind, job, turn), att.evac_at(kind, job, turn))
                    dve.tensor_reduce(neg_max[:, b, :], sc[:, b % 2], AX_X, ALU.max, negate=True)\
                        .then_inc(a_max.sem, 1)

                elif base == "S" and part == "add":
                    b = int(l)
                    dve.wait_ge(att.full, att.full_at(kind, job, turn))
                    if b == 0 and kind == "L1":
                        dve.wait_ge(adj1_loaded.sem, adj1_loaded.at("L1", "x", turn))
                    if b == 0 and kind == "L3":
                        dve.wait_ge(adj3_loaded.sem, adj3_loaded.at("L3", "x", turn))
                    edges = adj_of[kind][:, b // 2:b // 2 + 1, :].to_broadcast([P, HB, P])
                    dve.scalar_tensor_tensor(sc[:, b % 2], edges, 2.0 if kind == "L1" else 1.0,
                                             heads_of(att.tile(kind, job, turn)), ALU.mult, ALU.add)\
                       .then_inc(att.evac(kind, job, turn), 1)

                elif base == "X" and part == "lo":
                    dve.wait_ge(a_hi.sem, a_hi.at(kind, job, turn))
                    h0 = HB * (int(l) % 2)
                    dve.tensor_tensor(pt_lo[:, h0:h0 + HB, :], heads_of(att.tile(kind, job, turn)),
                                      pt_hi[:, h0:h0 + HB, :], ALU.subtract)\
                       .then_inc(att.evac(kind, job, turn), 1)

                elif base == "P" and part == "out":
                    g = int(l)
                    dve.wait_ge(att.full, att.full_at(kind, job, turn))
                    if g == 0:
                        dve.wait_ge(a_vlo.sem, a_vlo.at(kind, "x", turn))
                        dve.wait_ge(a_hi.sem, a_hi.at(kind, "V", turn))
                    dve.wait_ge(a_max.sem, a_max.at(kind, str(2 * g + 1), turn))
                    tile = att.tile(kind, job, turn)[:, 0:HEADS * (HD + 1)].rearrange("p (h d) -> p h d", d=HD + 1)
                    sums = tile[:, :, HD]
                    nonzero, keep, recip = a_small[:, 32:44], a_small[:, 44:56], a_small[:, 56:68]
                    dve.tensor_scalar(nonzero, neg_max[:, 2 * g:2 * g + 2, :].rearrange("p b h -> p (b h)"),
                                      0.0, None, ALU.not_equal).then_inc(vector_link, 1)
                    dve.reciprocal(recip, sums)
                    dve.wait_ge(vector_link, linked(turn))
                    dve.scalar_tensor_tensor(keep, sums, float(P), nonzero, ALU.is_lt, ALU.max)\
                       .then_inc(vector_link, 1)
                    dve.wait_ge(vector_link, linked(turn))
                    dve.tensor_tensor(recip, recip, keep, ALU.mult).then_inc(vector_link, 1)
                    dve.wait_ge(vector_link, linked(turn))
                    dve.tensor_tensor(row_a[:, g, :].rearrange("p (h d) -> p h d", d=HD), tile[:, :, 0:HD],
                                      recip.unsqueeze(2).to_broadcast([P, HEADS, HD]), ALU.mult)\
                       .then_inc(att.evac(kind, job, turn), 1)

                elif job == "Y" and part == "res":
                    dve.wait_ge(att.full, att.full_at(kind, job, turn))
                    dve.wait_ge(a_xb.sem, a_xb.at(kind, "x", turn))
                    if a_norm.again(kind, "x", turn):
                        dve.wait_ge(a_norm.sem, a_norm.at(kind, "x", turn, back=1))
                    dve.scalar_tensor_tensor(a_z[:, :, :], rows_of(att.tile(kind, job, turn), D), DESCALE,
                                             x_in[kind][:, :, :], ALU.mult, ALU.add)\
                       .then_inc(att.evac(kind, job, turn), 1)

                elif job == "Y" and part == "stats":
                    dve.wait_ge(att.evac(kind, job, turn), att.evac_at(kind, job, turn))
                    stats(a_z, a_small, turn)
                    dve.tensor_scalar(a_small[:, 22:24], variances(a_small), 1e-5, None, ALU.add)\
                       .then_inc(a_var.sem, 1)

            for n in range(LOOP_START):
                for step in steps_of(Turn(n)):
                    do(*step)
            before_loop = links["n"]
            with dve.Fori(LOOP_START, PAIRS - LOOP_TURNS + 1, LOOP_TURNS) as reg:
                for n in range(LOOP_TURNS):
                    for step in steps_of(Turn(n, reg)):
                        do(*step)
            assert links["n"] - before_loop == LOOP_TURNS * VECTOR_LINKS, links["n"] - before_loop
            links["n"] = before_loop + (PAIRS - LOOP_START) * VECTOR_LINKS
            for n in range(PAIRS, TURNS):
                for step in steps_of(Turn(n)):
                    do(*step)

        @block.gpsimd
        def _(pool):
            pool.memset(ident[:, :], 0.0).then_inc(consts_filled, 1)
            pool.memset(tri_scaled[:, :, :], 1.0 / TEMPER).then_inc(consts_filled, 1)
            pool.memset(tri_strict[:, :, :], 1.0).then_inc(consts_filled, 1)
            pool.memset(half[:, :], 0.5).then_inc(consts_filled, 1)
            pool.memset(neg_half[:, :], -0.5).then_inc(consts_filled, 1)
            pool.wait_ge(consts_filled, 5)
            pool.affine_select(out=ident[:, :], in_=ident[:, :], compare_op=ALU.not_equal, fill=1.0, base=0,
                               pattern=[[-1, P]], channel_multiplier=1).then_inc(consts_ready, 1)
            pool.affine_select(out=tri_scaled[:, 0, :], in_=tri_scaled[:, 0, :], compare_op=ALU.is_ge, fill=0.0,
                               base=0, pattern=[[-1, P]], channel_multiplier=1)
            pool.affine_select(out=tri_scaled[:, 1, :], in_=tri_scaled[:, 1, :], compare_op=ALU.is_ge, fill=0.0,
                               base=-1, pattern=[[1, P]], channel_multiplier=-1).then_inc(consts_ready, 1)
            pool.affine_select(out=tri_strict[:, 0, :], in_=tri_strict[:, 0, :], compare_op=ALU.is_ge, fill=0.0,
                               base=-1, pattern=[[-1, P]], channel_multiplier=1)
            pool.affine_select(out=tri_strict[:, 1, :], in_=tri_strict[:, 1, :], compare_op=ALU.is_ge, fill=0.0,
                               base=-1, pattern=[[1, P]], channel_multiplier=-1).then_inc(consts_ready, 1)
            pool.wait_ge(consts_ready, 3)
            pool.wait_ge(params_loaded, 16 * (len(rows) + len(cols)))

            def do(kind, job, part, turn):
                if kind == "W":
                    return
                s = slots[kind]
                base, l = job.rstrip("0123"), job[-1]

                if (kind, job) == ("L0", "masks"):
                    pool.wait_ge(adj0_loaded.sem, adj0_loaded.at("L0", "x", turn))
                    if turn.from_on(1):
                        pool.wait_ge(gnn.evac("L0", "U1", turn.before()), gnn.evac_at("L0", "U1", turn.before()))
                    for side, edges in enumerate((adjt0, adj0)):
                        m = pool.tensor_tensor(masks[:, side], edges[:, :, :],
                                               tri_scaled[:, side:side + 1, :].to_broadcast([P, 2, P]), ALU.mult)
                    m.then_inc(g_masks.sem, 1)

                elif base == "U" and part == "add":
                    pool.wait_ge(gnn.evac(kind, job, turn), gnn.evac_at(kind, job, turn))
                    pool.tensor_tensor(logits[:, :, :], gated[:, 0], gated[:, 1], ALU.add).then_inc(g_logits.sem, 1)

                elif part == "adj":
                    pool.wait_ge(g_expu.sem, g_expu.at("L0", l, turn))
                    pool.tensor_tensor(exp_adj[:, :, :], expu[:, :, :], adjt0[:, :, :], ALU.mult)\
                        .then_inc(g_exp_adj.sem, 1)

                elif part == "root":
                    var, rt, small = (g_var, g_root, g_small) if s is gnn else (a_var, a_root, a_small)
                    event = job if s is gnn else "x"
                    power, at = (half, 24) if kind == "L0" and base == "C" else (neg_half, 28)
                    pool.wait_ge(var.sem, var.at(kind, event, turn))
                    pool.tensor_tensor(small[:, at:at + 2], small[:, 22:24], power[:, :], ALU.pow).then_inc(rt.sem, 1)

                elif part == "bias":
                    pool.wait_ge(gnn.evac(kind, job, turn), gnn.evac_at(kind, job, turn))
                    pool.tensor_tensor(h_r, h_r, both_graphs(rows[f"L2_br{l}"]), ALU.add)\
                        .then_inc(g_biased.sem, 1)

                elif job == "V" and part == "lo":
                    pool.wait_ge(a_hi.sem, a_hi.at(kind, "V", turn))
                    pool.tensor_tensor(v_lo[:, :, :, :], row_a[:, :, :].rearrange("p g (h d) -> p g h d", d=HD),
                                       v_hi[:, :, :, 0:HD], ALU.subtract).then_inc(a_vlo.sem, 1)

                elif job == "xb":
                    pool.wait_ge(att.full, att.full_at(kind, "I", turn))
                    pool.tensor_tensor(x_in[kind][:, :, :], x_in[kind][:, :, :], both_graphs(rows[f"{kind}_bo"]),
                                       ALU.add).then_inc(a_xb.sem, 1)

            for n in range(LOOP_START):
                for step in steps_of(Turn(n)):
                    do(*step)
            with pool.Fori(LOOP_START, PAIRS - LOOP_TURNS + 1, LOOP_TURNS) as reg:
                for n in range(LOOP_TURNS):
                    for step in steps_of(Turn(n, reg)):
                        do(*step)
            for n in range(PAIRS, TURNS):
                for step in steps_of(Turn(n)):
                    do(*step)


def kernel(**inputs):
    import numpy as _np
    import concourse.bacc as _bacc
    from concourse import mybir as _mybir
    from concourse.bass_utils import run_bass_kernel_spmd as _run

    a = {k: _np.asarray(v) for k, v in inputs.items()}
    weights = {
        "L0_left0": a["L0_gnn_W_left"][0], "L0_right0": a["L0_gnn_W_right"][0], "L0_lin0": a["L0_gnn_W_lin"][0],
        "L0_left1": a["L0_gnn_W_left"][1], "L0_right1": a["L0_gnn_W_right"][1], "L0_lin1": a["L0_gnn_W_lin"][1],
        "L1_q": a["L1_gnn_Wq"], "L1_k": a["L1_gnn_Wk"], "L1_v": a["L1_gnn_Wv"], "L1_o": a["L1_gnn_Wo"],
        "L2_l0": a["L2_gnn_Wl"][0], "L2_s0": a["L2_gnn_Ws"][0], "L2_r0": a["L2_gnn_Wr"][0],
        "L2_l1": a["L2_gnn_Wl"][1], "L2_s1": a["L2_gnn_Ws"][1], "L2_r1": a["L2_gnn_Wr"][1],
        "L3_q": a["L3_gnn_Wq"], "L3_k": a["L3_gnn_Wk"], "L3_v": a["L3_gnn_Wv"], "L3_o": a["L3_gnn_Wo"],
    }
    vectors = {
        "L0_b0": a["L0_gnn_b_lin"][0], "L0_b1": a["L0_gnn_b_lin"][1],
        "L0_a": a["L0_gnn_ln_a"][1], "L0_c": a["L0_gnn_ln_b"][1],
        "col_L0_a": a["L0_gnn_ln_a"][0].reshape(C, P).T, "col_L0_c": a["L0_gnn_ln_b"][0].reshape(C, P).T,
        "L1_bv": a["L1_gnn_bv"], "L1_bo": a["L1_gnn_bo"],
        "L2_bl0": a["L2_gnn_bl"][0], "L2_bs0": a["L2_gnn_bs"][0], "L2_br0": a["L2_gnn_br"][0],
        "L2_bl1": a["L2_gnn_bl"][1], "L2_bs1": a["L2_gnn_bs"][1], "L2_br1": a["L2_gnn_br"][1],
        "L2_a": a["L2_gnn_ln_w"][1], "L2_c": a["L2_gnn_ln_b"][1],
        "col_L2_a": a["L2_gnn_ln_w"][0].reshape(C, P).T, "col_L2_c": a["L2_gnn_ln_b"][0].reshape(C, P).T,
        "L3_bv": a["L3_gnn_bv"], "L3_bo": a["L3_gnn_bo"],
    }
    arrays = {
        "x": _np.ascontiguousarray(a["x"]),
        "adj": _np.ascontiguousarray(a["adj"]),
        "adj_t": _np.ascontiguousarray(a["adj"].transpose(0, 2, 1)),
        "weights_t": _np.ascontiguousarray(_np.stack([weights[n].T for n in WEIGHTS])),
        **{f"vec_{n}": _np.ascontiguousarray(v) for n, v in vectors.items()},
    }
    nc = _bacc.Bacc("TRN2", target_bir_lowering=False, num_devices=1)
    dram = {n: nc.dram_tensor(n, v.shape, _mybir.dt.from_np(v.dtype), kind="ExternalInput").ap()
            for n, v in arrays.items()}
    out = nc.dram_tensor("out", (NG, P, D), _mybir.dt.float32, kind="ExternalOutput").ap()
    graph_stack_kernel(nc, dram["x"], dram["adj"], dram["adj_t"], dram["weights_t"],
                       {n: dram[f"vec_{n}"] for n in vectors}, out)
    r = _run(nc, [arrays], core_ids=[0])
    return r.results[0]["out"]
```
